# Optimizing a Trainium2 kernel written in Bass

```python
import numpy as np
import jax
import jax.numpy as jnp

def _softmax(x, axis=-1):
    return jax.nn.softmax(x, axis=axis)

def _gelu(x):
    return jax.nn.gelu(x, approximate=True)

def _silu(x):
    return jax.nn.silu(x)

def _sigmoid(x):
    return jax.nn.sigmoid(x)

def _layernorm(x, axis=-1, eps=1e-05):
    m = jnp.mean(x, axis=axis, keepdims=True)
    v = jnp.var(x, axis=axis, keepdims=True)
    return (x - m) / jnp.sqrt(v + eps)

def _scatter_add(tgt, idx, src, axis=0):
    return tgt.at[idx].add(src)

def _segment_sum(src, seg, n):
    return jax.ops.segment_sum(src, seg, n)
kernel_name = 'mk_gnn_resnorm_d4_gnn_r64_8779f1'

def setup_inputs(seed: int=0):
    np.random.seed(seed)
    _w = jnp.asarray

    def _rec_inputs():
        import jax
        import jax.numpy as jnp
        _gk = jax.random.key(seed)
        x = -0.0002928 + 1 * jax.random.normal(jax.random.fold_in(_gk, 1), (50000, 256), jnp.float32)
        src = jax.random.randint(jax.random.fold_in(_gk, 2), (25000,), 0, 50000, jnp.int32)
        dst = jnp.minimum((50000 * jax.random.uniform(jax.random.fold_in(_gk, 3), (25000,)) ** 2.0).astype(jnp.int32), 49999)
        _o = jnp.argsort(dst, stable=True)
        src = src[_o]
        dst = dst[_o]
        edge_attr_3 = -1.09012e-05 + 0.99985 * jax.random.normal(jax.random.fold_in(_gk, 12), (25000, 3), jnp.float32)
        return (x, src, dst, edge_attr_3)
    x, src, dst, edge_attr_3 = _rec_inputs()

    def _L0_gnn_setup():
        import jax, jax.numpy as jnp
        import numpy as np
        N_NODES = 256
        D_FEAT = 256
        N_EDGES = 4096
        HIDDEN = 512
        D_OUT = 256
        key = jax.random.key(seed)
        ks = jax.random.split(key, 5)
        x = jax.random.normal(ks[0], (N_NODES, D_FEAT), dtype=jnp.float32)
        W1 = jax.random.normal(ks[1], (2 * D_FEAT, HIDDEN), dtype=jnp.float32) * (1.0 / np.sqrt(2 * D_FEAT))
        b1 = jnp.zeros((HIDDEN,), dtype=jnp.float32)
        W2 = jax.random.normal(ks[2], (HIDDEN, D_OUT), dtype=jnp.float32) * (1.0 / np.sqrt(HIDDEN))
        b2 = jnp.zeros((D_OUT,), dtype=jnp.float32)
        nn_index = jax.random.randint(ks[3], (2, N_EDGES), 0, N_NODES, dtype=jnp.int64)
        return {'x': x, 'W1': W1, 'b1': b1, 'W2': W2, 'b2': b2, 'nn_index': nn_index, 'k': 16}
    _L0_gnn_all = _L0_gnn_setup()
    _L0_gnn_in = {k: v for k, v in _L0_gnn_all.items() if k in ('W1', 'b1', 'W2', 'b2')}
    del _L0_gnn_all

    def _L1_gnn_setup():
        import jax, jax.numpy as jnp
        import numpy as np
        N = 50000
        E = 6250
        IN = 256
        H = 8
        D = 32
        EF = 3
        key = jax.random.key(seed)
        ks = jax.random.split(key, 8)
        x = jax.random.normal(ks[0], (N, IN), dtype=jnp.float32)
        edge_index = jax.random.randint(ks[1], (2, E), 0, N, dtype=jnp.int64)
        edge_attr = jax.random.normal(ks[2], (E, EF), dtype=jnp.float32)
        W = jax.random.normal(ks[3], (H * D, IN), dtype=jnp.float32) * np.float32(np.sqrt(2.0 / (IN + H * D)))
        a_src = jax.random.normal(ks[4], (H, D), dtype=jnp.float32) * np.float32(np.sqrt(2.0 / (H + D)))
        a_dst = jax.random.normal(ks[5], (H, D), dtype=jnp.float32) * np.float32(np.sqrt(2.0 / (H + D)))
        edge_W = jax.random.normal(ks[6], (H * D, EF), dtype=jnp.float32) * np.float32(np.sqrt(2.0 / (EF + H * D)))
        edge_b = jnp.zeros((H * D,), dtype=jnp.float32)
        bias = jnp.zeros((H * D,), dtype=jnp.float32)
        return {'x': x, 'W': W, 'a_src': a_src, 'a_dst': a_dst, 'edge_W': edge_W, 'edge_b': edge_b, 'bias': bias, 'edge_attr': edge_attr, 'edge_index': edge_index}
    _L1_gnn_all = _L1_gnn_setup()
    _L1_gnn_in = {k: v for k, v in _L1_gnn_all.items() if k in ('W', 'a_src', 'a_dst', 'edge_W', 'edge_b', 'bias')}
    del _L1_gnn_all

    def _L2_gnn_setup():
        import jax, jax.numpy as jnp
        import numpy as np
        N_NODES = 100000
        N_EDGES = 50000
        IN_F = 256
        OUT_F = 256
        NEG_SLOPE = 0.2
        key = jax.random.key(seed)
        ks = jax.random.split(key, 8)
        x = jax.random.normal(ks[0], (N_NODES, IN_F), dtype=jnp.float32)
        Wv = jax.random.normal(ks[1], (IN_F, OUT_F), dtype=jnp.float32) / np.sqrt(IN_F)
        bv = jnp.zeros((OUT_F,), dtype=jnp.float32)
        wq = jax.random.normal(ks[2], (OUT_F,), dtype=jnp.float32) / np.sqrt(OUT_F)
        bq = jnp.zeros((), dtype=jnp.float32)
        wk = jax.random.normal(ks[3], (OUT_F,), dtype=jnp.float32) / np.sqrt(OUT_F)
        bk = jnp.zeros((), dtype=jnp.float32)
        src = jax.random.randint(ks[4], (N_EDGES,), 0, N_NODES, dtype=jnp.int32)
        dst = jax.random.randint(ks[5], (N_EDGES,), 0, N_NODES, dtype=jnp.int32)
        return {'x': x, 'Wv': Wv, 'bv': bv, 'wq': wq, 'bq': bq, 'wk': wk, 'bk': bk, 'src': src, 'dst': dst}
    _L2_gnn_all = _L2_gnn_setup()
    _L2_gnn_in = {k: v for k, v in _L2_gnn_all.items() if k in ('Wv', 'bv', 'wq', 'bq', 'wk', 'bk')}
    del _L2_gnn_all

    def _L3_gnn_setup():
        import jax, jax.numpy as jnp
        import numpy as np
        N_NODES = 50000

        def _gcn_conv(x, edge_index, W, b):
            n = x.shape[0]
            loop = jnp.arange(n, dtype=edge_index.dtype)
            src = jnp.concatenate([edge_index[0], loop])
            dst = jnp.concatenate([edge_index[1], loop])
            h = x @ W
            deg = jax.ops.segment_sum(jnp.ones_like(dst, dtype=h.dtype), dst, num_segments=n)
            dinv = jnp.where(deg > 0, jax.lax.rsqrt(deg), 0.0)
            norm = dinv[src] * dinv[dst]
            msg = h[src] * norm[:, None]
            out = jax.ops.segment_sum(msg, dst, num_segments=n)
            return out + b
        key = jax.random.key(seed)
        k1, k2, k3, k4 = jax.random.split(key, 4)
        in_c, hid = (256, 128)
        x = jax.random.normal(k1, (N_NODES, in_c), dtype=jnp.float32)
        edge_index = jax.random.randint(k2, (2, 12500), 0, N_NODES, dtype=jnp.int32)
        W_conv = jax.random.normal(k3, (in_c, hid), dtype=jnp.float32) * (1.0 / np.sqrt(in_c))
        b_conv = jnp.zeros((hid,), dtype=jnp.float32)
        limit = np.sqrt(6.0 / (hid + in_c))
        W_lin = jax.random.uniform(k4, (hid, in_c), dtype=jnp.float32, minval=-limit, maxval=limit)
        b_lin = jnp.zeros((in_c,), dtype=jnp.float32)
        return {'x': x, 'edge_index': edge_index, 'W_conv': W_conv, 'b_conv': b_conv, 'W_lin': W_lin, 'b_lin': b_lin}
    _L3_gnn_all = _L3_gnn_setup()
    _L3_gnn_in = {k: v for k, v in _L3_gnn_all.items() if k in ('W_conv', 'b_conv', 'W_lin', 'b_lin')}
    del _L3_gnn_all
    return {'x': x, 'src': src, 'dst': dst, 'edge_attr_3': edge_attr_3, 'L0_gnn_W1': _L0_gnn_in['W1'], 'L0_gnn_b1': _L0_gnn_in['b1'], 'L0_gnn_W2': _L0_gnn_in['W2'], 'L0_gnn_b2': _L0_gnn_in['b2'], 'L1_gnn_W': _L1_gnn_in['W'], 'L1_gnn_a_src': _L1_gnn_in['a_src'], 'L1_gnn_a_dst': _L1_gnn_in['a_dst'], 'L1_gnn_edge_W': _L1_gnn_in['edge_W'], 'L1_gnn_edge_b': _L1_gnn_in['edge_b'], 'L1_gnn_bias': _L1_gnn_in['bias'], 'L2_gnn_Wv': _L2_gnn_in['Wv'], 'L2_gnn_bv': _L2_gnn_in['bv'], 'L2_gnn_wq': _L2_gnn_in['wq'], 'L2_gnn_bq': _L2_gnn_in['bq'], 'L2_gnn_wk': _L2_gnn_in['wk'], 'L2_gnn_bk': _L2_gnn_in['bk'], 'L3_gnn_W_conv': _L3_gnn_in['W_conv'], 'L3_gnn_b_conv': _L3_gnn_in['b_conv'], 'L3_gnn_W_lin': _L3_gnn_in['W_lin'], 'L3_gnn_b_lin': _L3_gnn_in['b_lin']}

def reference(x, src, dst, edge_attr_3, L0_gnn_W1, L0_gnn_b1, L0_gnn_W2, L0_gnn_b2, L1_gnn_W, L1_gnn_a_src, L1_gnn_a_dst, L1_gnn_edge_W, L1_gnn_edge_b, L1_gnn_bias, L2_gnn_Wv, L2_gnn_bv, L2_gnn_wq, L2_gnn_bq, L2_gnn_wk, L2_gnn_bk, L3_gnn_W_conv, L3_gnn_b_conv, L3_gnn_W_lin, L3_gnn_b_lin):
    import jax
    import jax.numpy as jnp

    def _L0_gnn_ref(x, W1, b1, W2, b2, nn_index, k):
        import jax, jax.numpy as jnp
        import numpy as np
        N_NODES = 256
        D_FEAT = 256
        N_EDGES = 4096
        HIDDEN = 512
        D_OUT = 256
        num_nodes = x.shape[0]
        src = nn_index[0]
        tgt = nn_index[1]
        x_i = x[tgt]
        x_j = x[src]
        feat = jnp.concatenate([x_i, x_j - x_i], axis=-1)
        h = jax.nn.relu(feat @ W1 + b1)
        msg = h @ W2 + b2
        out = jax.ops.segment_sum(msg, tgt, num_segments=num_nodes)
        deg = jax.ops.segment_sum(jnp.ones((msg.shape[0], 1), dtype=msg.dtype), tgt, num_segments=num_nodes)
        return out / (deg + 1e-08)

    def _L1_gnn_ref(x, W, a_src, a_dst, edge_W, edge_b, bias, edge_attr, edge_index):
        import jax, jax.numpy as jnp
        import numpy as np
        N = 50000
        E = 6250
        IN = 256
        H = 8
        D = 32
        EF = 3
        n = x.shape[0]
        h = (x @ W.T).reshape(n, H, D)
        src, dst = (edge_index[0], edge_index[1])
        h_src = h[src]
        h_dst = h[dst]
        alpha = jnp.einsum('ehd,hd->eh', h_src, a_src) + jnp.einsum('ehd,hd->eh', h_dst, a_dst)
        enc = jax.nn.relu(edge_attr @ edge_W.T + edge_b).reshape(-1, H, D)
        alpha = alpha + jnp.sum(enc * h_dst, axis=-1)
        alpha = jnp.where(alpha >= 0, alpha, 0.2 * alpha)
        amax = jax.ops.segment_max(alpha, dst, num_segments=n)
        ex = jnp.exp(alpha - amax[dst])
        denom = jax.ops.segment_sum(ex, dst, num_segments=n)
        attn = ex / jnp.maximum(denom[dst], 1e-10)
        out = jax.ops.segment_sum(h_src * attn[..., None], dst, num_segments=n)
        return out.reshape(n, H * D) + bias

    def _L2_gnn_ref(x, Wv, bv, wq, bq, wk, bk, src, dst):
        import jax, jax.numpy as jnp
        import numpy as np
        N_NODES = 100000
        N_EDGES = 50000
        IN_F = 256
        OUT_F = 256
        NEG_SLOPE = 0.2
        n = x.shape[0]
        h = x @ Wv + bv
        q = h @ wq + bq
        k = h @ wk + bk
        e = q[src] + k[dst]
        c = jnp.where(e > 0, e, NEG_SLOPE * e)
        m = jax.ops.segment_max(c, dst, num_segments=n)
        ex = jnp.exp(c - m[dst])
        s = jax.ops.segment_sum(ex, dst, num_segments=n)
        attn = ex / s[dst]
        msg = h[src] * attn[:, None]
        out = jax.ops.segment_sum(msg, dst, num_segments=n)
        return out

    def _L3_gnn_ref(x, edge_index, W_conv, b_conv, W_lin, b_lin):
        import jax, jax.numpy as jnp
        import numpy as np
        N_NODES = 50000

        def _gcn_conv(x, edge_index, W, b):
            n = x.shape[0]
            loop = jnp.arange(n, dtype=edge_index.dtype)
            src = jnp.concatenate([edge_index[0], loop])
            dst = jnp.concatenate([edge_index[1], loop])
            h = x @ W
            deg = jax.ops.segment_sum(jnp.ones_like(dst, dtype=h.dtype), dst, num_segments=n)
            dinv = jnp.where(deg > 0, jax.lax.rsqrt(deg), 0.0)
            norm = dinv[src] * dinv[dst]
            msg = h[src] * norm[:, None]
            out = jax.ops.segment_sum(msg, dst, num_segments=n)
            return out + b
        h = _gcn_conv(x, edge_index, W_conv, b_conv)
        return h @ W_lin + b_lin
    edge_index = jnp.stack([src, dst])
    x = _layernorm(x + _L0_gnn_ref(x, L0_gnn_W1, L0_gnn_b1, L0_gnn_W2, L0_gnn_b2, edge_index, 16), axis=-1)
    x = _layernorm(x + _L1_gnn_ref(x, L1_gnn_W, L1_gnn_a_src, L1_gnn_a_dst, L1_gnn_edge_W, L1_gnn_edge_b, L1_gnn_bias, edge_attr_3, edge_index), axis=-1)
    x = _layernorm(x + _L2_gnn_ref(x, L2_gnn_Wv, L2_gnn_bv, L2_gnn_wq, L2_gnn_bq, L2_gnn_wk, L2_gnn_bk, src, dst), axis=-1)
    x = _layernorm(x + _L3_gnn_ref(x, edge_index, L3_gnn_W_conv, L3_gnn_b_conv, L3_gnn_W_lin, L3_gnn_b_lin), axis=-1)
    return x

_drawn_inputs = setup_inputs


def setup_inputs(seed=0):
    import zlib

    import numpy as np

    out = dict(_drawn_inputs(seed))
    spreads = {'L0_gnn_b1': (0.0, 0.401),
     'L0_gnn_b2': (0.0, 0.1),
     'L1_gnn_edge_b': (0.0, 0.62),
     'L1_gnn_bias': (0.0, 0.1),
     'L2_gnn_bv': (0.0, 0.1),
     'L3_gnn_b_conv': (0.0, 0.1),
     'L3_gnn_b_lin': (0.0, 0.1)}
    factors = {'L1_gnn_a_dst': 2.774, 'L2_gnn_wk': 3.175}
    for name, (base, spread) in spreads.items():
        noise = np.random.default_rng([zlib.crc32(name.encode()), seed]).standard_normal(out[name].shape)
        drawn = base * np.exp(spread * noise) if base else spread * noise
        out[name] = jnp.asarray(drawn.astype(out[name].dtype))
    for name, factor in factors.items():
        out[name] = (out[name] * factor).astype(out[name].dtype)
    return out
```

```python
from collections import namedtuple
from contextlib import ExitStack

import concourse.bass as bass
from concourse import mybir

F32 = mybir.dt.float32
BF16 = mybir.dt.bfloat16
I32 = mybir.dt.int32
ALU = mybir.AluOpType
ACT = mybir.ActivationFunctionType
AX = mybir.AxisListType

P = 128
NODES = 50000
EDGES = 25000
FEAT = 256
HIDDEN = 512
HEADS = 8
HEAD_DIM = FEAT // HEADS
EDGE_FEAT = 3
GCN_HIDDEN = 128
FC = FEAT // P
HC = HIDDEN // P
UNROLL = 4
TILES = -(-EDGES // (P * UNROLL)) * UNROLL
EPAD = TILES * P
BLOCKS = 2
ROWS = TILES // BLOCKS
MAP_COLS = -(-NODES // P)
PLAIN_COLS = NODES // P
TAIL = NODES - PLAIN_COLS * P
BATCH = 15
PIECE = 5
NOWHERE = 1 << 20
LOW = -1.0e30
EPS = 1e-5

Tile = namedtuple("Tile", "t slot pair turn")
ScanSpace = namedtuple("ScanSpace", "total between carry")


class Memory:
    pass



def tile_at(g, u, lag, unroll=UNROLL, tiles=TILES):
    t = g * unroll + (u - lag)
    if isinstance(g, int) and not 0 <= t < tiles:
        return None
    return Tile(t, (u - lag) % unroll, (u - lag) % unroll % 2, g + (u - lag) // unroll)


def run_steps(eng, step, lag, unroll=UNROLL, tiles=TILES):
    bodies = tiles // unroll
    peeled = min(bodies, max(1, 2 * UNROLL // unroll))
    for j in range(peeled * unroll):
        step(j // unroll, j % unroll)
    if bodies > peeled:
        with eng.Fori(peeled, bodies) as g:
            for u in range(unroll):
                step(g, u)
    for u in range(lag):
        step(bodies + u // unroll, u % unroll)


def wait(eng, sem, value):
    if not (isinstance(value, int) and value <= 0):
        eng.wait_ge(sem, value)


def hold(eng, sem, value):
    if not (isinstance(value, int) and value <= 0):
        eng.wait_ge(sem, value)
        eng.nop(nofuse=True)


def col(ap, t, n=1):
    return ap[:, t:t + n] if isinstance(t, int) else ap[:, bass.ds(t, n)]


def tile_rows(ap, t):
    return ap[t * P:(t + 1) * P, :] if isinstance(t, int) else ap[bass.ds(t * P, P), :]


class Chain:

    def __init__(self, eng, sem, base=0):
        self.eng, self.sem, self.base, self.n = eng, sem, base, 0

    def __call__(self, ins):
        self.n += 1
        ins.then_inc(self.sem, 1)
        self.eng.wait_ge(self.sem, self.base + self.n)


def phase(nc, label, names, rings=(), more=()):
    taken = []

    def take(name):
        taken.append(nc.alloc_semaphore(f"{label}_{name}"))
        return taken[-1]

    def clear():
        nc.clear_and_free_semaphores(taken)
        nc.all_engine_barrier()
    ctx = ExitStack()
    ctx.callback(clear)
    sized = [(n, UNROLL) for n in rings] + list(more)
    found = [take(n) for n in names] + [[take(f"{n}{i}") for i in range(size)] for n, size in sized]
    return ctx, namedtuple("Semaphores", list(names) + [n for n, _ in sized])(*found)


def build(nc, d, out):
    ctx = ExitStack()
    with ctx:
        def sb(name, shape, dt=F32):
            return ctx.enter_context(nc.sbuf_tensor(name, shape, dt))

        def dram(name, shape, dt=F32):
            return nc.dram_tensor(name, shape, dt).ap()

        bank = [ctx.enter_context(nc.psum_tensor(f"bank{i}", [P, 512], F32)) for i in range(8)]
        m = Memory()
        m.bank = bank
        m.dst_f = dram("dst_f", [EPAD + 2])
        m.node_map = dram("node_map", [MAP_COLS * P, 1], I32)
        m.x_src = dram("x_src", [EPAD, FEAT])
        m.h_src = dram("h_src", [EPAD, FEAT])
        m.x2_src = dram("x2_src", [EPAD, FEAT])
        m.state = [None] + [dram(f"state{i}", [EPAD, FEAT]) for i in (1, 2, 3)]
        m.ident = sb("ident", [P, P])
        m.eps = sb("eps", [P, 1])
        m.dst = sb("dst_col", [P, TILES])
        m.idx_l0 = sb("idx_l0", [P, TILES, 2], I32)
        m.idx_l1 = sb("idx_l1", [P, TILES, 2], I32)
        m.map_idx = sb("map_idx", [P, TILES], I32)
        m.edge_id = sb("edge_id", [P, TILES], I32)
        m.indeg = sb("indeg", [P, TILES])
        m.rdeg = sb("rdeg", [P, TILES])
        m.degr = sb("degr", [P, TILES])
        m.sdeg = sb("sdeg", [P, TILES])
        m.dinv = sb("dinv", [P, TILES])
        m.keep = sb("keep", [ROWS, BLOCKS, P])
        m.pen_f = sb("pen_f", [ROWS, BLOCKS, P])
        m.pen_b = sb("pen_b", [ROWS, BLOCKS, P])
        m.last = sb("last_row", [ROWS, BLOCKS, P])
        m.open_row = sb("open_row", [HEADS, 3, TILES])
        m.row_stat = sb("row_stat", [P, 3, TILES])
        m.touched = sb("touched", [P, TILES])
        m.untouched = sb("untouched", [P, TILES])
        m.affine = sb("affine", [P, 2, 3, TILES])
        m.score = sb("score", [P, TILES, HEADS])
        m.q_src = sb("q_src", [P, TILES])
        m.k_dst = sb("k_dst", [P, TILES])
        m.attn2 = sb("attn2", [P, TILES])
        weights(nc, d, m, sb)
        structure(nc, d, m, ctx)
        edge_mlp(nc, d, m)
        untouched_nodes(nc, d, m, out, P, 0, PLAIN_COLS, 2 * BATCH, BATCH, PIECE)
        untouched_nodes(nc, d, m, out, TAIL, P * PLAIN_COLS, 1, 1, 1, 1)
        gat_scores(nc, d, m)
        gat_softmax(nc, m)
        gat_sum(nc, d, m)
        scalar_scores(nc, d, m)
        scalar_softmax(nc, m)
        scalar_sum(nc, d, m)
        gcn(nc, d, m, out)


def weights(nc, d, m, sb):
    m.w1d, m.w1b, m.w2 = sb("w1d", [P, FC, HIDDEN]), sb("w1b", [P, FC, HIDDEN]), sb("w2", [P, HC, FEAT])
    m.b1_parts, m.res_parts, m.ones3 = sb("b1_parts", [3, HIDDEN], BF16), sb("res_parts", [3, FEAT], BF16), sb("ones3", [3, P], BF16)
    m.w_src = sb("w_src", [P, FC, FEAT + HEADS])
    m.w_dst = sb("w_dst", [P, FC, HEADS])
    m.w_enc = sb("w_enc", [EDGE_FEAT + 1, FEAT])
    m.wv = sb("wv", [P, FC, FEAT])
    m.w_gcn = sb("w_gcn", [P, FC, FEAT])
    m.w_res = sb("w_res", [P, FC, FEAT])
    rows = ("b2", "bias", "bv", "bl", "q_row", "k_row")
    m.b2, m.bias, m.bv, m.res_bias, m.q_row, m.k_row = (sb(n + "_all", [P, FEAT]) for n in rows)
    m.bias_mv, m.bias_var_eps, m.qk_bias = sb("bias_mv", [P, 2]), sb("bias_var_eps", [P, 1]), sb("qk_bias", [P, 1])
    names = ["ident_done", "load_done", "dve_chain", "parts_done", "parts_in", "masked", "prod_done", "prod_taken",
             "const_done"]
    ctx, s = phase(nc, "weights", names)
    with (ctx, nc.Block() as block):
        def tmp(name, shape, dt=F32):
            return ctx.enter_context(nc.sbuf_tensor("tmp_" + name, shape, dt))
        b1_row, b1_split, rest = tmp("b1_row", [1, HIDDEN]), tmp("b1_split", [1, 3, HIDDEN], BF16), tmp("rest", [1, HIDDEN])
        res_split = tmp("res_split", [1, 3, FEAT], BF16)
        w_nat, mask, a_col = tmp("w_nat", [P, FC, FEAT]), tmp("mask", [P, FC, HEADS]), tmp("a_col", [P, 2, FC])
        masked = tmp("masked", [P, 2, FC, HEADS])
        wvT, qk_col, qk_all = tmp("wvT", [P, FC, FEAT]), tmp("qk_col", [P, 2, FC]), tmp("qk_all", [P, 2, FC, P])
        bv_col, bv_all, qk_sum, qk_b = tmp("bv_col", [P, FC]), tmp("bv_all", [P, FC, P]), tmp("qk_sum", [P, FC]), tmp("qk_b", [P, 2])
        wcT, wl, bc_col, bc_all = tmp("wcT", [P, FEAT]), tmp("wl", [P, FEAT]), tmp("bc_col", [P, 1]), tmp("bc_all", [P, P])
        stats = tmp("bias_stats", [P, 6])

        def chunks(ap):
            return ap.rearrange("(c p) n -> p c n", p=P)

        def column(ap):
            return ap.rearrange("(c p) o -> p (c o)", p=P)
        loads = [
            (m.w1d[:], chunks(d.L0_W1[0:FEAT, :])), (m.w1b[:], chunks(d.L0_W1[FEAT:2 * FEAT, :])),
            (m.w2[:], chunks(d.L0_W2)), (m.b2[:], d.L0_b2.partition_broadcast(P)), (b1_row[:], d.L0_b1.unsqueeze(0)),
            (m.w_src[:, :, 0:FEAT], chunks(d.L1_WT)), (w_nat[:], chunks(d.L1_W)), (mask[:], chunks(d.head_mask)),
            (a_col[:, 0, :], column(d.L1_a_src)), (a_col[:, 1, :], column(d.L1_a_dst)),
            (m.w_enc[0:EDGE_FEAT, :], d.L1_eWT), (m.w_enc[EDGE_FEAT:EDGE_FEAT + 1, :], d.L1_eb.unsqueeze(0)),
            (m.bias[:], d.L1_bias.partition_broadcast(P)),
            (m.wv[:], chunks(d.L2_Wv)), (wvT[:], chunks(d.L2_WvT)), (m.bv[:], d.L2_bv.partition_broadcast(P)),
            (qk_col[:, 0, :], column(d.L2_wq)), (qk_col[:, 1, :], column(d.L2_wk)),
            (bv_col[:], column(d.L2_bv.unsqueeze(1))),
            (qk_b[:, 0:1], d.L2_bq.partition_broadcast(P)), (qk_b[:, 1:2], d.L2_bk.partition_broadcast(P)),
            (wcT[:], d.L3_WcT), (wl[:], d.L3_Wl), (bc_col[:], d.L3_bc), (m.res_bias[:], d.L3_bl.partition_broadcast(P)),
        ]

        @block.sync
        def _(sp):
            with nc.allow_non_contiguous_dma("columns of small vectors"):
                for to, frm in loads:
                    sp.dma_start(to, frm).then_inc(s.load_done, 16)
            sp.wait_ge(s.parts_done, 1)
            sp.dma_start(m.b1_parts[:], b1_split[:].rearrange("o k n -> o (k n)")).then_inc(s.parts_in, 16)
            sp.dma_start(m.res_parts[:], res_split[:].rearrange("o k n -> o (k n)")).then_inc(s.parts_in, 16)
            sp.wait_ge(s.parts_in, 32)

        @block.gpsimd
        def _(pool):
            pool.memset(m.ident[:], 0.0).then_inc(s.ident_done, 1)
            pool.wait_ge(s.ident_done, 1)
            pool.affine_select(out=m.ident[:], in_=m.ident[:], compare_op=ALU.not_equal, fill=1.0,
                               base=0, pattern=[[-1, P]], channel_multiplier=1).then_inc(s.ident_done, 1)
            pool.memset(m.eps[:], EPS)
            pool.memset(m.ones3[:], 1.0).then_inc(s.const_done, 1)

        @block.tensor
        def _(pe):
            pe.wait_ge(s.masked, 1)
            for k in range(2):
                for c in range(FC):
                    at = (k * FC + c) * HEADS
                    for o in range(FC):
                        pe.matmul(m.bank[0][:, at:at + HEADS], w_nat[:, o, c * P:(c + 1) * P], masked[:, k, o, :],
                                  start=o == 0, stop=o == FC - 1)
            for k in range(2):
                for o in range(FC):
                    pe.matmul(m.bank[1][:, k * FEAT:(k + 1) * FEAT], qk_all[:, k, o, :], wvT[:, o, :],
                              start=o == 0, stop=o == FC - 1)
            for o in range(FC):
                pe.matmul(m.bank[2][:, 0:1], bv_all[:, o, :], qk_sum[:, o:o + 1], start=o == 0, stop=o == FC - 1)
            for c in range(FC):
                pe.matmul(m.bank[3][:, c * FEAT:(c + 1) * FEAT], wcT[:, c * P:(c + 1) * P], wl[:], start=True, stop=True)
            pe.matmul(m.bank[4][:, 0:FEAT], bc_all[:], wl[:], start=True, stop=True).then_inc(s.prod_done, 1)

        @block.vector
        def _(dve):
            link = Chain(dve, s.dve_chain)

            def split(row, parts, n):
                link(dve.tensor_copy(parts[:, 0, :], row))
                link(dve.tensor_tensor(rest[:, 0:n], row, parts[:, 0, :], ALU.subtract))
                link(dve.tensor_copy(parts[:, 1, :], rest[:, 0:n]))
                link(dve.tensor_tensor(rest[:, 0:n], rest[:, 0:n], parts[:, 1, :], ALU.subtract))
                return dve.tensor_copy(parts[:, 2, :], rest[:, 0:n])

            dve.wait_ge(s.load_done, 16 * len(loads))
            link(dve.tensor_tensor(m.w1d[:], m.w1d[:], m.w1b[:], ALU.subtract))
            for k in range(2):
                for o in range(FC):
                    dve.tensor_scalar(masked[:, k, o, :], mask[:, o, :], a_col[:, k, o:o + 1], None, ALU.mult)
                    dve.tensor_copy(qk_all[:, k, o, :], qk_col[:, k, o:o + 1].to_broadcast([P, P]))
            for o in range(FC):
                dve.tensor_copy(bv_all[:, o, :], bv_col[:, o:o + 1].to_broadcast([P, P]))
            dve.tensor_tensor(qk_sum[:], qk_col[:, 0, :], qk_col[:, 1, :], ALU.add)
            link(dve.tensor_copy(bc_all[:], bc_col[:].to_broadcast([P, P])))
            dve.sem_inc(s.masked, 1)
            link(dve.bn_stats(stats[:], m.bias[:]))
            dve.nop(nofuse=True)
            link(dve.bn_aggr(m.bias_mv[:], stats[:]))
            dve.tensor_scalar(m.bias_var_eps[:], m.bias_mv[:, 1:2], EPS, None, ALU.add)
            link(split(b1_row[:], b1_split, HIDDEN))
            dve.wait_ge(s.prod_done, 1)
            dve.wait_ge(s.ident_done, 2)
            dve.tensor_copy(m.w_src[:, :, FEAT:FEAT + HEADS],
                            m.bank[0][:, 0:FC * HEADS].rearrange("p (c h) -> p c h", c=FC))
            dve.tensor_copy(m.w_dst[:], m.bank[0][:, FC * HEADS:2 * FC * HEADS].rearrange("p (c h) -> p c h", c=FC))
            dve.tensor_copy(m.q_row[:], m.bank[1][:, 0:FEAT])
            dve.tensor_copy(m.k_row[:], m.bank[1][:, FEAT:2 * FEAT])
            dve.tensor_tensor(m.qk_bias[:], qk_b[:, 0:1], qk_b[:, 1:2], ALU.add)
            dve.tensor_copy(m.w_gcn[:], m.bank[3][:].rearrange("p (c n) -> p c n", c=FC))
            link(dve.tensor_tensor(m.res_bias[:], m.bank[4][:, 0:FEAT], m.res_bias[:], ALU.add))
            dve.tensor_tensor(m.qk_bias[:], m.bank[2][:, 0:1], m.qk_bias[:], ALU.add)
            link(dve.tensor_copy(m.w_res[:], m.w_gcn[:]))
            for c in range(FC):
                block_c = m.w_res[:, c, c * P:(c + 1) * P]
                dve.tensor_tensor(block_c, block_c, m.ident[:], ALU.add)
            split(m.res_bias[0:1, :], res_split, FEAT).then_inc(s.parts_done, 1)


def scan_rows(dve, link, m, s, w, vals, out, heads, n, kind):
    back = kind == "back"
    weight, op0, op1, start, which = {
        "max": (m.pen_f, ALU.add, ALU.max, LOW, 0), "sum": (m.keep, ALU.mult, ALU.add, 0.0, 1),
        "back": (m.pen_b, ALU.add, ALU.max, LOW, 2)}[kind]
    turn = slice(None, None, -1) if back else slice(None)

    def scans(initial):
        for h in range(heads):
            for b in range(BLOCKS):
                first = start if initial is None else initial[:, b, h:h + 1]
                ins = dve.tensor_tensor_scan(out[:, h, b, turn], weight[:, b, turn], vals[:, h, b, turn],
                                             first, op0, op1)
        return ins

    link(scans(None))
    dve.tensor_copy(w.total[:, :, 0:heads].rearrange("r b h -> r h b"),
                    out[:, :, :, 0 if back else P - 1]).then_inc(s.totals_ready, 1)
    link(dve.memset(w.between[0:heads, TILES if back else 0:TILES + 1 if back else 1], start))
    dve.wait_ge(s.totals_in_row, n + 1)
    tot = m.bank[0][0:heads, 0:TILES]
    opens = m.open_row[0:heads, which, :]
    if back:
        dve.tensor_tensor_scan(w.between[0:heads, 0:TILES][:, ::-1], opens[:, ::-1], tot[:, ::-1], start,
                               op0, op1).then_inc(s.between_ready, 1)
    else:
        dve.tensor_tensor_scan(w.between[0:heads, 1:TILES + 1], opens, tot, start,
                               op0, op1).then_inc(s.between_ready, 1)
    dve.wait_ge(s.carry_ready, n + 1)
    link(dve.tensor_copy(w.carry[:, :, 0:heads],
                         m.bank[1][0:ROWS, 0:BLOCKS * heads].rearrange("r (b h) -> r b h", b=BLOCKS)))
    link(scans(w.carry))


def scan_rows_pe(pe, m, s, w, heads, n, back):
    pe.wait_ge(s.totals_ready, n + 1)
    for b in range(BLOCKS):
        ins = pe.transpose(m.bank[0][0:heads, b * ROWS:(b + 1) * ROWS], w.total[:, b, 0:heads],
                           m.ident[0:ROWS, 0:ROWS])
    ins.then_inc(s.totals_in_row, 1)
    pe.wait_ge(s.between_ready, n + 1)
    for b in range(BLOCKS):
        at = b * ROWS + (1 if back else 0)
        ins = pe.transpose(m.bank[1][0:ROWS, b * heads:(b + 1) * heads], w.between[0:heads, at:at + ROWS],
                           m.ident[0:heads, 0:heads])
    ins.then_inc(s.carry_ready, 1)


SCAN_SEMS = ["totals_ready", "totals_in_row", "between_ready", "carry_ready"]


def structure(nc, d, m, outer):
    names = ["rows_in", "ids_ready", "dve_chain", "rows_out", "flags_ready", "opens_ready", "cols_ready",
             "cols_done", "map_ready", "map_in", "act_done", "deg_ready", "flat_in"] + SCAN_SEMS
    ctx, s = phase(nc, "structure", names)
    R = [ROWS, BLOCKS, P]
    with ctx:
        def sb(name, shape, dt=F32):
            return ctx.enter_context(nc.sbuf_tensor(name, shape, dt))
        dst_i, prev_i, next_i, src_i, id_i = (sb(n, R, I32) for n in ("dst_i", "prev_i", "next_i", "src_i", "id_i"))
        dst, prev, nxt, src, eid, first = (sb(n, R) for n in ("dst_r", "prev_r", "next_r", "src_r", "id_r", "first_r"))
        count, end = sb("count_r", [ROWS, 1, BLOCKS, P]), sb("end_r", [ROWS, 1, BLOCKS, P])
        ones = sb("ones_r", [ROWS, 1, BLOCKS, P])
        map_i = sb("map_r", R)
        opens = sb("opens_r", [ROWS, BLOCKS, 3, HEADS])
        flag = sb("flag_r", [ROWS, BLOCKS, 2])
        nowhere = sb("nowhere", [P, MAP_COLS], I32)
        gathered = sb("dst_gather", [P, TILES])
        w = ScanSpace(total=sb("total_s", [ROWS, BLOCKS, HEADS]), between=sb("between_s", [HEADS, TILES + 1]),
                            carry=sb("carry_s", [ROWS, BLOCKS, HEADS]))
        flat = [(dst_i, d.dst_pad, 1), (prev_i, d.dst_pad, 0), (next_i, d.dst_pad, 2), (src_i, d.src_pad, 0)]
        cols = [dst, src, map_i, eid, count[:, 0], end[:, 0]]

        with nc.Block() as block:
            @block.sync
            def _(sp):
                for to, frm, off in flat:
                    sp.dma_start(to[:], frm[off:off + EPAD].rearrange("(b r e) -> r b e", b=BLOCKS, e=P))\
                      .then_inc(s.rows_in, 16)
                sp.wait_ge(s.rows_out, 1)
                sp.dma_start(m.dst_f[1:1 + EPAD].rearrange("(b r e) -> r b e", b=BLOCKS, e=P), dst[:])\
                  .then_inc(s.flat_in, 16)
                sp.dma_start(m.dst_f[0:1].unsqueeze(0), prev[0:1, 0, 0:1]).then_inc(s.flat_in, 16)
                sp.wait_ge(s.map_ready, 1)
                sp.dma_start(m.node_map.rearrange("(p c) o -> p (c o)", p=P), nowhere[:]).then_inc(s.map_in, 16)
                sp.wait_ge(s.flat_in, 32)
                sp.wait_ge(s.map_in, 16)

            @block.gpsimd
            def _(pool):
                pool.iota(id_i[:], pattern=[[ROWS * P, BLOCKS], [1, P]], base=0, channel_multiplier=P)\
                    .then_inc(s.ids_ready, 1)
                pool.memset(nowhere[:], NOWHERE).then_inc(s.map_ready, 1)

            @block.scalar
            def _(act):
                act.wait_ge(s.deg_ready, 1)
                act.activation(m.sdeg[:], m.sdeg[:], ACT.Sqrt).then_inc(s.act_done, 1)

            @block.vector
            def _(dve):
                link = Chain(dve, s.dve_chain)
                dve.wait_ge(s.rows_in, 16 * len(flat))
                dve.wait_ge(s.ids_ready, 1)
                for to, frm in ((dst, dst_i), (prev, prev_i), (nxt, next_i), (src, src_i), (eid, id_i)):
                    ins = dve.tensor_copy(to[:], frm[:])
                link(ins)
                dve.sem_inc(s.rows_out, 1)
                dve.tensor_tensor(m.keep[:], dst[:], prev[:], ALU.is_equal)
                dve.tensor_tensor(first[:], dst[:], prev[:], ALU.not_equal)
                link(dve.tensor_tensor(m.last[:], dst[:], nxt[:], ALU.not_equal))
                dve.tensor_scalar(m.pen_f[:], first[:], LOW, None, ALU.mult)
                dve.tensor_scalar(m.pen_b[:], m.last[:], LOW, None, ALU.mult)
                dve.tensor_scalar(map_i[:], m.last[:], -float(NOWHERE), float(NOWHERE), ALU.mult, ALU.add)
                dve.tensor_reduce(flag[:, :, 0:1], first[:], AX.X, ALU.max)
                link(dve.tensor_reduce(flag[:, :, 1:2], m.last[:], AX.X, ALU.max))
                dve.tensor_tensor(map_i[:], map_i[:], dst[:], ALU.add)
                for h in range(HEADS):
                    dve.tensor_scalar(opens[:, :, 0, h:h + 1], flag[:, :, 0:1], LOW, None, ALU.mult)
                    dve.tensor_scalar(opens[:, :, 1, h:h + 1], flag[:, :, 0:1], -1.0, 1.0, ALU.mult, ALU.add)
                    ins = dve.tensor_scalar(opens[:, :, 2, h:h + 1], flag[:, :, 1:2], LOW, None, ALU.mult)
                ins.then_inc(s.flags_ready, 1)
                link(dve.memset(ones[:], 1.0))
                dve.wait_ge(s.opens_ready, 1)
                link(dve.tensor_copy(m.open_row[:, 0:2, :], m.bank[2][0:HEADS, 0:2 * TILES].rearrange("h (k t) -> h k t", k=2)))
                link(dve.tensor_copy(m.open_row[:, 2, :], m.bank[3][0:HEADS, 0:TILES]))
                scan_rows(dve, link, m, s, w, ones, count, 1, 0, "sum")
                scan_rows(dve, link, m, s, w, eid[:].unsqueeze(1), end, 1, 1, "back")
                dve.sem_inc(s.cols_ready, 1)
                dve.wait_ge(s.cols_done, 1)
                c = [m.bank[4 + k // 2][:, (k % 2) * TILES:(k % 2 + 1) * TILES] for k in range(len(cols))]
                dve.tensor_copy(m.dst[:], c[0])
                dve.tensor_copy(m.idx_l0[:, :, 0], c[1])
                dve.tensor_scalar(gathered[:], c[0], float(NODES - 1), None, ALU.min)
                dve.tensor_copy(m.map_idx[:], c[2])
                dve.tensor_copy(m.edge_id[:], c[3])
                dve.tensor_copy(m.indeg[:], c[4])
                link(dve.tensor_copy(m.idx_l1[:, :, 1], c[5]))
                dve.tensor_copy(m.idx_l0[:, :, 1], gathered[:])
                dve.tensor_scalar(m.rdeg[:], m.indeg[:], 1e-8, None, ALU.add)
                link(dve.tensor_scalar(m.sdeg[:], m.indeg[:], 1.0, None, ALU.add))
                dve.sem_inc(s.deg_ready, 1)
                link(dve.reciprocal(m.rdeg[:], m.rdeg[:]))
                dve.tensor_tensor(m.degr[:], m.indeg[:], m.rdeg[:], ALU.mult)
                dve.wait_ge(s.act_done, 1)
                link(dve.reciprocal(m.dinv[:], m.sdeg[:]))

            @block.tensor
            def _(pe):
                pe.wait_ge(s.flags_ready, 1)
                for k in range(3):
                    for b in range(BLOCKS):
                        at = (k % 2) * TILES + b * ROWS
                        ins = pe.transpose(m.bank[2 + k // 2][0:HEADS, at:at + ROWS], opens[:, b, k, :],
                                           m.ident[0:ROWS, 0:ROWS])
                ins.then_inc(s.opens_ready, 1)
                scan_rows_pe(pe, m, s, w, 1, 0, False)
                scan_rows_pe(pe, m, s, w, 1, 1, True)
                pe.wait_ge(s.cols_ready, 1)
                for k, rows in enumerate(cols):
                    for b in range(BLOCKS):
                        at = (k % 2) * TILES + b * ROWS
                        ins = pe.transpose(m.bank[4 + k // 2][:, at:at + ROWS], rows[:, b, :],
                                           m.ident[0:ROWS, 0:ROWS])
                ins.then_inc(s.cols_done, 1)


def load_key(sp, m, s, key, k):
    hold(sp, s.sel_done, k.t - (UNROLL - 1))
    frm = m.dst_f[k.t * P:k.t * P + P + 1] if isinstance(k.t, int) else m.dst_f[bass.ds(k.t * P, P + 1)]
    sp.dma_start(key[:, k.slot, :], frm.partition_broadcast(P)).then_inc(s.key_in[k.slot], 16)


def norm_stats(dve, s, y, stats, mv, k, y_sem):
    dve.wait_ge(y_sem, k.t + 1)
    dve.bn_stats(stats[:, k.pair, :], y[:, k.pair, :]).then_inc(s.bn_done, 1)
    wait(dve, s.root_done, k.t - 1)
    hold(dve, s.bn_done, k.t + 1)
    dve.bn_aggr(mv[:, k.pair, :], stats[:, k.pair, :]).then_inc(s.mv_done, 1)


def norm_root(act, m, s, mv, root, k):
    act.wait_ge(s.mv_done, k.t + 1)
    wait(act, s.rows_done, k.t - 1)
    act.activation(root[:, k.pair, :], mv[:, k.pair, 1:2], ACT.Sqrt, bias=m.eps[:]).then_inc(s.root_done, 1)


def edge_mlp(nc, d, m):
    names = ["idx_staged", "tr_done", "evac_done", "hid_done", "relu_done", "sel_done", "agg_done",
             "carry_done", "proj_done", "res_done", "y_done", "bn_done", "mv_done", "root_done", "recip_done",
             "rows_done", "zero_done", "map_staged"]
    rings = ["src_in", "dst_in", "key_in", "src_out", "state_out", "map_out"]
    ctx, s = phase(nc, "edge_mlp", names, rings)
    with ctx:
        def sb(name, shape, dt=F32):
            return ctx.enter_context(nc.sbuf_tensor("mlp_" + name, shape, dt))
        idx = sb("idx", [P, UNROLL, 2], I32)
        map_at, map_val = sb("map_at", [P, UNROLL], I32), sb("map_val", [P, UNROLL], I32)
        xs, xd = sb("xs", [P, UNROLL, FEAT]), sb("xd", [P, UNROLL, FEAT])
        key = sb("key", [P, UNROLL, P + 1])
        xT = sb("xT", [P, 2, 2 * FEAT])
        hid = sb("hid", [P, 2, HIDDEN])
        same, cont = sb("same", [P, UNROLL, P]), sb("cont", [P, UNROLL, P])
        aggT = sb("aggT", [P, 2, HC, P])
        res, y, rows = sb("res", [P, UNROLL, FEAT]), sb("y", [P, 2, FEAT]), sb("rows", [P, UNROLL, FEAT])
        stats, mv = sb("stats", [P, 2, 6]), sb("mv", [P, 2, 2])
        root, rstd = sb("root", [P, 2, 1]), sb("rstd", [P, 2, 1])
        p_tr, p_hid, p_agg, p_out = (m.bank[2 * i:2 * i + 2] for i in range(4))

        with nc.Block() as block:
            @block.gpsimd
            def _(pool):
                def step(g, u):
                    if k := tile_at(g, u, 0):
                        hold(pool, s.src_in[k.slot], 16 * k.turn)
                        hold(pool, s.dst_in[k.slot], 16 * k.turn)
                        now = m.idx_l0[:, k.t, :] if isinstance(k.t, int) else \
                            m.idx_l0[:, bass.ds(k.t, 1), :].rearrange("p o k -> p (o k)")
                        pool.tensor_copy(idx[:, k.slot, :], now).then_inc(s.idx_staged, 1)
                        hold(pool, s.tr_done, k.t - (UNROLL - 1))
                        hold(pool, s.src_out[k.slot], 16 * k.turn)
                        hold(pool, s.res_done, k.t - (UNROLL - 1))
                        hold(pool, s.idx_staged, k.t + 1)
                        pool.indirect_dma_start(xs[:, k.slot, :], None, d.x,
                                                bass.IndirectOffsetOnAxis(ap=idx[:, k.slot, 0:1], axis=0))\
                            .then_inc(s.src_in[k.slot], 16)
                        pool.indirect_dma_start(xd[:, k.slot, :], None, d.x,
                                                bass.IndirectOffsetOnAxis(ap=idx[:, k.slot, 1:2], axis=0))\
                            .then_inc(s.dst_in[k.slot], 16)
                        hold(pool, s.map_out[k.slot], 16 * k.turn)
                        pool.tensor_copy(map_at[:, k.slot:k.slot + 1], col(m.map_idx, k.t))
                        pool.tensor_copy(map_val[:, k.slot:k.slot + 1], col(m.edge_id, k.t)).then_inc(s.map_staged, 1)
                        hold(pool, s.map_staged, k.t + 1)
                        pool.indirect_dma_start(m.node_map,
                                                bass.IndirectOffsetOnAxis(ap=map_at[:, k.slot:k.slot + 1], axis=0),
                                                map_val[:, k.slot:k.slot + 1], None,
                                                bounds_check=NODES - 1, oob_is_err=False)\
                            .then_inc(s.map_out[k.slot], 16)
                run_steps(pool, step, 0)
                for slot in range(UNROLL):
                    pool.wait_ge(s.map_out[slot], 16 * (TILES // UNROLL))

            @block.sync
            def _(sp):
                def step(g, u):
                    if k := tile_at(g, u, 0):
                        load_key(sp, m, s, key, k)
                    if k := tile_at(g, u, 1):
                        hold(sp, s.src_in[k.slot], 16 * (k.turn + 1))
                        sp.dma_start(tile_rows(m.x_src, k.t), xs[:, k.slot, :]).then_inc(s.src_out[k.slot], 16)
                    if k := tile_at(g, u, 4):
                        hold(sp, s.rows_done, k.t + 1)
                        sp.dma_start(tile_rows(m.state[1], k.t), rows[:, k.slot, :]).then_inc(s.state_out[k.slot], 16)
                run_steps(sp, step, 4)
                for slot in range(UNROLL):
                    sp.wait_ge(s.src_out[slot], 16 * (TILES // UNROLL))
                    sp.wait_ge(s.state_out[slot], 16 * (TILES // UNROLL))

            @block.tensor
            def _(pe):
                def step(g, u):
                    if k := tile_at(g, u, 0):
                        pe.wait_ge(s.src_in[k.slot], 16 * (k.turn + 1))
                        pe.wait_ge(s.dst_in[k.slot], 16 * (k.turn + 1))
                        wait(pe, s.evac_done, k.t - 1)
                        for c in range(FC):
                            pe.transpose(p_tr[k.pair][:, c * P:(c + 1) * P], xd[:, k.slot, c * P:(c + 1) * P], m.ident[:])
                        for c in range(FC):
                            ins = pe.transpose(p_tr[k.pair][:, FEAT + c * P:FEAT + (c + 1) * P],
                                               xs[:, k.slot, c * P:(c + 1) * P], m.ident[:])
                        ins.then_inc(s.tr_done, 1)
                    if k := tile_at(g, u, 1):
                        pe.wait_ge(s.evac_done, k.t + 1)
                        wait(pe, s.relu_done, k.t - 1)
                        pe.matmul(p_hid[k.pair][:], m.ones3[:], m.b1_parts[:], start=True, stop=False)
                        for c in range(2 * FC):
                            wgt = m.w1d[:, c, :] if c < FC else m.w1b[:, c - FC, :]
                            ins = pe.matmul(p_hid[k.pair][:], xT[:, k.pair, c * P:(c + 1) * P], wgt,
                                            start=False, stop=c == 2 * FC - 1)
                        ins.then_inc(s.hid_done, 1)
                    if k := tile_at(g, u, 2):
                        pe.wait_ge(s.relu_done, k.t + 1)
                        pe.wait_ge(s.sel_done, k.t + 1)
                        wait(pe, s.carry_done, k.t - 1)
                        for c in range(HC):
                            ins = pe.matmul(p_agg[k.pair][:, c * P:(c + 1) * P], hid[:, k.pair, c * P:(c + 1) * P],
                                            same[:, k.slot, :], start=True, stop=True)
                        ins.then_inc(s.agg_done, 1)
                    if k := tile_at(g, u, 3):
                        pe.wait_ge(s.carry_done, k.t + 1)
                        wait(pe, s.y_done, k.t - 1)
                        for c in range(HC):
                            ins = pe.matmul(p_out[k.pair][:, 0:FEAT], aggT[:, k.pair, c, :], m.w2[:, c, :],
                                            start=c == 0, stop=c == HC - 1)
                        ins.then_inc(s.proj_done, 1)
                run_steps(pe, step, 3)

            @block.scalar
            def _(act):
                def step(g, u):
                    if k := tile_at(g, u, 0):
                        act.wait_ge(s.tr_done, k.t + 1)
                        wait(act, s.hid_done, k.t - 1)
                        act.copy(xT[:, k.pair, :], p_tr[k.pair][:]).then_inc(s.evac_done, 1)
                    if k := tile_at(g, u, 1):
                        act.wait_ge(s.hid_done, k.t + 1)
                        wait(act, s.agg_done, k.t - 1)
                        act.activation(hid[:, k.pair, :], p_hid[k.pair][:], ACT.Relu).then_inc(s.relu_done, 1)
                    if k := tile_at(g, u, 3):
                        norm_root(act, m, s, mv, root, k)
                run_steps(act, step, 3)

            @block.vector
            def _(dve):
                dve.memset(aggT[:, 1, :, P - 1], 0.0).then_inc(s.zero_done, 1)
                dve.wait_ge(s.zero_done, 1)

                def step(g, u):
                    if k := tile_at(g, u, 1):
                        dve.wait_ge(s.key_in[k.slot], 16 * (k.turn + 1))
                        wait(dve, s.agg_done, k.t - (UNROLL - 1))
                        dve.tensor_scalar(cont[:, k.slot, :], key[:, k.slot, 1:P + 1], key[:, k.slot, 0:1], None, ALU.is_equal)
                        dve.tensor_scalar(same[:, k.slot, :], key[:, k.slot, 1:P + 1], col(m.dst, k.t), None,
                                          ALU.is_equal).then_inc(s.sel_done, 1)
                        dve.wait_ge(s.dst_in[k.slot], 16 * (k.turn + 1))
                        dve.scalar_tensor_tensor(res[:, k.slot, :], m.b2[:], col(m.degr, k.t), xd[:, k.slot, :],
                                                 ALU.mult, ALU.add).then_inc(s.res_done, 1)
                    if k := tile_at(g, u, 2):
                        dve.wait_ge(s.agg_done, k.t + 1)
                        dve.wait_ge(s.sel_done, k.t + 1)
                        wait(dve, s.proj_done, k.t - 1)
                        wait(dve, s.carry_done, k.t)
                        for c in range(HC):
                            ins = dve.scalar_tensor_tensor(aggT[:, k.pair, c, :], cont[:, k.slot, :],
                                                           aggT[:, 1 - k.pair, c, P - 1:P],
                                                           p_agg[k.pair][:, c * P:(c + 1) * P], ALU.mult, ALU.add)
                        ins.then_inc(s.carry_done, 1)
                    if k := tile_at(g, u, 3):
                        dve.wait_ge(s.proj_done, k.t + 1)
                        dve.wait_ge(s.res_done, k.t + 1)
                        wait(dve, s.rows_done, k.t - 1)
                        dve.scalar_tensor_tensor(y[:, k.pair, :], p_out[k.pair][:, 0:FEAT], col(m.rdeg, k.t),
                                                 res[:, k.slot, :], ALU.mult, ALU.add).then_inc(s.y_done, 1)
                        norm_stats(dve, s, y, stats, mv, k, s.y_done)
                    if k := tile_at(g, u, 4):
                        dve.wait_ge(s.root_done, k.t + 1)
                        dve.reciprocal(rstd[:, k.pair, :], root[:, k.pair, :]).then_inc(s.recip_done, 1)
                        dve.wait_ge(s.recip_done, k.t + 1)
                        wait(dve, s.state_out[k.slot], 16 * k.turn)
                        dve.tensor_scalar(rows[:, k.slot, :], y[:, k.pair, :], mv[:, k.pair, 0:1], rstd[:, k.pair, :],
                                          ALU.subtract, ALU.mult).then_inc(s.rows_done, 1)
                run_steps(dve, step, 4)


AFFINE_LINKS = 13


def affine_scalars(dve, link, s, m, n, base, mean, var, cov, root, out, tmp):
    r1, r3, t, u = tmp
    alpha, beta, gamma = out
    bm, bv = m.bias_mv[0:n, 0:1], m.bias_mv[0:n, 1:2]
    dve.wait_ge(s.aff_root, base + 1)
    link(dve.reciprocal(r1, root))
    link(dve.scalar_tensor_tensor(t, mean, bm, cov, ALU.mult, ALU.subtract))
    link(dve.tensor_tensor(t, t, r1, ALU.mult))
    link(dve.tensor_tensor(u, r1, r1, ALU.mult))
    link(dve.tensor_tensor(u, u, var, ALU.mult))
    link(dve.scalar_tensor_tensor(u, t, -2.0, u, ALU.mult, ALU.add))
    dve.tensor_scalar(cov, u, bv, None, ALU.add).then_inc(s.aff_ask, 1)
    link(dve.tensor_tensor(t, r1, mean, ALU.mult))
    link(dve.tensor_scalar(t, t, bm, -1.0, ALU.add, ALU.mult))
    dve.wait_ge(s.aff_root, base + 2)
    link(dve.reciprocal(beta, root))
    link(dve.tensor_tensor(u, beta, beta, ALU.mult))
    dve.tensor_tensor(cov, cov, u, ALU.mult).then_inc(s.aff_ask, 1)
    link(dve.tensor_tensor(alpha, r1, beta, ALU.mult))
    link(dve.tensor_tensor(gamma, t, beta, ALU.mult))
    dve.wait_ge(s.aff_root, base + 3)
    link(dve.reciprocal(r3, root))


def affine_roots(act, s, m, n, base, var, cov, root):
    for k, v in enumerate((var, cov, cov)):
        act.wait_ge(s.aff_ask, base + k + 1)
        act.activation(root, v, ACT.Sqrt, bias=m.eps[0:n]).then_inc(s.aff_root, 1)


def untouched_nodes(nc, d, m, out, n, first, tiles, unroll, batch, piece):
    main = tiles > 1
    pieces, slots = unroll // piece, min(2 * piece, unroll)
    names = ["seen", "dve_chain", "aff_ask", "aff_root", "scalars_done", "scaled", "tr_done", "evac_done",
             "proj_done", "bn_done", "mv_done", "root_done", "recip_done", "rows_done", "bn2_done",
             "staged", "x3_done", "norm_chain"]
    ctx, s = phase(nc, "untouched" if main else "tail", names, (),
                   [("x_in", pieces), ("out_done", 2), ("found", 5)])
    with ctx:
        tag = "main_" if main else "tail_"

        def sb(name, shape, dt=F32):
            return ctx.enter_context(nc.sbuf_tensor(tag + name, shape, dt))
        xin = sb("xin", [n, unroll, FEAT])
        stats, junk = sb("stats", [n, 2, 6]), sb("junk", [n, 2, FEAT])
        mom = sb("moments", [n, 2, 3, batch])
        root_b, out2, tmp = sb("root_b", [n, batch]), sb("out2", [n, 3, batch]), sb("tmpb", [n, 4, batch])
        aff = sb("aff", [n, 2, 3, batch])
        x3, x3T = sb("x3", [n, 2, FEAT]), sb("x3T", [P, 2, FC, n])
        ystats, mv = sb("ystats", [n, 2, 6]), sb("mv", [n, 2, 2])
        root, rstd, shift = sb("root", [n, 2, 1]), sb("rstd", [n, 2, 1]), sb("shift", [n, 2, 1])
        yrows = sb("yrows", [n, slots, FEAT])
        stage, pos = sb("stage", [P, 5], I32), sb("pos", [P, 5], I32)
        p_tr, p_out = m.bank[0:2], m.bank[2:4]
        x_at = d.x[first:first + n * tiles, :].rearrange("(p k) f -> p (k f)", p=n)
        out_at = out[first:first + n * tiles, :].rearrange("(p k) f -> p (k f)", p=n)

        def at(g, u, lag):
            return tile_at(g, u, lag, unroll, tiles)

        def steps(eng, step, lag):
            run_steps(eng, step, lag, unroll, tiles)

        def batch_of(g, u, lag):
            v = u - lag
            return g * (unroll // batch) + v // batch, v % unroll // batch, v % batch

        def piece_ap(ap, t):
            size = piece * FEAT
            return ap[:, t * FEAT:t * FEAT + size] if isinstance(t, int) else ap[:, bass.ds(t * FEAT, size)]
        B = batch

        with nc.Block() as block:
            @block.sync
            def _(sp):
                def step(g, u):
                    if (k := at(g, u, 0)) and u % piece == 0:
                        hold(sp, s.x3_done, k.t - unroll + piece)
                        sp.dma_start(xin[:, k.slot:k.slot + piece, :].rearrange("p k f -> p (k f)"), piece_ap(x_at, k.t))\
                          .then_inc(s.x_in[k.slot // piece], 16)
                    v = u - (B + 3)
                    if (k := at(g, u, B + 3)) and v % piece == piece - 1:
                        slot = (v % slots) // piece
                        hold(sp, s.rows_done, k.t + 1)
                        lo = slot * piece
                        sp.dma_start(piece_ap(out_at, k.t - (piece - 1)),
                                     yrows[:, lo:lo + piece, :].rearrange("p k f -> p (k f)"))\
                          .then_inc(s.out_done[slot], 16)
                steps(sp, step, B + 3)
                stores = tiles // piece
                for slot in range(2):
                    hold(sp, s.out_done[slot], 16 * ((stores + 1 - slot) // 2))

            @block.gpsimd
            def _(pool):
                def look_up(t, slot, turn):
                    put_away(t, slot, turn)
                    pool.tensor_copy(stage[:, slot:slot + 1], m.idx_l0[:, t:t + 1, 0] if isinstance(t, int) else
                                     m.idx_l0[:, bass.ds(t, 1), 0]).then_inc(s.staged, 1)
                    hold(pool, s.staged, t - (0 if main else TILES - 1) + 1)
                    pool.indirect_dma_start(pos[:, slot:slot + 1], None, m.node_map,
                                            bass.IndirectOffsetOnAxis(ap=stage[:, slot:slot + 1], axis=0))\
                        .then_inc(s.found[slot], 16)

                def put_away(t, slot, turn):
                    if isinstance(turn, int) and turn == 0:
                        return
                    hold(pool, s.found[slot], 16 * turn)
                    to = m.idx_l1[:, t - 5:t - 4, 0] if isinstance(t, int) else m.idx_l1[:, bass.ds(t - 5, 1), 0]
                    pool.tensor_copy(to, pos[:, slot:slot + 1])

                def step(g, u):
                    if u % 2 == 1:
                        j = u // 2
                        look_up(g * (unroll // 2) + j, j % 5, g * (unroll // 10) + j // 5)
                if main:
                    steps(pool, step, 0)
                    done = tiles // 2
                    for i in range(5):
                        put_away(done + i, (done + i) % 5, done // 5)
                else:
                    look_up(TILES - 1, 0, 0)
                    put_away(TILES + 4, 0, 1)

            @block.scalar
            def _(act):
                def step(g, u):
                    if (k := at(g, u, 0)) and u % batch == batch - 1:
                        b, slot, _ = batch_of(g, u, 0)
                        affine_roots(act, s, m, n, b * 3, mom[:, slot, 1, :], mom[:, slot, 2, :], root_b[:])
                    if k := at(g, u, B):
                        _, slot, i = batch_of(g, u, B)
                        act.wait_ge(s.scalars_done, batch_of(g, u, B)[0] + 1)
                        wait(act, s.tr_done, k.t - 1)
                        act.activation(x3[:, k.pair, :], xin[:, k.slot, :], ACT.Identity,
                                       bias=aff[:, slot, 2, i:i + 1], scale=aff[:, slot, 0, i:i + 1])\
                           .then_inc(s.scaled, 1)
                    if k := at(g, u, B + 1):
                        act.wait_ge(s.tr_done, k.t + 1)
                        wait(act, s.proj_done, k.t - 1)
                        act.copy(x3T[:, k.pair, :, :], p_tr[k.pair][:, 0:FC * n].rearrange("p (c n) -> p c n", c=FC))\
                           .then_inc(s.evac_done, 1)
                    if k := at(g, u, B + 2):
                        act.wait_ge(s.mv_done, k.t + 1)
                        wait(act, s.recip_done, k.t - 1)
                        act.activation(root[:, k.pair, :], mv[:, k.pair, 1:2], ACT.Sqrt, bias=m.eps[0:n])\
                           .then_inc(s.root_done, 1)
                    if k := at(g, u, B + 3):
                        v = u - (B + 3)
                        slot = v % slots
                        act.wait_ge(s.recip_done, k.t + 1)
                        if v % piece == 0:
                            wait(act, s.out_done[slot // piece], 16 * (k.t // (2 * piece)) if isinstance(k.t, int)
                                 else 16 * (g * (unroll // (2 * piece)) + v // (2 * piece)))
                        act.activation(yrows[:, slot, :], p_out[k.pair][0:n, 0:FEAT], ACT.Identity,
                                       bias=shift[:, k.pair, :], scale=rstd[:, k.pair, :]).then_inc(s.rows_done, 1)
                steps(act, step, B + 3)

            @block.tensor
            def _(pe):
                def step(g, u):
                    if k := at(g, u, B + 1):
                        pe.wait_ge(s.x3_done, k.t + 1)
                        wait(pe, s.evac_done, k.t - 1)
                        for c in range(FC):
                            ins = pe.transpose(p_tr[k.pair][:, c * n:(c + 1) * n], x3[:, k.pair, c * P:(c + 1) * P],
                                               m.ident[0:n, 0:n])
                        ins.then_inc(s.tr_done, 1)
                    if k := at(g, u, B + 2):
                        pe.wait_ge(s.evac_done, k.t + 1)
                        wait(pe, s.rows_done, k.t - 1)
                        pe.matmul(p_out[k.pair][0:n, 0:FEAT], m.ones3[:, 0:n], m.res_parts[:], start=True, stop=False)
                        for c in range(FC):
                            ins = pe.matmul(p_out[k.pair][0:n, 0:FEAT], x3T[:, k.pair, c, :], m.w_res[:, c, :],
                                            start=False, stop=c == FC - 1)
                        ins.then_inc(s.proj_done, 1)
                steps(pe, step, B + 2)

            @block.vector
            def _(dve):
                def step(g, u):
                    if k := at(g, u, 0):
                        b, slot, i = batch_of(g, u, 0)
                        if u % piece == 0:
                            dve.wait_ge(s.x_in[k.slot // piece], 16 * (k.turn + 1))
                        wait(dve, s.seen, k.t - 1)
                        dve.bn_stats(stats[:, k.pair, :], xin[:, k.slot, :]).then_inc(s.bn_done, 1)
                        dve.scalar_tensor_tensor(junk[:, k.pair, :], xin[:, k.slot, :], 1.0 / FEAT, m.bias[0:n], ALU.mult, ALU.mult,
                                                 accum_out=mom[:, slot, 2, i:i + 1])
                        hold(dve, s.bn_done, k.t + 1)
                        dve.bn_aggr(mom[:, slot, 0:2, i], stats[:, k.pair, :]).then_inc(s.seen, 1)
                        if i == batch - 1:
                            link = Chain(dve, s.dve_chain, b * (AFFINE_LINKS + 1))
                            hold(dve, s.seen, k.t + 1)
                            dve.sem_inc(s.aff_ask, 1)
                            tm = [tmp[:, j, :] for j in range(4)]
                            affine_scalars(dve, link, s, m, n, b * 3, *(mom[:, slot, j, :] for j in range(3)),
                                           root_b[:], [out2[:, j, :] for j in range(3)], tm)
                            wait(dve, s.x3_done, k.t + 1 - 2 * batch)
                            for j in range(3):
                                ins = dve.tensor_tensor(aff[:, slot, j, :], out2[:, j, :], tm[1], ALU.mult)
                            link(ins)
                            dve.sem_inc(s.scalars_done, 1)
                    if k := at(g, u, B):
                        _, slot, i = batch_of(g, u, B)
                        dve.wait_ge(s.scaled, k.t + 1)
                        dve.scalar_tensor_tensor(x3[:, k.pair, :], m.bias[0:n], aff[:, slot, 1, i:i + 1],
                                                 x3[:, k.pair, :], ALU.mult, ALU.add).then_inc(s.x3_done, 1)
                    if k := at(g, u, B + 2):
                        dve.wait_ge(s.proj_done, k.t + 1)
                        wait(dve, s.bn2_done, k.t - 1)
                        dve.bn_stats(ystats[:, k.pair, :], p_out[k.pair][0:n, 0:FEAT]).then_inc(s.bn2_done, 1)
                        wait(dve, s.root_done, k.t - 1)
                        hold(dve, s.bn2_done, k.t + 1)
                        dve.bn_aggr(mv[:, k.pair, :], ystats[:, k.pair, :]).then_inc(s.mv_done, 1)
                    if k := at(g, u, B + 3):
                        dve.wait_ge(s.root_done, k.t + 1)
                        wait(dve, s.rows_done, k.t - 1)
                        link = Chain(dve, s.norm_chain, k.t)
                        link(dve.reciprocal(rstd[:, k.pair, :], root[:, k.pair, :]))
                        dve.scalar_tensor_tensor(shift[:, k.pair, :], mv[:, k.pair, 0:1], -1.0, rstd[:, k.pair, :],
                                                 ALU.mult, ALU.mult).then_inc(s.recip_done, 1)
                steps(dve, step, B + 3)


def gather_pos(pool, m, s, k, to, table, idx, ready):
    pool.indirect_dma_start(to, None, table, bass.IndirectOffsetOnAxis(ap=idx, axis=0),
                            bounds_check=EPAD - 1, oob_is_err=False).then_inc(ready, 16)


def gat_scores(nc, d, m):
    names = ["idx_staged", "bn_done", "seen", "root_done", "recip_done", "scal_done", "put_done", "x1_done", "tr_done", "evac_done",
             "prod_done", "enc_done", "h_done", "mul_done", "red_done", "score_done", "dve_chain", "aff_ask", "aff_root",
             "flags_done", "ones_done"]
    rings = ["x_in", "src_in", "dst_in", "edge_in", "h_out"]
    ctx, s = phase(nc, "gat_scores", names, rings)
    with ctx:
        def sb(name, shape, dt=F32):
            return ctx.enter_context(nc.sbuf_tensor("gs_" + name, shape, dt))
        idx = sb("idx", [P, UNROLL, 2], I32)
        xs, xd = sb("xs", [P, UNROLL, FEAT]), sb("xd", [P, UNROLL, FEAT])
        edge = sb("edge", [EDGE_FEAT + 1, UNROLL, P])
        stats, mom, junk = sb("stats", [P, 2, 6]), sb("mom", [P, UNROLL, 3]), sb("junk", [P, 2, FEAT])
        root, rstd, scal = sb("root", [P, 2, 1]), sb("rstd", [P, 2, 1]), sb("scal", [P, UNROLL, 2])
        x1, xT = sb("x1", [P, 2, FEAT]), sb("xT", [P, 2, 2 * FEAT])
        enc, prod, red, h = sb("enc", [P, 2, FEAT]), sb("prod", [P, 2, FEAT]), sb("red", [P, 2, HEADS]), sb("h", [P, UNROLL, FEAT])
        root_all, tmp = sb("root_all", [P, TILES]), sb("tmp", [P, 4, TILES])
        p_tr, p_src, p_dst, p_lin = (m.bank[2 * i:2 * i + 2] for i in range(4))
        neg_un = sb("neg_un", [P, TILES])

        with nc.Block() as block:
            @block.sync
            def _(sp):
                def step(g, u):
                    if k := tile_at(g, u, 0):
                        hold(sp, s.x1_done, k.t - (UNROLL - 1))
                        hold(sp, s.seen, k.t - (UNROLL - 1))
                        sp.dma_start(xs[:, k.slot, :], tile_rows(m.x_src, k.t)).then_inc(s.x_in[k.slot], 16)
                        if k.t == 0 if isinstance(k.t, int) else False:
                            sp.wait_ge(s.ones_done, 1)
                        hold(sp, s.prod_done, k.t - (UNROLL - 1))
                        frm = d.edge_attr_T[:, k.t * P:k.t * P + P] if isinstance(k.t, int) else \
                            d.edge_attr_T[:, bass.ds(k.t * P, P)]
                        sp.dma_start(edge[0:EDGE_FEAT, k.slot, :], frm).then_inc(s.edge_in[k.slot], 16)
                    if k := tile_at(g, u, 4):
                        hold(sp, s.h_done, k.t + 1)
                        sp.dma_start(tile_rows(m.h_src, k.t), h[:, k.slot, :]).then_inc(s.h_out[k.slot], 16)
                run_steps(sp, step, 4)
                for slot in range(UNROLL):
                    sp.wait_ge(s.h_out[slot], 16 * (TILES // UNROLL))

            @block.gpsimd
            def _(pool):
                pool.memset(edge[:], 1.0).then_inc(s.ones_done, 1)

                def step(g, u):
                    if k := tile_at(g, u, 0):
                        hold(pool, s.src_in[k.slot], 16 * k.turn)
                        hold(pool, s.dst_in[k.slot], 16 * k.turn)
                        now = m.idx_l1[:, k.t, :] if isinstance(k.t, int) else \
                            m.idx_l1[:, bass.ds(k.t, 1), :].rearrange("p o k -> p (o k)")
                        pool.tensor_copy(idx[:, k.slot, :], now).then_inc(s.idx_staged, 1)
                        hold(pool, s.tr_done, k.t - (UNROLL - 1))
                        hold(pool, s.idx_staged, k.t + 1)
                        gather_pos(pool, m, s, k, xd[:, k.slot, :], m.state[1], idx[:, k.slot, 1:2], s.dst_in[k.slot])
                        hold(pool, s.x_in[k.slot], 16 * (k.turn + 1))
                        gather_pos(pool, m, s, k, xs[:, k.slot, :], m.state[1], idx[:, k.slot, 0:1], s.src_in[k.slot])
                run_steps(pool, step, 0)

            @block.scalar
            def _(act):
                def step(g, u):
                    if k := tile_at(g, u, 1):
                        act.wait_ge(s.seen, k.t + 1)
                        wait(act, s.recip_done, k.t - 1)
                        act.activation(root[:, k.pair, :], mom[:, k.slot, 1:2], ACT.Sqrt, bias=m.eps[:]).then_inc(s.root_done, 1)
                    if k := tile_at(g, u, 2):
                        act.wait_ge(s.scal_done, k.t + 1)
                        wait(act, s.tr_done, k.t - 1)
                        act.activation(x1[:, k.pair, :], xs[:, k.slot, :], ACT.Identity, bias=scal[:, k.slot, 1:2],
                                       scale=scal[:, k.slot, 0:1]).then_inc(s.x1_done, 1)
                    if k := tile_at(g, u, 3):
                        act.wait_ge(s.tr_done, k.t + 1)
                        wait(act, s.prod_done, k.t - 1)
                        act.copy(xT[:, k.pair, :], p_tr[k.pair][:]).then_inc(s.evac_done, 1)
                    if k := tile_at(g, u, 4):
                        act.wait_ge(s.prod_done, k.t + 1)
                        wait(act, s.mul_done, k.t - 1)
                        act.activation(enc[:, k.pair, :], p_dst[k.pair][:, FEAT:2 * FEAT], ACT.Relu).then_inc(s.enc_done, 1)
                        wait(act, s.h_out[k.slot], 16 * k.turn)
                        act.copy(h[:, k.slot, :], p_src[k.pair][:, 0:FEAT]).then_inc(s.h_done, 1)
                run_steps(act, step, 4)
                affine_roots(act, s, m, P, 0, m.row_stat[:, 1, :], m.row_stat[:, 2, :], root_all[:])

            @block.tensor
            def _(pe):
                def step(g, u):
                    if k := tile_at(g, u, 3):
                        pe.wait_ge(s.x1_done, k.t + 1)
                        pe.wait_ge(s.dst_in[k.slot], 16 * (k.turn + 1))
                        wait(pe, s.evac_done, k.t - 1)
                        for c in range(FC):
                            pe.transpose(p_tr[k.pair][:, c * P:(c + 1) * P], x1[:, k.pair, c * P:(c + 1) * P], m.ident[:])
                        for c in range(FC):
                            ins = pe.transpose(p_tr[k.pair][:, FEAT + c * P:FEAT + (c + 1) * P],
                                               xd[:, k.slot, c * P:(c + 1) * P], m.ident[:])
                        ins.then_inc(s.tr_done, 1)
                    if k := tile_at(g, u, 4):
                        pe.wait_ge(s.evac_done, k.t + 1)
                        pe.wait_ge(s.edge_in[k.slot], 16 * (k.turn + 1))
                        wait(pe, s.score_done, k.t - 1)
                        wait(pe, s.h_done, k.t - 1)
                        src = [xT[:, k.pair, c * P:(c + 1) * P] for c in range(FC)]
                        dst = [xT[:, k.pair, FEAT + c * P:FEAT + (c + 1) * P] for c in range(FC)]
                        for c in range(FC):
                            pe.matmul(p_src[k.pair][:, 0:FEAT], src[c], m.w_src[:, c, 0:FEAT], start=c == 0, stop=c == FC - 1)
                        linear = [(src[c], m.w_src[:, c, FEAT:FEAT + HEADS]) for c in range(FC)]
                        linear += [(dst[c], m.w_dst[:, c, :]) for c in range(FC)]
                        for i, (rows, wgt) in enumerate(linear):
                            pe.matmul(p_lin[k.pair][:, 0:HEADS], rows, wgt, start=i == 0, stop=i == len(linear) - 1)
                        for c in range(FC):
                            pe.matmul(p_dst[k.pair][:, 0:FEAT], dst[c], m.w_src[:, c, 0:FEAT], start=c == 0, stop=c == FC - 1)
                        pe.matmul(p_dst[k.pair][:, FEAT:2 * FEAT], edge[:, k.slot, :], m.w_enc[:], start=True, stop=True)\
                          .then_inc(s.prod_done, 1)
                run_steps(pe, step, 4)

            @block.vector
            def _(dve):
                dve.tensor_scalar(m.touched[:], m.idx_l1[:, :, 0], float(NOWHERE), None, ALU.is_lt)
                dve.tensor_scalar(m.untouched[:], m.idx_l1[:, :, 0], float(NOWHERE), None, ALU.is_ge)
                dve.tensor_scalar(neg_un[:], m.idx_l1[:, :, 0], float(NOWHERE), -1.0, ALU.is_ge, ALU.mult).then_inc(s.flags_done, 1)
                dve.wait_ge(s.flags_done, 1)

                def step(g, u):
                    if k := tile_at(g, u, 1):
                        dve.wait_ge(s.src_in[k.slot], 16 * (k.turn + 1))
                        wait(dve, s.seen, k.t - 1)
                        wait(dve, s.put_done, k.t - (UNROLL - 1))
                        dve.bn_stats(stats[:, k.pair, :], xs[:, k.slot, :]).then_inc(s.bn_done, 1)
                        dve.scalar_tensor_tensor(junk[:, k.pair, :], xs[:, k.slot, :], 1.0 / FEAT, m.bias[:], ALU.mult, ALU.mult,
                                                 accum_out=mom[:, k.slot, 2:3])
                        hold(dve, s.bn_done, k.t + 1)
                        dve.bn_aggr(mom[:, k.slot, 0:2], stats[:, k.pair, :]).then_inc(s.seen, 1)
                    if k := tile_at(g, u, 2):
                        dve.wait_ge(s.root_done, k.t + 1)
                        wait(dve, s.x1_done, k.t - (UNROLL - 1))
                        dve.reciprocal(rstd[:, k.pair, :], root[:, k.pair, :]).then_inc(s.recip_done, 1)
                        dve.wait_ge(s.recip_done, k.t + 1)
                        dve.scalar_tensor_tensor(scal[:, k.slot, 0:1], rstd[:, k.pair, :], col(m.untouched, k.t),
                                                 col(m.touched, k.t), ALU.mult, ALU.add)
                        dve.scalar_tensor_tensor(scal[:, k.slot, 1:2], mom[:, k.slot, 0:1], rstd[:, k.pair, :],
                                                 col(neg_un, k.t), ALU.mult, ALU.mult).then_inc(s.scal_done, 1)
                        to = m.row_stat[:, :, k.t] if isinstance(k.t, int) else \
                            m.row_stat[:, :, bass.ds(k.t, 1)].rearrange("p k o -> p (k o)")
                        dve.tensor_copy(to, mom[:, k.slot, :]).then_inc(s.put_done, 1)
                    if k := tile_at(g, u, 4):
                        dve.wait_ge(s.enc_done, k.t + 1)
                        wait(dve, s.red_done, k.t - 1)
                        dve.tensor_tensor(prod[:, k.pair, :], enc[:, k.pair, :], p_dst[k.pair][:, 0:FEAT], ALU.mult)\
                           .then_inc(s.mul_done, 1)
                        dve.wait_ge(s.mul_done, k.t + 1)
                        wait(dve, s.score_done, k.t - 1)
                        dve.tensor_reduce(red[:, k.pair, :], prod[:, k.pair, :].rearrange("p (h d) -> p h d", h=HEADS),
                                          AX.X, ALU.add).then_inc(s.red_done, 1)
                        dve.wait_ge(s.red_done, k.t + 1)
                        to = m.score[:, k.t, :] if isinstance(k.t, int) else \
                            m.score[:, bass.ds(k.t, 1), :].rearrange("p o h -> p (o h)")
                        dve.tensor_tensor(to, red[:, k.pair, :], p_lin[k.pair][:, 0:HEADS], ALU.add)\
                           .then_inc(s.score_done, 1)
                run_steps(dve, step, 4)
                dve.wait_ge(s.put_done, TILES)
                dve.sem_inc(s.aff_ask, 1)
                link = Chain(dve, s.dve_chain, 0)
                tm = [tmp[:, j, :] for j in range(4)]
                second, third = ([m.affine[:, i, j, :] for j in range(3)] for i in range(2))
                affine_scalars(dve, link, s, m, P, 0, *(m.row_stat[:, j, :] for j in range(3)), root_all[:], second, tm)
                for j in range(3):
                    ins = dve.tensor_tensor(third[j], second[j], tm[1], ALU.mult)
                link(ins)
                for part in (*second, *third):
                    ins = dve.tensor_tensor(part, part, m.untouched[:], ALU.mult)
                link(ins)
                for part in (second[0], third[0]):
                    dve.tensor_tensor(part, part, m.touched[:], ALU.add)


def softmax_rows(dve, link, act_exp, m, s, w, score, run, spread, heads, n):
    scan_rows(dve, link, m, s, w, score, run, heads, n, "max")
    scan_rows(dve, link, m, s, w, run, spread, heads, n + 1, "back")
    link(dve.tensor_tensor(score, score, spread, ALU.subtract))
    act_exp()
    scan_rows(dve, link, m, s, w, score, run, heads, n + 2, "sum")
    scan_rows(dve, link, m, s, w, run, spread, heads, n + 3, "back")


def gat_softmax(nc, m):
    ctx, s = phase(nc, "gat_softmax", ["dve_chain", "leaky_done", "in_rows", "exp_ask", "exp_done", "weights_done", "in_cols"] + SCAN_SEMS)
    with ctx:
        def sb(name, shape, dt=F32):
            return ctx.enter_context(nc.sbuf_tensor("sm_" + name, shape, dt))
        shape = [ROWS, HEADS, BLOCKS, P]
        score, run, spread = sb("score", shape), sb("run", shape), sb("spread", shape)
        w = ScanSpace(total=sb("total", [ROWS, BLOCKS, HEADS]), between=sb("between", [HEADS, TILES + 1]),
                            carry=sb("carry", [ROWS, BLOCKS, HEADS]))
        pairs = [(h, b) for h in range(HEADS) for b in range(BLOCKS)]
        with nc.Block() as block:
            @block.tensor
            def _(pe):
                pe.wait_ge(s.leaky_done, 1)
                for k, (h, b) in enumerate(pairs):
                    ins = pe.transpose(m.bank[2 + k // 4][0:ROWS, (k % 4) * P:(k % 4 + 1) * P],
                                       m.score[:, b * ROWS:(b + 1) * ROWS, h], m.ident[:])
                ins.then_inc(s.in_rows, 1)
                for n, back in enumerate((False, True, False, True)):
                    scan_rows_pe(pe, m, s, w, HEADS, n, back)
                pe.wait_ge(s.weights_done, 1)
                for k, (h, b) in enumerate(pairs):
                    ins = pe.transpose(m.bank[2 + k // 4][:, (k % 4) * ROWS:(k % 4 + 1) * ROWS], score[:, h, b, :],
                                       m.ident[0:ROWS, 0:ROWS])
                ins.then_inc(s.in_cols, 1)

            @block.scalar
            def _(act):
                act.wait_ge(s.exp_ask, 1)
                act.activation(score[:], score[:], ACT.Exp).then_inc(s.exp_done, 1)

            @block.vector
            def _(dve):
                link = Chain(dve, s.dve_chain)
                flat = m.score[:].rearrange("p t h -> p (t h)")
                dve.scalar_tensor_tensor(flat, flat, 0.2, flat, ALU.mult, ALU.max).then_inc(s.leaky_done, 1)
                dve.wait_ge(s.in_rows, 1)
                for j in range(4):
                    ins = dve.tensor_copy(score[:, 2 * j:2 * j + 2, :, :].rearrange("r h b e -> r (h b e)"),
                                          m.bank[2 + j][0:ROWS, :])
                link(ins)

                def exp():
                    dve.sem_inc(s.exp_ask, 1)
                    dve.wait_ge(s.exp_done, 1)
                softmax_rows(dve, link, exp, m, s, w, score[:], run[:], spread[:], HEADS, 0)
                link(dve.tensor_scalar(spread[:], spread[:], 1e-10, None, ALU.max))
                link(dve.reciprocal(spread[:], spread[:]))
                dve.tensor_tensor(score[:], score[:], spread[:], ALU.mult).then_inc(s.weights_done, 1)
                dve.wait_ge(s.in_cols, 1)
                for j in range(4):
                    dve.tensor_copy(m.score[:].rearrange("p (b r) h -> p h b r", b=BLOCKS)[:, 2 * j:2 * j + 2, :, :],
                                    m.bank[2 + j][:, 0:4 * ROWS].rearrange("p (h b r) -> p h b r", h=2, b=BLOCKS))


def scalar_softmax(nc, m):
    ctx, s = phase(nc, "scalar_softmax", ["dve_chain", "in_rows", "exp_ask", "exp_done", "weights_done", "in_cols"] + SCAN_SEMS)
    with ctx:
        def sb(name, shape, dt=F32):
            return ctx.enter_context(nc.sbuf_tensor("sq_" + name, shape, dt))
        shape = [ROWS, 1, BLOCKS, P]
        q, k, score, run, spread = (sb(n, shape) for n in ("q", "k", "score", "run", "spread"))
        w = ScanSpace(total=sb("total", [ROWS, BLOCKS, 1]), between=sb("between", [1, TILES + 1]),
                            carry=sb("carry", [ROWS, BLOCKS, 1]))
        with nc.Block() as block:
            @block.tensor
            def _(pe):
                for i, cols in enumerate((m.q_src, m.k_dst)):
                    for b in range(BLOCKS):
                        at = (i * BLOCKS + b) * P
                        ins = pe.transpose(m.bank[2][0:ROWS, at:at + P], cols[:, b * ROWS:(b + 1) * ROWS], m.ident[:])
                ins.then_inc(s.in_rows, 1)
                for n, back in enumerate((True, False, True, False, True)):
                    scan_rows_pe(pe, m, s, w, 1, n, back)
                pe.wait_ge(s.weights_done, 1)
                for b in range(BLOCKS):
                    ins = pe.transpose(m.bank[2][:, b * ROWS:(b + 1) * ROWS], score[:, 0, b, :], m.ident[0:ROWS, 0:ROWS])
                ins.then_inc(s.in_cols, 1)

            @block.scalar
            def _(act):
                act.wait_ge(s.exp_ask, 1)
                act.activation(score[:], score[:], ACT.Exp).then_inc(s.exp_done, 1)

            @block.vector
            def _(dve):
                link = Chain(dve, s.dve_chain)
                dve.wait_ge(s.in_rows, 1)
                dve.tensor_copy(q[:].rearrange("r o b e -> r (o b e)"), m.bank[2][0:ROWS, 0:BLOCKS * P])
                link(dve.tensor_tensor(run[:, 0], m.bank[2][0:ROWS, BLOCKS * P:2 * BLOCKS * P].rearrange("r (b e) -> r b e", b=BLOCKS),
                                       m.last[:], ALU.mult))
                link(dve.tensor_scalar(k[:, 0], m.last[:], -LOW, LOW, ALU.mult, ALU.add))
                link(dve.tensor_tensor(k[:], run[:], k[:], ALU.add))
                scan_rows(dve, link, m, s, w, k[:], spread[:], 1, 0, "back")
                link(dve.tensor_tensor(score[:], q[:], spread[:], ALU.add))
                link(dve.tensor_scalar(score[:], score[:], m.qk_bias[0:ROWS, :], None, ALU.add))
                link(dve.scalar_tensor_tensor(score[:], score[:], 0.2, score[:], ALU.mult, ALU.max))

                def exp():
                    dve.sem_inc(s.exp_ask, 1)
                    dve.wait_ge(s.exp_done, 1)
                softmax_rows(dve, link, exp, m, s, w, score[:], run[:], spread[:], 1, 1)
                link(dve.reciprocal(spread[:], spread[:]))
                dve.tensor_tensor(score[:], score[:], spread[:], ALU.mult).then_inc(s.weights_done, 1)
                dve.wait_ge(s.in_cols, 1)
                dve.tensor_copy(m.attn2[:], m.bank[2][:, 0:TILES])


def select(dve, m, s, key, same, cont, k, weight=None):
    dve.wait_ge(s.key_in[k.slot], 16 * (k.turn + 1))
    wait(dve, s.agg_done, k.t - (UNROLL - 1))
    dve.tensor_scalar(cont[:, k.slot, :], key[:, k.slot, 1:P + 1], key[:, k.slot, 0:1], None, ALU.is_equal)
    if weight is None:
        ins = dve.tensor_scalar(same[:, k.slot, :], key[:, k.slot, 1:P + 1], col(m.dst, k.t), None, ALU.is_equal)
    else:
        ins = dve.tensor_scalar(same[:, k.slot, :], key[:, k.slot, 1:P + 1], col(m.dst, k.t), col(weight, k.t),
                                ALU.is_equal, ALU.mult)
    ins.then_inc(s.sel_done, 1)


def carry_over(dve, s, aggT, cont, p_agg, k, chunks, user_done):
    dve.wait_ge(s.agg_done, k.t + 1)
    wait(dve, user_done, k.t - 1)
    dve.wait_ge(s.sel_done, k.t + 1)
    wait(dve, s.carry_done, k.t)
    for c in range(chunks):
        ins = dve.scalar_tensor_tensor(aggT[:, k.pair, c, :], cont[:, k.slot, :], aggT[:, 1 - k.pair, c, P - 1:P],
                                       p_agg[k.pair][:, c * P:(c + 1) * P], ALU.mult, ALU.add)
    ins.then_inc(s.carry_done, 1)


def norm_rows(dve, m, s, y, mv, root, rstd, rows, k, free, scale=None):
    dve.wait_ge(s.root_done, k.t + 1)
    dve.reciprocal(rstd[:, k.pair, :], root[:, k.pair, :]).then_inc(s.recip_done, 1)
    dve.wait_ge(s.recip_done, k.t + 1)
    if scale is not None:
        dve.tensor_tensor(rstd[:, k.pair, :], rstd[:, k.pair, :], col(scale, k.t), ALU.mult).then_inc(s.scale_done, 1)
        dve.wait_ge(s.scale_done, k.t + 1)
    wait(dve, free[k.slot], 16 * k.turn)
    return dve.tensor_scalar(rows[:, k.slot, :], y[:, k.pair, :], mv[:, k.pair, 0:1], rstd[:, k.pair, :],
                             ALU.subtract, ALU.mult)


NORM_SEMS = ["y_done", "bn_done", "mv_done", "root_done", "recip_done", "scale_done", "rows_done"]


def norm_tiles(sb):
    return (sb("y", [P, 2, FEAT]), sb("ystats", [P, 2, 6]), sb("mv", [P, 2, 2]), sb("root", [P, 2, 1]),
            sb("rstd", [P, 2, 1]), sb("rows", [P, UNROLL, FEAT]))


def gat_sum(nc, d, m):
    names = ["sel_done", "weigh_done", "agg_done", "carry_done", "back_done", "res_done", "zero_done", "k_done"] + NORM_SEMS
    ctx, s = phase(nc, "gat_sum", names, ["key_in", "h_in", "own_in", "state_out"])
    with ctx:
        def sb(name, shape, dt=F32):
            return ctx.enter_context(nc.sbuf_tensor("gc_" + name, shape, dt))
        key, same, cont = sb("key", [P, UNROLL, P + 1]), sb("same", [P, UNROLL, P]), sb("cont", [P, UNROLL, P])
        h, own, res, msg = (sb("h", [P, UNROLL, FEAT]), sb("own", [P, UNROLL, FEAT]), sb("res", [P, UNROLL, FEAT]),
                            sb("msg", [P, 2, FEAT]))
        aggT, junk = sb("aggT", [P, 2, FC, P]), sb("junk", [P, 2, FEAT])
        y, stats, mv, root, rstd, rows = norm_tiles(sb)
        p_agg, p_out = m.bank[0:2], m.bank[2:4]

        with nc.Block() as block:
            @block.sync
            def _(sp):
                def step(g, u):
                    if k := tile_at(g, u, 0):
                        load_key(sp, m, s, key, k)
                        hold(sp, s.weigh_done, k.t - (UNROLL - 1))
                        sp.dma_start(h[:, k.slot, :], tile_rows(m.h_src, k.t)).then_inc(s.h_in[k.slot], 16)
                        hold(sp, s.res_done, k.t - (UNROLL - 1))
                        sp.dma_start(own[:, k.slot, :], tile_rows(m.state[1], k.t)).then_inc(s.own_in[k.slot], 16)
                    if k := tile_at(g, u, 4):
                        hold(sp, s.rows_done, k.t + 1)
                        sp.dma_start(tile_rows(m.state[2], k.t), rows[:, k.slot, :]).then_inc(s.state_out[k.slot], 16)
                run_steps(sp, step, 4)
                for slot in range(UNROLL):
                    sp.wait_ge(s.state_out[slot], 16 * (TILES // UNROLL))

            @block.gpsimd
            def _(pool):
                def step(g, u):
                    if k := tile_at(g, u, 1):
                        hold(pool, s.own_in[k.slot], 16 * (k.turn + 1))
                        hold(pool, s.y_done, k.t - (UNROLL - 1))
                        pool.tensor_tensor(res[:, k.slot, :], own[:, k.slot, :], m.bias[:], ALU.add).then_inc(s.res_done, 1)
                run_steps(pool, step, 1)

            @block.scalar
            def _(act):
                def step(g, u):
                    if k := tile_at(g, u, 3):
                        norm_root(act, m, s, mv, root, k)
                run_steps(act, step, 3)

            @block.tensor
            def _(pe):
                def step(g, u):
                    if k := tile_at(g, u, 2):
                        pe.wait_ge(s.weigh_done, k.t + 1)
                        pe.wait_ge(s.sel_done, k.t + 1)
                        wait(pe, s.carry_done, k.t - 1)
                        for c in range(FC):
                            ins = pe.matmul(p_agg[k.pair][:, c * P:(c + 1) * P], msg[:, k.pair, c * P:(c + 1) * P],
                                            same[:, k.slot, :], start=True, stop=True)
                        ins.then_inc(s.agg_done, 1)
                    if k := tile_at(g, u, 3):
                        pe.wait_ge(s.carry_done, k.t + 1)
                        wait(pe, s.y_done, k.t - 1)
                        for c in range(FC):
                            ins = pe.transpose(p_out[k.pair][:, c * P:(c + 1) * P], aggT[:, k.pair, c, :], m.ident[:])
                        ins.then_inc(s.back_done, 1)
                run_steps(pe, step, 3)

            @block.vector
            def _(dve):
                dve.memset(aggT[:, 1, :, P - 1], 0.0).then_inc(s.zero_done, 1)
                dve.wait_ge(s.zero_done, 1)

                def step(g, u):
                    if k := tile_at(g, u, 1):
                        select(dve, m, s, key, same, cont, k)
                        dve.wait_ge(s.h_in[k.slot], 16 * (k.turn + 1))
                        wait(dve, s.agg_done, k.t - 1)
                        attn = m.score[:, k.t, :] if isinstance(k.t, int) else \
                            m.score[:, bass.ds(k.t, 1), :].rearrange("p o h -> p (o h)")
                        dve.tensor_tensor(msg[:, k.pair, :].rearrange("p (h d) -> p h d", h=HEADS),
                                          h[:, k.slot, :].rearrange("p (h d) -> p h d", h=HEADS),
                                          attn.unsqueeze(2).to_broadcast([P, HEADS, HEAD_DIM]), ALU.mult)\
                           .then_inc(s.weigh_done, 1)
                    if k := tile_at(g, u, 2):
                        carry_over(dve, s, aggT, cont, p_agg, k, FC, s.back_done)
                    if k := tile_at(g, u, 3):
                        dve.wait_ge(s.back_done, k.t + 1)
                        dve.wait_ge(s.res_done, k.t + 1)
                        wait(dve, s.rows_done, k.t - 1)
                        dve.tensor_tensor(y[:, k.pair, :], p_out[k.pair][:, 0:FEAT], res[:, k.slot, :], ALU.add)\
                           .then_inc(s.y_done, 1)
                        norm_stats(dve, s, y, stats, mv, k, s.y_done)
                    if k := tile_at(g, u, 4):
                        norm_rows(dve, m, s, y, mv, root, rstd, rows, k, s.state_out).then_inc(s.rows_done, 1)
                        wait(dve, s.k_done, k.t - 1)
                        dve.wait_ge(s.rows_done, k.t + 1)
                        dve.scalar_tensor_tensor(junk[:, k.pair, :], rows[:, k.slot, :], 1.0, m.k_row[:], ALU.mult, ALU.mult,
                                                 accum_out=col(m.k_dst, k.t)).then_inc(s.k_done, 1)
                run_steps(dve, step, 4)


def load_sources(sp, m, s, xs, free, k):
    hold(sp, free, k.t - (UNROLL - 1))
    sp.dma_start(xs[:, k.slot, :], tile_rows(m.x_src, k.t)).then_inc(s.x_in[k.slot], 16)


def overlay(pool, m, s, xs, idx, table, k):
    hold(pool, s.src_in[k.slot], 16 * k.turn)
    pool.tensor_copy(idx[:, k.slot:k.slot + 1], m.idx_l1[:, k.t:k.t + 1, 0] if isinstance(k.t, int) else
                     m.idx_l1[:, bass.ds(k.t, 1), 0]).then_inc(s.idx_staged, 1)
    hold(pool, s.idx_staged, k.t + 1)
    hold(pool, s.x_in[k.slot], 16 * (k.turn + 1))
    gather_pos(pool, m, s, k, xs[:, k.slot, :], table, idx[:, k.slot:k.slot + 1], s.src_in[k.slot])


def scalar_scores(nc, d, m):
    ctx, s = phase(nc, "scalar_scores", ["idx_staged", "scaled", "x2_done", "q_done"], ["x_in", "src_in", "x2_out"])
    with ctx:
        def sb(name, shape, dt=F32):
            return ctx.enter_context(nc.sbuf_tensor("ss_" + name, shape, dt))
        idx, xs = sb("idx", [P, UNROLL], I32), sb("xs", [P, UNROLL, FEAT])
        ax, x2, junk = sb("ax", [P, 2, FEAT]), sb("x2", [P, UNROLL, FEAT]), sb("junk", [P, 2, FEAT])
        alpha, beta, gamma = (m.affine[:, 0, j, :] for j in range(3))
        with nc.Block() as block:
            @block.sync
            def _(sp):
                def step(g, u):
                    if k := tile_at(g, u, 0):
                        load_sources(sp, m, s, xs, s.scaled, k)
                    if k := tile_at(g, u, 3):
                        hold(sp, s.x2_done, k.t + 1)
                        sp.dma_start(tile_rows(m.x2_src, k.t), x2[:, k.slot, :]).then_inc(s.x2_out[k.slot], 16)
                run_steps(sp, step, 3)
                for slot in range(UNROLL):
                    sp.wait_ge(s.x2_out[slot], 16 * (TILES // UNROLL))

            @block.gpsimd
            def _(pool):
                def step(g, u):
                    if k := tile_at(g, u, 0):
                        overlay(pool, m, s, xs, idx, m.state[2], k)
                run_steps(pool, step, 0)

            @block.scalar
            def _(act):
                def step(g, u):
                    if k := tile_at(g, u, 1):
                        act.wait_ge(s.src_in[k.slot], 16 * (k.turn + 1))
                        wait(act, s.x2_done, k.t - 1)
                        act.activation(ax[:, k.pair, :], xs[:, k.slot, :], ACT.Identity, bias=col(gamma, k.t),
                                       scale=col(alpha, k.t)).then_inc(s.scaled, 1)
                run_steps(act, step, 1)

            @block.vector
            def _(dve):
                def step(g, u):
                    if k := tile_at(g, u, 1):
                        wait(dve, s.x2_out[k.slot], 16 * k.turn)
                        dve.wait_ge(s.scaled, k.t + 1)
                        dve.scalar_tensor_tensor(x2[:, k.slot, :], m.bias[:], col(beta, k.t), ax[:, k.pair, :],
                                                 ALU.mult, ALU.add).then_inc(s.x2_done, 1)
                        wait(dve, s.q_done, k.t - 1)
                        dve.wait_ge(s.x2_done, k.t + 1)
                        dve.scalar_tensor_tensor(junk[:, k.pair, :], x2[:, k.slot, :], 1.0, m.q_row[:], ALU.mult, ALU.mult,
                                                 accum_out=col(m.q_src, k.t)).then_inc(s.q_done, 1)
                run_steps(dve, step, 1)


def scalar_sum(nc, d, m):
    names = ["sel_done", "agg_done", "carry_done", "proj_done", "res_done", "zero_done"] + NORM_SEMS
    ctx, s = phase(nc, "scalar_sum", names, ["key_in", "x_in", "own_in", "state_out"])
    with ctx:
        def sb(name, shape, dt=F32):
            return ctx.enter_context(nc.sbuf_tensor("sc_" + name, shape, dt))
        key, same, cont = sb("key", [P, UNROLL, P + 1]), sb("same", [P, UNROLL, P]), sb("cont", [P, UNROLL, P])
        xs, own, res = sb("xs", [P, UNROLL, FEAT]), sb("own", [P, UNROLL, FEAT]), sb("res", [P, UNROLL, FEAT])
        aggT = sb("aggT", [P, 2, FC, P])
        y, stats, mv, root, rstd, rows = norm_tiles(sb)
        p_agg, p_out = m.bank[0:2], m.bank[2:4]

        with nc.Block() as block:
            @block.sync
            def _(sp):
                def step(g, u):
                    if k := tile_at(g, u, 0):
                        load_key(sp, m, s, key, k)
                        hold(sp, s.agg_done, k.t - (UNROLL - 1))
                        sp.dma_start(xs[:, k.slot, :], tile_rows(m.x2_src, k.t)).then_inc(s.x_in[k.slot], 16)
                        hold(sp, s.res_done, k.t - (UNROLL - 1))
                        sp.dma_start(own[:, k.slot, :], tile_rows(m.state[2], k.t)).then_inc(s.own_in[k.slot], 16)
                    if k := tile_at(g, u, 4):
                        hold(sp, s.rows_done, k.t + 1)
                        sp.dma_start(tile_rows(m.state[3], k.t), rows[:, k.slot, :]).then_inc(s.state_out[k.slot], 16)
                run_steps(sp, step, 4)
                for slot in range(UNROLL):
                    sp.wait_ge(s.state_out[slot], 16 * (TILES // UNROLL))

            @block.gpsimd
            def _(pool):
                def step(g, u):
                    if k := tile_at(g, u, 1):
                        hold(pool, s.own_in[k.slot], 16 * (k.turn + 1))
                        hold(pool, s.y_done, k.t - (UNROLL - 1))
                        pool.tensor_tensor(res[:, k.slot, :], own[:, k.slot, :], m.bv[:], ALU.add).then_inc(s.res_done, 1)
                run_steps(pool, step, 1)

            @block.scalar
            def _(act):
                def step(g, u):
                    if k := tile_at(g, u, 3):
                        norm_root(act, m, s, mv, root, k)
                run_steps(act, step, 3)

            @block.tensor
            def _(pe):
                def step(g, u):
                    if k := tile_at(g, u, 2):
                        pe.wait_ge(s.x_in[k.slot], 16 * (k.turn + 1))
                        pe.wait_ge(s.sel_done, k.t + 1)
                        wait(pe, s.carry_done, k.t - 1)
                        for c in range(FC):
                            ins = pe.matmul(p_agg[k.pair][:, c * P:(c + 1) * P], xs[:, k.slot, c * P:(c + 1) * P],
                                            same[:, k.slot, :], start=True, stop=True)
                        ins.then_inc(s.agg_done, 1)
                    if k := tile_at(g, u, 3):
                        pe.wait_ge(s.carry_done, k.t + 1)
                        wait(pe, s.y_done, k.t - 1)
                        for c in range(FC):
                            ins = pe.matmul(p_out[k.pair][:, 0:FEAT], aggT[:, k.pair, c, :], m.wv[:, c, :],
                                            start=c == 0, stop=c == FC - 1)
                        ins.then_inc(s.proj_done, 1)
                run_steps(pe, step, 3)

            @block.vector
            def _(dve):
                dve.memset(aggT[:, 1, :, P - 1], 0.0).then_inc(s.zero_done, 1)
                dve.wait_ge(s.zero_done, 1)

                def step(g, u):
                    if k := tile_at(g, u, 1):
                        select(dve, m, s, key, same, cont, k, m.attn2)
                    if k := tile_at(g, u, 2):
                        carry_over(dve, s, aggT, cont, p_agg, k, FC, s.proj_done)
                    if k := tile_at(g, u, 3):
                        dve.wait_ge(s.proj_done, k.t + 1)
                        dve.wait_ge(s.res_done, k.t + 1)
                        wait(dve, s.rows_done, k.t - 1)
                        dve.tensor_tensor(y[:, k.pair, :], p_out[k.pair][:, 0:FEAT], res[:, k.slot, :], ALU.add)\
                           .then_inc(s.y_done, 1)
                        norm_stats(dve, s, y, stats, mv, k, s.y_done)
                    if k := tile_at(g, u, 4):
                        norm_rows(dve, m, s, y, mv, root, rstd, rows, k, s.state_out, m.dinv).then_inc(s.rows_done, 1)
                run_steps(dve, step, 4)


def gcn(nc, d, m, out):
    names = ["idx_staged", "scaled", "x3_done", "sel_done", "agg_done", "carry_done", "total_done", "proj_done", "un_done", "res_done",
             "zero_done", "out_staged"] + NORM_SEMS
    ctx, s = phase(nc, "gcn", names, ["key_in", "x_in", "src_in", "own_in", "out_done"])
    with ctx:
        def sb(name, shape, dt=F32):
            return ctx.enter_context(nc.sbuf_tensor("gn_" + name, shape, dt))
        idx, out_idx = sb("idx", [P, UNROLL], I32), sb("out_idx", [P, UNROLL], I32)
        key, same, cont = sb("key", [P, UNROLL, P + 1]), sb("same", [P, UNROLL, P]), sb("cont", [P, UNROLL, P])
        xs, own, res = sb("xs", [P, UNROLL, FEAT]), sb("own", [P, UNROLL, FEAT]), sb("res", [P, UNROLL, FEAT])
        ax, x3, un = sb("ax", [P, 2, FEAT]), sb("x3", [P, UNROLL, FEAT]), sb("un", [P, UNROLL, FEAT])
        aggT, totT = sb("aggT", [P, 2, FC, P]), sb("totT", [P, 2, FC, P])
        y, stats, mv, root, rstd, rows = norm_tiles(sb)
        p_agg, p_out = m.bank[0:2], m.bank[2:4]
        alpha, beta, gamma = (m.affine[:, 1, j, :] for j in range(3))

        with nc.Block() as block:
            @block.sync
            def _(sp):
                def step(g, u):
                    if k := tile_at(g, u, 0):
                        load_key(sp, m, s, key, k)
                        load_sources(sp, m, s, xs, s.scaled, k)
                        hold(sp, s.un_done, k.t - (UNROLL - 1))
                        hold(sp, s.agg_done, k.t - (UNROLL - 1))
                        sp.dma_start(own[:, k.slot, :], tile_rows(m.state[3], k.t)).then_inc(s.own_in[k.slot], 16)
                run_steps(sp, step, 0)

            @block.gpsimd
            def _(pool):
                def step(g, u):
                    if k := tile_at(g, u, 0):
                        overlay(pool, m, s, xs, idx, m.state[3], k)
                    if k := tile_at(g, u, 1):
                        hold(pool, s.y_done, k.t - (UNROLL - 1))
                        hold(pool, s.un_done, k.t + 1)
                        pool.tensor_tensor(res[:, k.slot, :], un[:, k.slot, :], m.res_bias[:], ALU.add).then_inc(s.res_done, 1)
                    if k := tile_at(g, u, 4):
                        hold(pool, s.out_done[k.slot], 16 * k.turn)
                        pool.tensor_copy(out_idx[:, k.slot:k.slot + 1], col(m.map_idx, k.t)).then_inc(s.out_staged, 1)
                        hold(pool, s.out_staged, k.t + 1)
                        hold(pool, s.rows_done, k.t + 1)
                        pool.indirect_dma_start(out, bass.IndirectOffsetOnAxis(ap=out_idx[:, k.slot:k.slot + 1], axis=0),
                                                rows[:, k.slot, :], None, bounds_check=NODES - 1, oob_is_err=False)\
                            .then_inc(s.out_done[k.slot], 16)
                run_steps(pool, step, 4)
                for slot in range(UNROLL):
                    pool.wait_ge(s.out_done[slot], 16 * (TILES // UNROLL))

            @block.scalar
            def _(act):
                def step(g, u):
                    if k := tile_at(g, u, 1):
                        act.wait_ge(s.own_in[k.slot], 16 * (k.turn + 1))
                        wait(act, s.res_done, k.t - (UNROLL - 1))
                        act.activation(un[:, k.slot, :], own[:, k.slot, :], ACT.Copy, scale=col(m.sdeg, k.t)).then_inc(s.un_done, 1)
                        act.wait_ge(s.src_in[k.slot], 16 * (k.turn + 1))
                        wait(act, s.x3_done, k.t - 1)
                        act.activation(ax[:, k.pair, :], xs[:, k.slot, :], ACT.Identity, bias=col(gamma, k.t),
                                       scale=col(alpha, k.t)).then_inc(s.scaled, 1)
                    if k := tile_at(g, u, 3):
                        norm_root(act, m, s, mv, root, k)
                run_steps(act, step, 3)

            @block.tensor
            def _(pe):
                def step(g, u):
                    if k := tile_at(g, u, 2):
                        pe.wait_ge(s.own_in[k.slot], 16 * (k.turn + 1))
                        wait(pe, s.total_done, k.t - 1)
                        for c in range(FC):
                            pe.transpose(p_agg[k.pair][:, FEAT + c * P:FEAT + (c + 1) * P],
                                         own[:, k.slot, c * P:(c + 1) * P], m.ident[:])
                        pe.wait_ge(s.x3_done, k.t + 1)
                        pe.wait_ge(s.sel_done, k.t + 1)
                        for c in range(FC):
                            ins = pe.matmul(p_agg[k.pair][:, c * P:(c + 1) * P], x3[:, k.slot, c * P:(c + 1) * P],
                                            same[:, k.slot, :], start=True, stop=True)
                        ins.then_inc(s.agg_done, 1)
                    if k := tile_at(g, u, 3):
                        pe.wait_ge(s.total_done, k.t + 1)
                        wait(pe, s.y_done, k.t - 1)
                        for c in range(FC):
                            ins = pe.matmul(p_out[k.pair][:, 0:FEAT], totT[:, k.pair, c, :], m.w_gcn[:, c, :],
                                            start=c == 0, stop=c == FC - 1)
                        ins.then_inc(s.proj_done, 1)
                run_steps(pe, step, 3)

            @block.vector
            def _(dve):
                dve.memset(aggT[:, 1, :, P - 1], 0.0).then_inc(s.zero_done, 1)
                dve.wait_ge(s.zero_done, 1)

                def step(g, u):
                    if k := tile_at(g, u, 1):
                        select(dve, m, s, key, same, cont, k)
                        dve.wait_ge(s.scaled, k.t + 1)
                        dve.scalar_tensor_tensor(x3[:, k.slot, :], m.bias[:], col(beta, k.t), ax[:, k.pair, :],
                                                 ALU.mult, ALU.add).then_inc(s.x3_done, 1)
                    if k := tile_at(g, u, 2):
                        carry_over(dve, s, aggT, cont, p_agg, k, FC, s.proj_done)
                        dve.wait_ge(s.carry_done, k.t + 1)
                        dve.tensor_tensor(totT[:, k.pair, :, :], aggT[:, k.pair, :, :],
                                          p_agg[k.pair][:, FEAT:2 * FEAT].rearrange("p (c n) -> p c n", c=FC), ALU.add)\
                           .then_inc(s.total_done, 1)
                    if k := tile_at(g, u, 3):
                        dve.wait_ge(s.proj_done, k.t + 1)
                        dve.wait_ge(s.res_done, k.t + 1)
                        wait(dve, s.rows_done, k.t - 1)
                        dve.scalar_tensor_tensor(y[:, k.pair, :], p_out[k.pair][:, 0:FEAT], col(m.dinv, k.t),
                                                 res[:, k.slot, :], ALU.mult, ALU.add).then_inc(s.y_done, 1)
                        norm_stats(dve, s, y, stats, mv, k, s.y_done)
                    if k := tile_at(g, u, 4):
                        norm_rows(dve, m, s, y, mv, root, rstd, rows, k, s.out_done).then_inc(s.rows_done, 1)
                run_steps(dve, step, 4)


_OUTS = [((NODES, FEAT), "float32")]


def kernel(x, src, dst, edge_attr_3, L0_gnn_W1, L0_gnn_b1, L0_gnn_W2, L0_gnn_b2, L1_gnn_W, L1_gnn_a_src,
           L1_gnn_a_dst, L1_gnn_edge_W, L1_gnn_edge_b, L1_gnn_bias, L2_gnn_Wv, L2_gnn_bv, L2_gnn_wq, L2_gnn_bq,
           L2_gnn_wk, L2_gnn_bk, L3_gnn_W_conv, L3_gnn_b_conv, L3_gnn_W_lin, L3_gnn_b_lin):
    import numpy as np
    import concourse.bacc as bacc
    from concourse.bass_utils import run_bass_kernel_spmd

    c = np.ascontiguousarray
    x, src, dst, edge_attr_3 = (np.asarray(a) for a in (x, src, dst, edge_attr_3))
    pad = EPAD - EDGES
    heads = np.arange(FEAT)[:, None] // HEAD_DIM == np.arange(HEADS)[None, :]
    arrays = {
        "x": c(x),
        "dst_pad": np.concatenate([np.full(1, -1, np.int32), dst, np.full(pad, NODES, np.int32),
                                   np.full(1, NODES + 1, np.int32)]),
        "src_pad": np.concatenate([src, np.zeros(pad, np.int32)]),
        "edge_attr_T": c(np.concatenate([edge_attr_3, np.zeros((pad, EDGE_FEAT), np.float32)]).T),
        "head_mask": heads.astype(np.float32),
        "L0_W1": c(L0_gnn_W1), "L0_b1": c(L0_gnn_b1), "L0_W2": c(L0_gnn_W2), "L0_b2": c(L0_gnn_b2),
        "L1_W": c(L1_gnn_W), "L1_WT": c(np.asarray(L1_gnn_W).T), "L1_a_src": c(L1_gnn_a_src).reshape(FEAT, 1),
        "L1_a_dst": c(L1_gnn_a_dst).reshape(FEAT, 1), "L1_eWT": c(np.asarray(L1_gnn_edge_W).T),
        "L1_eb": c(L1_gnn_edge_b), "L1_bias": c(L1_gnn_bias),
        "L2_Wv": c(L2_gnn_Wv), "L2_WvT": c(np.asarray(L2_gnn_Wv).T), "L2_bv": c(L2_gnn_bv),
        "L2_wq": c(L2_gnn_wq).reshape(FEAT, 1), "L2_wk": c(L2_gnn_wk).reshape(FEAT, 1),
        "L2_bq": c(L2_gnn_bq).reshape(1), "L2_bk": c(L2_gnn_bk).reshape(1),
        "L3_WcT": c(np.asarray(L3_gnn_W_conv).T), "L3_bc": c(L3_gnn_b_conv).reshape(GCN_HIDDEN, 1),
        "L3_Wl": c(L3_gnn_W_lin), "L3_bl": c(L3_gnn_b_lin),
    }
    arrays = {n: np.asarray(a) for n, a in arrays.items()}
    nc = bacc.Bacc("TRN2", target_bir_lowering=False, num_devices=1)
    d = namedtuple("Inputs", list(arrays))(*(nc.dram_tensor(n, a.shape, mybir.dt.from_np(a.dtype), kind="ExternalInput").ap()
                                             for n, a in arrays.items()))
    (shape, dtype), = _OUTS
    out = nc.dram_tensor("out", shape, mybir.dt.from_np(np.dtype(dtype)), kind="ExternalOutput").ap()
    build(nc, d, out)
    r = run_bass_kernel_spmd(nc, [arrays], core_ids=[0])
    return r.results[0]["out"]
```

```python
from collections import namedtuple
from contextlib import ExitStack

import concourse.bass as bass
from concourse import mybir

F32 = mybir.dt.float32
F32R = mybir.dt.float32r
BF16 = mybir.dt.bfloat16
I32 = mybir.dt.int32
ALU = mybir.AluOpType
ACT = mybir.ActivationFunctionType
AX = mybir.AxisListType

P = 128
NODES = 50000
EDGES = 25000
FEAT = 256
HIDDEN = 512
HEADS = 8
HEAD_DIM = FEAT // HEADS
EDGE_FEAT = 3
GCN_HIDDEN = 128
FC = FEAT // P
HC = HIDDEN // P
RING = 7
UNROLL = 2 * RING
TILES = -(-EDGES // (P * UNROLL)) * UNROLL
EPAD = TILES * P
BLOCKS = 2
ROWS = TILES // BLOCKS
MAP_COLS = -(-NODES // P)
PLAIN_COLS = NODES // P
TAIL = NODES - PLAIN_COLS * P
BATCH = 15
PIECE = 5
LOOKUPS = 5
Y_BANKS = 5
AFFINE_LINKS = (8, 4, 1)
NOWHERE = 1 << 20
LOW = -1.0e30
EPS = 1e-5

Tile = namedtuple("Tile", "t slot pair turn body_slot body")
ScanSpace = namedtuple("ScanSpace", "total between carry")


class Memory:
    pass



def tile_at(g, u, lag, unroll=UNROLL, tiles=TILES):
    v = u - lag
    t = g * unroll + v
    if isinstance(g, int) and not 0 <= t < tiles:
        return None
    return Tile(t, v % unroll % RING, v % unroll % 2, g * (unroll // RING) + v // RING, v % unroll, g + v // unroll)


def run_steps(eng, step, lag, unroll=UNROLL, tiles=TILES, peeled=None):
    bodies = tiles // unroll
    peeled = min(bodies, peeled or 1 + -(-lag // unroll))
    for j in range(peeled * unroll):
        step(j // unroll, j % unroll)
    if bodies > peeled:
        with eng.Fori(peeled, bodies) as g:
            for u in range(unroll):
                step(g, u)
    for u in range(lag):
        step(bodies + u // unroll, u % unroll)


def wait(eng, sem, value):
    if not (isinstance(value, int) and value <= 0):
        eng.wait_ge(sem, value)


def hold(eng, sem, value):
    if not (isinstance(value, int) and value <= 0):
        eng.wait_ge(sem, value)
        eng.nop(nofuse=True)


def col(ap, t, n=1):
    return ap[:, t:t + n] if isinstance(t, int) else ap[:, bass.ds(t, n)]


def tile_rows(ap, t):
    return ap[t * P:(t + 1) * P, :] if isinstance(t, int) else ap[bass.ds(t * P, P), :]


class Chain:

    def __init__(self, eng, sem, base=0):
        self.eng, self.sem, self.base, self.n = eng, sem, base, 0

    def __call__(self, ins):
        self.n += 1
        ins.then_inc(self.sem, 1)
        self.eng.wait_ge(self.sem, self.base + self.n)


def phase(nc, label, names, rings=(), more=()):
    taken = []

    def take(name):
        taken.append(nc.alloc_semaphore(f"{label}_{name}"))
        return taken[-1]

    def clear():
        nc.clear_and_free_semaphores(taken)
        nc.all_engine_barrier()
    ctx = ExitStack()
    ctx.callback(clear)
    sized = [(n, RING) for n in rings] + list(more)
    found = [take(n) for n in names] + [[take(f"{n}{i}") for i in range(size)] for n, size in sized]
    return ctx, namedtuple("Semaphores", list(names) + [n for n, _ in sized])(*found)


def build(nc, d, out):
    ctx = ExitStack()
    with ctx:
        def sb(name, shape, dt=F32):
            return ctx.enter_context(nc.sbuf_tensor(name, shape, dt))

        def dram(name, shape, dt=F32):
            return nc.dram_tensor(name, shape, dt).ap()

        bank = [ctx.enter_context(nc.psum_tensor(f"bank{i}", [P, 512], F32)) for i in range(8)]
        m = Memory()
        m.bank = bank
        m.dst_f = dram("dst_f", [EPAD + 2])
        m.node_map = dram("node_map", [MAP_COLS * P, 1], I32)
        m.x_src = dram("x_src", [EPAD, FEAT])
        m.h_src = dram("h_src", [EPAD, FEAT])
        m.x2_src = dram("x2_src", [EPAD, FEAT])
        m.state = [None] + [dram(f"state{i}", [EPAD, FEAT]) for i in (1, 2, 3)]
        m.res3 = dram("res3", [EPAD, FEAT])
        m.ident = sb("ident", [P, P])
        m.eps = sb("eps", [P, 1])
        m.dst = sb("dst_col", [P, TILES])
        m.idx_l0 = sb("idx_l0", [P, TILES, 2], I32)
        m.idx_l1 = sb("idx_l1", [P, TILES, 2], I32)
        m.map_idx = sb("map_idx", [P, TILES], I32)
        m.edge_id = sb("edge_id", [P, TILES], I32)
        m.indeg = sb("indeg", [P, TILES])
        m.rdeg = sb("rdeg", [P, TILES])
        m.sdeg = sb("sdeg", [P, TILES])
        m.dinv = sb("dinv", [P, TILES])
        m.keep = sb("keep", [ROWS, BLOCKS, P])
        m.pen_f = sb("pen_f", [ROWS, BLOCKS, P])
        m.pen_b = sb("pen_b", [ROWS, BLOCKS, P])
        m.last = sb("last_row", [ROWS, BLOCKS, P])
        m.open_row = sb("open_row", [HEADS, 3, TILES])
        m.row_stat = sb("row_stat", [P, 3, TILES])
        m.touched = sb("touched", [P, TILES])
        m.untouched = sb("untouched", [P, TILES])
        m.affine = sb("affine", [P, 2, 3, TILES])
        m.score = sb("score", [P, TILES, HEADS])
        m.q_src = sb("q_src", [P, TILES])
        m.k_dst = sb("k_dst", [P, TILES])
        m.attn2 = sb("attn2", [P, TILES])
        weights(nc, d, m, sb)
        structure(nc, d, m, ctx)
        edge_mlp(nc, d, m)
        untouched_nodes(nc, d, m, out, P, 0, PLAIN_COLS, 2 * BATCH, BATCH, PIECE)
        untouched_nodes(nc, d, m, out, TAIL, P * PLAIN_COLS, 1, 1, 1, 1)
        gat_scores(nc, d, m)
        gat_softmax(nc, m)
        gat_sum(nc, d, m)
        scalar_scores(nc, d, m)
        scalar_softmax(nc, m)
        scalar_sum(nc, d, m)
        gcn(nc, d, m, out)


def weights(nc, d, m, sb):
    m.w1, m.w2 = sb("w1", [P, 2, 2 * FC, HIDDEN], F32R), sb("w2", [P, 2, HC, FEAT], F32R)
    m.b1_parts, m.ones3 = sb("b1_parts", [3, HIDDEN], BF16), sb("ones3", [3, P], BF16)
    m.res_parts, m.bias_parts, m.bv_parts = (sb(n, [3, FEAT], BF16) for n in ("res_parts", "bias_parts", "bv_parts"))
    m.w_src = sb("w_src", [P, FC, FEAT + HEADS])
    m.w_dst = sb("w_dst", [P, FC, HEADS])
    m.w_enc = sb("w_enc", [EDGE_FEAT + 1, FEAT])
    m.wv = sb("wv", [P, FC, FEAT])
    m.w_gcn = sb("w_gcn", [P, FC, FEAT])
    m.w_res = sb("w_res", [P, FC, FEAT])
    rows = ("b2", "bias", "bv", "bl", "q_row", "k_row")
    m.b2, m.bias, m.bv, m.res_bias, m.q_row, m.k_row = (sb(n + "_all", [P, FEAT]) for n in rows)
    m.bias_mv, m.bias_var_eps, m.qk_bias = sb("bias_mv", [P, 2]), sb("bias_var_eps", [P, 1]), sb("qk_bias", [P, 1])
    names = ["ident_done", "load_done", "dve_chain", "parts_done", "parts_in", "masked", "prod_done", "prod_taken",
             "const_done"]
    ctx, s = phase(nc, "weights", names)
    with (ctx, nc.Block() as block):
        def tmp(name, shape, dt=F32):
            return ctx.enter_context(nc.sbuf_tensor("tmp_" + name, shape, dt))
        b1_row, b1_split, rest = tmp("b1_row", [1, HIDDEN]), tmp("b1_split", [1, 3, HIDDEN], BF16), tmp("rest", [1, HIDDEN])
        res_split, bias_split, bv_split = (tmp(n, [1, 3, FEAT], BF16) for n in ("res_split", "bias_split", "bv_split"))
        w1, w2 = tmp("w1", [P, 2 * FC, HIDDEN]), tmp("w2", [P, HC, FEAT])
        w_nat, mask, a_col = tmp("w_nat", [P, FC, FEAT]), tmp("mask", [P, FC, HEADS]), tmp("a_col", [P, 2, FC])
        masked = tmp("masked", [P, 2, FC, HEADS])
        wvT, qk_col, qk_all = tmp("wvT", [P, FC, FEAT]), tmp("qk_col", [P, 2, FC]), tmp("qk_all", [P, 2, FC, P])
        bv_col, bv_all, qk_sum, qk_b = tmp("bv_col", [P, FC]), tmp("bv_all", [P, FC, P]), tmp("qk_sum", [P, FC]), tmp("qk_b", [P, 2])
        wcT, wl, bc_col, bc_all = tmp("wcT", [P, FEAT]), tmp("wl", [P, FEAT]), tmp("bc_col", [P, 1]), tmp("bc_all", [P, P])
        stats = tmp("bias_stats", [P, 6])

        def chunks(ap):
            return ap.rearrange("(c p) n -> p c n", p=P)

        def column(ap):
            return ap.rearrange("(c p) o -> p (c o)", p=P)
        loads = [
            (w1[:], chunks(d.L0_W1)), (w2[:], chunks(d.L0_W2)), (m.b2[:], d.L0_b2.partition_broadcast(P)), (b1_row[:], d.L0_b1.unsqueeze(0)),
            (m.w_src[:, :, 0:FEAT], chunks(d.L1_WT)), (w_nat[:], chunks(d.L1_W)), (mask[:], chunks(d.head_mask)),
            (a_col[:, 0, :], column(d.L1_a_src)), (a_col[:, 1, :], column(d.L1_a_dst)),
            (m.w_enc[0:EDGE_FEAT, :], d.L1_eWT), (m.w_enc[EDGE_FEAT:EDGE_FEAT + 1, :], d.L1_eb.unsqueeze(0)),
            (m.bias[:], d.L1_bias.partition_broadcast(P)),
            (m.wv[:], chunks(d.L2_Wv)), (wvT[:], chunks(d.L2_WvT)), (m.bv[:], d.L2_bv.partition_broadcast(P)),
            (qk_col[:, 0, :], column(d.L2_wq)), (qk_col[:, 1, :], column(d.L2_wk)),
            (bv_col[:], column(d.L2_bv.unsqueeze(1))),
            (qk_b[:, 0:1], d.L2_bq.partition_broadcast(P)), (qk_b[:, 1:2], d.L2_bk.partition_broadcast(P)),
            (wcT[:], d.L3_WcT), (wl[:], d.L3_Wl), (bc_col[:], d.L3_bc), (m.res_bias[:], d.L3_bl.partition_broadcast(P)),
        ]

        @block.sync
        def _(sp):
            with nc.allow_non_contiguous_dma("columns of small vectors"):
                for to, frm in loads:
                    sp.dma_start(to, frm).then_inc(s.load_done, 16)
            sp.wait_ge(s.parts_done, 1)
            sp.dma_start(m.b1_parts[:], b1_split[:].rearrange("o k n -> o (k n)")).then_inc(s.parts_in, 16)
            for to, parts in ((m.res_parts, res_split), (m.bias_parts, bias_split), (m.bv_parts, bv_split)):
                sp.dma_start(to[:], parts[:].rearrange("o k n -> o (k n)")).then_inc(s.parts_in, 16)
            sp.wait_ge(s.parts_in, 64)

        @block.gpsimd
        def _(pool):
            pool.memset(m.ident[:], 0.0).then_inc(s.ident_done, 1)
            pool.wait_ge(s.ident_done, 1)
            pool.affine_select(out=m.ident[:], in_=m.ident[:], compare_op=ALU.not_equal, fill=1.0,
                               base=0, pattern=[[-1, P]], channel_multiplier=1).then_inc(s.ident_done, 1)
            pool.memset(m.eps[:], EPS)
            pool.memset(m.ones3[:], 1.0).then_inc(s.const_done, 1)

        @block.tensor
        def _(pe):
            pe.wait_ge(s.masked, 1)
            for k in range(2):
                for c in range(FC):
                    at = (k * FC + c) * HEADS
                    for o in range(FC):
                        pe.matmul(m.bank[0][:, at:at + HEADS], w_nat[:, o, c * P:(c + 1) * P], masked[:, k, o, :],
                                  start=o == 0, stop=o == FC - 1)
            for k in range(2):
                for o in range(FC):
                    pe.matmul(m.bank[1][:, k * FEAT:(k + 1) * FEAT], qk_all[:, k, o, :], wvT[:, o, :],
                              start=o == 0, stop=o == FC - 1)
            for o in range(FC):
                pe.matmul(m.bank[2][:, 0:1], bv_all[:, o, :], qk_sum[:, o:o + 1], start=o == 0, stop=o == FC - 1)
            for c in range(FC):
                pe.matmul(m.bank[3][:, c * FEAT:(c + 1) * FEAT], wcT[:, c * P:(c + 1) * P], wl[:], start=True, stop=True)
            pe.matmul(m.bank[4][:, 0:FEAT], bc_all[:], wl[:], start=True, stop=True).then_inc(s.prod_done, 1)

        @block.vector
        def _(dve):
            link = Chain(dve, s.dve_chain)

            def split(row, parts, n):
                link(dve.tensor_copy(parts[:, 0, :], row))
                link(dve.tensor_tensor(rest[:, 0:n], row, parts[:, 0, :], ALU.subtract))
                link(dve.tensor_copy(parts[:, 1, :], rest[:, 0:n]))
                link(dve.tensor_tensor(rest[:, 0:n], rest[:, 0:n], parts[:, 1, :], ALU.subtract))
                return dve.tensor_copy(parts[:, 2, :], rest[:, 0:n])

            dve.wait_ge(s.load_done, 16 * len(loads))
            link(dve.tensor_tensor(w1[:, 0:FC, :], w1[:, 0:FC, :], w1[:, FC:2 * FC, :], ALU.subtract))
            dve.tensor_copy(m.w1[:, 0], w1[:])
            link(dve.tensor_copy(m.w2[:, 0], w2[:]))
            dve.tensor_tensor(m.w1[:, 1], w1[:], m.w1[:, 0].bitcast(F32), ALU.subtract)
            dve.tensor_tensor(m.w2[:, 1], w2[:], m.w2[:, 0].bitcast(F32), ALU.subtract)
            for k in range(2):
                for o in range(FC):
                    dve.tensor_scalar(masked[:, k, o, :], mask[:, o, :], a_col[:, k, o:o + 1], None, ALU.mult)
                    dve.tensor_copy(qk_all[:, k, o, :], qk_col[:, k, o:o + 1].to_broadcast([P, P]))
            for o in range(FC):
                dve.tensor_copy(bv_all[:, o, :], bv_col[:, o:o + 1].to_broadcast([P, P]))
            dve.tensor_tensor(qk_sum[:], qk_col[:, 0, :], qk_col[:, 1, :], ALU.add)
            link(dve.tensor_copy(bc_all[:], bc_col[:].to_broadcast([P, P])))
            dve.sem_inc(s.masked, 1)
            link(dve.bn_stats(stats[:], m.bias[:]))
            dve.nop(nofuse=True)
            link(dve.bn_aggr(m.bias_mv[:], stats[:]))
            dve.tensor_scalar(m.bias_var_eps[:], m.bias_mv[:, 1:2], EPS, None, ALU.add)
            link(split(b1_row[:], b1_split, HIDDEN))
            link(split(m.bias[0:1, :], bias_split, FEAT))
            link(split(m.bv[0:1, :], bv_split, FEAT))
            dve.wait_ge(s.prod_done, 1)
            dve.wait_ge(s.ident_done, 2)
            dve.tensor_copy(m.w_src[:, :, FEAT:FEAT + HEADS],
                            m.bank[0][:, 0:FC * HEADS].rearrange("p (c h) -> p c h", c=FC))
            dve.tensor_copy(m.w_dst[:], m.bank[0][:, FC * HEADS:2 * FC * HEADS].rearrange("p (c h) -> p c h", c=FC))
            dve.tensor_copy(m.q_row[:], m.bank[1][:, 0:FEAT])
            dve.tensor_copy(m.k_row[:], m.bank[1][:, FEAT:2 * FEAT])
            dve.tensor_tensor(m.qk_bias[:], qk_b[:, 0:1], qk_b[:, 1:2], ALU.add)
            dve.tensor_copy(m.w_gcn[:], m.bank[3][:].rearrange("p (c n) -> p c n", c=FC))
            link(dve.tensor_tensor(m.res_bias[:], m.bank[4][:, 0:FEAT], m.res_bias[:], ALU.add))
            dve.tensor_tensor(m.qk_bias[:], m.bank[2][:, 0:1], m.qk_bias[:], ALU.add)
            link(dve.tensor_copy(m.w_res[:], m.w_gcn[:]))
            for c in range(FC):
                block_c = m.w_res[:, c, c * P:(c + 1) * P]
                dve.tensor_tensor(block_c, block_c, m.ident[:], ALU.add)
            split(m.res_bias[0:1, :], res_split, FEAT).then_inc(s.parts_done, 1)


def scan_rows(dve, link, m, s, w, vals, out, heads, n, kind):
    back = kind == "back"
    weight, op0, op1, start, which = {
        "max": (m.pen_f, ALU.add, ALU.max, LOW, 0), "sum": (m.keep, ALU.mult, ALU.add, 0.0, 1),
        "back": (m.pen_b, ALU.add, ALU.max, LOW, 2)}[kind]
    turn = slice(None, None, -1) if back else slice(None)

    def scans(initial):
        for h in range(heads):
            for b in range(BLOCKS):
                first = start if initial is None else initial[:, b, h:h + 1]
                ins = dve.tensor_tensor_scan(out[:, h, b, turn], weight[:, b, turn], vals[:, h, b, turn],
                                             first, op0, op1)
        return ins

    link(scans(None))
    dve.tensor_copy(w.total[:, :, 0:heads].rearrange("r b h -> r h b"),
                    out[:, :, :, 0 if back else P - 1]).then_inc(s.totals_ready, 1)
    link(dve.memset(w.between[0:heads, TILES if back else 0:TILES + 1 if back else 1], start))
    dve.wait_ge(s.totals_in_row, n + 1)
    tot = m.bank[0][0:heads, 0:TILES]
    opens = m.open_row[0:heads, which, :]
    if back:
        dve.tensor_tensor_scan(w.between[0:heads, 0:TILES][:, ::-1], opens[:, ::-1], tot[:, ::-1], start,
                               op0, op1).then_inc(s.between_ready, 1)
    else:
        dve.tensor_tensor_scan(w.between[0:heads, 1:TILES + 1], opens, tot, start,
                               op0, op1).then_inc(s.between_ready, 1)
    dve.wait_ge(s.carry_ready, n + 1)
    link(dve.tensor_copy(w.carry[:, :, 0:heads],
                         m.bank[1][0:ROWS, 0:BLOCKS * heads].rearrange("r (b h) -> r b h", b=BLOCKS)))
    link(scans(w.carry))


def scan_rows_pe(pe, m, s, w, heads, n, back):
    pe.wait_ge(s.totals_ready, n + 1)
    for b in range(BLOCKS):
        ins = pe.transpose(m.bank[0][0:heads, b * ROWS:(b + 1) * ROWS], w.total[:, b, 0:heads],
                           m.ident[0:ROWS, 0:ROWS])
    ins.then_inc(s.totals_in_row, 1)
    pe.wait_ge(s.between_ready, n + 1)
    for b in range(BLOCKS):
        at = b * ROWS + (1 if back else 0)
        ins = pe.transpose(m.bank[1][0:ROWS, b * heads:(b + 1) * heads], w.between[0:heads, at:at + ROWS],
                           m.ident[0:heads, 0:heads])
    ins.then_inc(s.carry_ready, 1)


SCAN_SEMS = ["totals_ready", "totals_in_row", "between_ready", "carry_ready"]


def structure(nc, d, m, outer):
    names = ["rows_in", "ids_ready", "dve_chain", "rows_out", "flags_ready", "opens_ready", "cols_ready",
             "cols_done", "map_ready", "map_in", "act_done", "deg_ready", "flat_in"] + SCAN_SEMS
    ctx, s = phase(nc, "structure", names)
    R = [ROWS, BLOCKS, P]
    with ctx:
        def sb(name, shape, dt=F32):
            return ctx.enter_context(nc.sbuf_tensor(name, shape, dt))
        dst_i, prev_i, next_i, src_i, id_i = (sb(n, R, I32) for n in ("dst_i", "prev_i", "next_i", "src_i", "id_i"))
        dst, prev, nxt, src, eid, first = (sb(n, R) for n in ("dst_r", "prev_r", "next_r", "src_r", "id_r", "first_r"))
        count, end = sb("count_r", [ROWS, 1, BLOCKS, P]), sb("end_r", [ROWS, 1, BLOCKS, P])
        ones = sb("ones_r", [ROWS, 1, BLOCKS, P])
        map_i = sb("map_r", R)
        opens = sb("opens_r", [ROWS, BLOCKS, 3, HEADS])
        flag = sb("flag_r", [ROWS, BLOCKS, 2])
        nowhere = sb("nowhere", [P, MAP_COLS], I32)
        gathered = sb("dst_gather", [P, TILES])
        w = ScanSpace(total=sb("total_s", [ROWS, BLOCKS, HEADS]), between=sb("between_s", [HEADS, TILES + 1]),
                            carry=sb("carry_s", [ROWS, BLOCKS, HEADS]))
        flat = [(dst_i, d.dst_pad, 1), (prev_i, d.dst_pad, 0), (next_i, d.dst_pad, 2), (src_i, d.src_pad, 0)]
        cols = [dst, src, map_i, eid, count[:, 0], end[:, 0]]

        with nc.Block() as block:
            @block.sync
            def _(sp):
                for to, frm, off in flat:
                    sp.dma_start(to[:], frm[off:off + EPAD].rearrange("(b r e) -> r b e", b=BLOCKS, e=P))\
                      .then_inc(s.rows_in, 16)
                sp.wait_ge(s.rows_out, 1)
                sp.dma_start(m.dst_f[1:1 + EPAD].rearrange("(b r e) -> r b e", b=BLOCKS, e=P), dst[:])\
                  .then_inc(s.flat_in, 16)
                sp.dma_start(m.dst_f[0:1].unsqueeze(0), prev[0:1, 0, 0:1]).then_inc(s.flat_in, 16)
                sp.wait_ge(s.map_ready, 1)
                sp.dma_start(m.node_map.rearrange("(p c) o -> p (c o)", p=P), nowhere[:]).then_inc(s.map_in, 16)
                sp.wait_ge(s.flat_in, 32)
                sp.wait_ge(s.map_in, 16)

            @block.gpsimd
            def _(pool):
                pool.iota(id_i[:], pattern=[[ROWS * P, BLOCKS], [1, P]], base=0, channel_multiplier=P)\
                    .then_inc(s.ids_ready, 1)
                pool.memset(nowhere[:], NOWHERE).then_inc(s.map_ready, 1)

            @block.scalar
            def _(act):
                act.wait_ge(s.deg_ready, 1)
                act.activation(m.sdeg[:], m.sdeg[:], ACT.Sqrt).then_inc(s.act_done, 1)

            @block.vector
            def _(dve):
                link = Chain(dve, s.dve_chain)
                dve.wait_ge(s.rows_in, 16 * len(flat))
                dve.wait_ge(s.ids_ready, 1)
                for to, frm in ((dst, dst_i), (prev, prev_i), (nxt, next_i), (src, src_i), (eid, id_i)):
                    ins = dve.tensor_copy(to[:], frm[:])
                link(ins)
                dve.sem_inc(s.rows_out, 1)
                dve.tensor_tensor(m.keep[:], dst[:], prev[:], ALU.is_equal)
                dve.tensor_tensor(first[:], dst[:], prev[:], ALU.not_equal)
                link(dve.tensor_tensor(m.last[:], dst[:], nxt[:], ALU.not_equal))
                dve.tensor_scalar(m.pen_f[:], first[:], LOW, None, ALU.mult)
                dve.tensor_scalar(m.pen_b[:], m.last[:], LOW, None, ALU.mult)
                dve.tensor_scalar(map_i[:], m.last[:], -float(NOWHERE), float(NOWHERE), ALU.mult, ALU.add)
                dve.tensor_reduce(flag[:, :, 0:1], first[:], AX.X, ALU.max)
                link(dve.tensor_reduce(flag[:, :, 1:2], m.last[:], AX.X, ALU.max))
                dve.tensor_tensor(map_i[:], map_i[:], dst[:], ALU.add)
                for h in range(HEADS):
                    dve.tensor_scalar(opens[:, :, 0, h:h + 1], flag[:, :, 0:1], LOW, None, ALU.mult)
                    dve.tensor_scalar(opens[:, :, 1, h:h + 1], flag[:, :, 0:1], -1.0, 1.0, ALU.mult, ALU.add)
                    ins = dve.tensor_scalar(opens[:, :, 2, h:h + 1], flag[:, :, 1:2], LOW, None, ALU.mult)
                ins.then_inc(s.flags_ready, 1)
                link(dve.memset(ones[:], 1.0))
                dve.wait_ge(s.opens_ready, 1)
                link(dve.tensor_copy(m.open_row[:, 0:2, :], m.bank[2][0:HEADS, 0:2 * TILES].rearrange("h (k t) -> h k t", k=2)))
                link(dve.tensor_copy(m.open_row[:, 2, :], m.bank[3][0:HEADS, 0:TILES]))
                scan_rows(dve, link, m, s, w, ones, count, 1, 0, "sum")
                scan_rows(dve, link, m, s, w, eid[:].unsqueeze(1), end, 1, 1, "back")
                dve.sem_inc(s.cols_ready, 1)
                dve.wait_ge(s.cols_done, 1)
                c = [m.bank[4 + k // 2][:, (k % 2) * TILES:(k % 2 + 1) * TILES] for k in range(len(cols))]
                dve.tensor_copy(m.dst[:], c[0])
                dve.tensor_copy(m.idx_l0[:, :, 0], c[1])
                dve.tensor_scalar(gathered[:], c[0], float(NODES - 1), None, ALU.min)
                dve.tensor_copy(m.map_idx[:], c[2])
                dve.tensor_copy(m.edge_id[:], c[3])
                dve.tensor_copy(m.indeg[:], c[4])
                link(dve.tensor_copy(m.idx_l1[:, :, 1], c[5]))
                dve.tensor_copy(m.idx_l0[:, :, 1], gathered[:])
                dve.tensor_scalar(m.rdeg[:], m.indeg[:], 1e-8, None, ALU.add)
                link(dve.tensor_scalar(m.sdeg[:], m.indeg[:], 1.0, None, ALU.add))
                dve.sem_inc(s.deg_ready, 1)
                link(dve.reciprocal(m.rdeg[:], m.rdeg[:]))
                dve.wait_ge(s.act_done, 1)
                link(dve.reciprocal(m.dinv[:], m.sdeg[:]))

            @block.tensor
            def _(pe):
                pe.wait_ge(s.flags_ready, 1)
                for k in range(3):
                    for b in range(BLOCKS):
                        at = (k % 2) * TILES + b * ROWS
                        ins = pe.transpose(m.bank[2 + k // 2][0:HEADS, at:at + ROWS], opens[:, b, k, :],
                                           m.ident[0:ROWS, 0:ROWS])
                ins.then_inc(s.opens_ready, 1)
                scan_rows_pe(pe, m, s, w, 1, 0, False)
                scan_rows_pe(pe, m, s, w, 1, 1, True)
                pe.wait_ge(s.cols_ready, 1)
                for k, rows in enumerate(cols):
                    for b in range(BLOCKS):
                        at = (k % 2) * TILES + b * ROWS
                        ins = pe.transpose(m.bank[4 + k // 2][:, at:at + ROWS], rows[:, b, :],
                                           m.ident[0:ROWS, 0:ROWS])
                ins.then_inc(s.cols_done, 1)


def load_key(sp, m, s, key, k):
    hold(sp, s.sel_done, k.t - (RING - 1))
    frm = m.dst_f[k.t * P:k.t * P + P + 1] if isinstance(k.t, int) else m.dst_f[bass.ds(k.t * P, P + 1)]
    sp.dma_start(key[:, k.slot, :], frm.partition_broadcast(P)).then_inc(s.key_in[k.slot], 16)


NORM_SEMS = ["bn_done", "mv_done", "root_done", "recip_done", "shift_done", "rows_done"]
NormSpace = namedtuple("NormSpace", "ring stats mv root rstd shift")


def norm_space(sb, n=P, ring=RING):
    return NormSpace(ring, sb("ystats", [n, ring, 6]), sb("mv", [n, ring, 2]), sb("root", [n, ring, 1]),
                     sb("rstd", [n, ring, 1]), sb("shift", [n, ring, 1]))


def norm_stats(dve, s, v, y, k):
    dve.bn_stats(v.stats[:, k.slot, :], y).then_inc(s.bn_done, 1)


def norm_aggregate(dve, s, v, k):
    hold(dve, s.bn_done, k.t + 1)
    dve.bn_aggr(v.mv[:, k.slot, :], v.stats[:, k.slot, :]).then_inc(s.mv_done, 1)


def norm_root(act, m, s, v, k, n=P):
    wait(act, s.recip_done, k.t - (v.ring - 1))
    act.wait_ge(s.mv_done, k.t + 1)
    act.activation(v.root[:, k.slot, :], v.mv[:, k.slot, 1:2], ACT.Sqrt, bias=m.eps[0:n]).then_inc(s.root_done, 1)


def norm_recip(dve, s, v, k):
    wait(dve, s.rows_done, k.t - (v.ring - 1))
    dve.wait_ge(s.root_done, k.t + 1)
    dve.reciprocal(v.rstd[:, k.slot, :], v.root[:, k.slot, :]).then_inc(s.recip_done, 1)


def norm_shift(dve, s, v, k):
    dve.wait_ge(s.recip_done, k.t + 1)
    dve.scalar_tensor_tensor(v.shift[:, k.slot, :], v.mv[:, k.slot, 0:1], -1.0, v.rstd[:, k.slot, :],
                             ALU.mult, ALU.mult).then_inc(s.shift_done, 1)


def norm_rows(act, s, v, to, y, k):
    act.wait_ge(s.shift_done, k.t + 1)
    act.activation(to, y, ACT.Identity, bias=v.shift[:, k.slot, :], scale=v.rstd[:, k.slot, :]).then_inc(s.rows_done, 1)


def edge_mlp(nc, d, m):
    names = ["idx_staged", "tr_done", "high_done", "low_done", "hid_done", "relu_done", "relu_low_done", "sel_done",
             "agg_done", "carry_done", "agg_high_done", "agg_low_done", "proj_done", "res_done", "y_done",
             "zero_done", "map_staged"] + NORM_SEMS
    rings = ["src_in", "dst_in", "key_in", "src_out", "state_out", "map_out"]
    ctx, s = phase(nc, "edge_mlp", names, rings)
    with ctx:
        def sb(name, shape, dt=F32):
            return ctx.enter_context(nc.sbuf_tensor("mlp_" + name, shape, dt))
        idx = sb("idx", [P, RING, 2], I32)
        map_at, map_val = sb("map_at", [P, RING], I32), sb("map_val", [P, RING], I32)
        xs, xd = sb("xs", [P, RING, FEAT]), sb("xd", [P, RING, FEAT])
        key = sb("key", [P, RING, P + 1])
        x_high, x_low = sb("x_high", [P, 2, 2 * FEAT], F32R), sb("x_low", [P, 2, 2 * FEAT], F32R)
        h_high, h_low = sb("h_high", [P, 2, HIDDEN], F32R), sb("h_low", [P, 2, HIDDEN], F32R)
        same, cont = sb("same", [P, RING, P], F32R), sb("cont", [P, RING, P])
        aggT = sb("aggT", [P, 2, HC, P])
        a_high, a_low = sb("a_high", [P, 2, HC, P], F32R), sb("a_low", [P, 2, HC, P], F32R)
        res, y, rows = sb("res", [P, RING, FEAT]), sb("y", [P, RING, FEAT]), sb("rows", [P, RING, FEAT])
        v = norm_space(sb)
        p_tr, p_hid, p_agg, p_out = (m.bank[2 * i:2 * i + 2] for i in range(4))

        with nc.Block() as block:
            @block.gpsimd
            def _(pool):
                def step(g, u):
                    if k := tile_at(g, u, 0):
                        hold(pool, s.src_in[k.slot], 16 * k.turn)
                        hold(pool, s.dst_in[k.slot], 16 * k.turn)
                        now = m.idx_l0[:, k.t, :] if isinstance(k.t, int) else \
                            m.idx_l0[:, bass.ds(k.t, 1), :].rearrange("p o k -> p (o k)")
                        pool.tensor_copy(idx[:, k.slot, :], now).then_inc(s.idx_staged, 1)
                        hold(pool, s.tr_done, k.t - (RING - 1))
                        hold(pool, s.src_out[k.slot], 16 * k.turn)
                        hold(pool, s.idx_staged, k.t + 1)
                        pool.indirect_dma_start(xs[:, k.slot, :], None, d.x,
                                                bass.IndirectOffsetOnAxis(ap=idx[:, k.slot, 0:1], axis=0))\
                            .then_inc(s.src_in[k.slot], 16)
                        hold(pool, s.res_done, k.t - (RING - 1))
                        pool.indirect_dma_start(xd[:, k.slot, :], None, d.x,
                                                bass.IndirectOffsetOnAxis(ap=idx[:, k.slot, 1:2], axis=0))\
                            .then_inc(s.dst_in[k.slot], 16)
                        hold(pool, s.map_out[k.slot], 16 * k.turn)
                        pool.tensor_copy(map_at[:, k.slot:k.slot + 1], col(m.map_idx, k.t))
                        pool.tensor_copy(map_val[:, k.slot:k.slot + 1], col(m.edge_id, k.t)).then_inc(s.map_staged, 1)
                        hold(pool, s.map_staged, k.t + 1)
                        pool.indirect_dma_start(m.node_map,
                                                bass.IndirectOffsetOnAxis(ap=map_at[:, k.slot:k.slot + 1], axis=0),
                                                map_val[:, k.slot:k.slot + 1], None,
                                                bounds_check=NODES - 1, oob_is_err=False)\
                            .then_inc(s.map_out[k.slot], 16)
                    if k := tile_at(g, u, 1):
                        hold(pool, s.dst_in[k.slot], 16 * (k.turn + 1))
                        hold(pool, s.y_done, k.t - (RING - 1))
                        pool.tensor_tensor(res[:, k.slot, :], xd[:, k.slot, :], m.b2[:], ALU.add).then_inc(s.res_done, 1)
                run_steps(pool, step, 1)
                for slot in range(RING):
                    pool.wait_ge(s.map_out[slot], 16 * (TILES // RING))

            @block.sync
            def _(sp):
                def step(g, u):
                    if k := tile_at(g, u, 0):
                        load_key(sp, m, s, key, k)
                    if k := tile_at(g, u, 1):
                        hold(sp, s.src_in[k.slot], 16 * (k.turn + 1))
                        sp.dma_start(tile_rows(m.x_src, k.t), xs[:, k.slot, :]).then_inc(s.src_out[k.slot], 16)
                    if k := tile_at(g, u, 8):
                        hold(sp, s.rows_done, k.t + 1)
                        sp.dma_start(tile_rows(m.state[1], k.t), rows[:, k.slot, :]).then_inc(s.state_out[k.slot], 16)
                run_steps(sp, step, 8)
                for slot in range(RING):
                    sp.wait_ge(s.src_out[slot], 16 * (TILES // RING))
                    sp.wait_ge(s.state_out[slot], 16 * (TILES // RING))

            @block.tensor
            def _(pe):
                def products(out_ap, high, low, w, start):
                    for c in range(len(high)):
                        for j, (a, b) in enumerate(((high[c], w[:, 0, c, :]), (high[c], w[:, 1, c, :]), (low[c], w[:, 0, c, :]))):
                            ins = pe.matmul(out_ap, a, b, start=start and c == 0 and j == 0,
                                            stop=c == len(high) - 1 and j == 2)
                    return ins

                def step(g, u):
                    if k := tile_at(g, u, 0):
                        pe.wait_ge(s.src_in[k.slot], 16 * (k.turn + 1))
                        pe.wait_ge(s.dst_in[k.slot], 16 * (k.turn + 1))
                        wait(pe, s.low_done, k.t - 1)
                        for c in range(FC):
                            pe.transpose(p_tr[k.pair][:, c * P:(c + 1) * P], xd[:, k.slot, c * P:(c + 1) * P], m.ident[:])
                        for c in range(FC):
                            ins = pe.transpose(p_tr[k.pair][:, FEAT + c * P:FEAT + (c + 1) * P],
                                               xs[:, k.slot, c * P:(c + 1) * P], m.ident[:])
                        ins.then_inc(s.tr_done, 1)
                    if k := tile_at(g, u, 1):
                        wait(pe, s.relu_low_done, k.t - 1)
                        pe.matmul(p_hid[k.pair][:], m.ones3[:], m.b1_parts[:], start=True, stop=False)
                        pe.wait_ge(s.low_done, k.t + 1)
                        cut = [slice(c * P, (c + 1) * P) for c in range(2 * FC)]
                        products(p_hid[k.pair][:], [x_high[:, k.pair, c] for c in cut], [x_low[:, k.pair, c] for c in cut],
                                 m.w1, False).then_inc(s.hid_done, 1)
                    if k := tile_at(g, u, 2):
                        pe.wait_ge(s.relu_low_done, k.t + 1)
                        pe.wait_ge(s.sel_done, k.t + 1)
                        wait(pe, s.carry_done, k.t - 1)
                        for c in range(HC):
                            for part in (h_high, h_low):
                                ins = pe.matmul(p_agg[k.pair][:, c * P:(c + 1) * P], part[:, k.pair, c * P:(c + 1) * P],
                                                same[:, k.slot, :], start=part is h_high, stop=part is h_low)
                        ins.then_inc(s.agg_done, 1)
                    if k := tile_at(g, u, 4):
                        pe.wait_ge(s.agg_low_done, k.t + 1)
                        wait(pe, s.y_done, k.t - 1)
                        products(p_out[k.pair][:, 0:FEAT], [a_high[:, k.pair, c, :] for c in range(HC)],
                                 [a_low[:, k.pair, c, :] for c in range(HC)], m.w2, True).then_inc(s.proj_done, 1)
                run_steps(pe, step, 4)

            @block.scalar
            def _(act):
                def step(g, u):
                    if k := tile_at(g, u, 7):
                        wait(act, s.state_out[k.slot], 16 * k.turn)
                        norm_rows(act, s, v, rows[:, k.slot, :], y[:, k.slot, :], k)
                    if k := tile_at(g, u, 0):
                        act.wait_ge(s.tr_done, k.t + 1)
                        wait(act, s.hid_done, k.t - 1)
                        act.copy(x_high[:, k.pair, :], p_tr[k.pair][:]).then_inc(s.high_done, 1)
                    if k := tile_at(g, u, 1):
                        act.wait_ge(s.hid_done, k.t + 1)
                        wait(act, s.agg_done, k.t - 1)
                        act.activation(h_high[:, k.pair, :], p_hid[k.pair][:], ACT.Relu).then_inc(s.relu_done, 1)
                    if k := tile_at(g, u, 3):
                        act.wait_ge(s.carry_done, k.t + 1)
                        wait(act, s.proj_done, k.t - 1)
                        act.copy(a_high[:, k.pair, :, :], aggT[:, k.pair, :, :]).then_inc(s.agg_high_done, 1)
                    if k := tile_at(g, u, 5):
                        norm_root(act, m, s, v, k)
                run_steps(act, step, 7)

            @block.vector
            def _(dve):
                dve.memset(aggT[:, 1, :, P - 1], 0.0).then_inc(s.zero_done, 1)
                dve.wait_ge(s.zero_done, 1)

                def step(g, u):
                    if k := tile_at(g, u, 4):
                        dve.wait_ge(s.agg_high_done, k.t + 1)
                        dve.tensor_tensor(a_low[:, k.pair, :, :], aggT[:, k.pair, :, :],
                                          a_high[:, k.pair, :, :].bitcast(F32), ALU.subtract).then_inc(s.agg_low_done, 1)
                    if k := tile_at(g, u, 2):
                        dve.wait_ge(s.relu_done, k.t + 1)
                        dve.scalar_tensor_tensor(h_low[:, k.pair, :], p_hid[k.pair][:], 0.0,
                                                 h_high[:, k.pair, :].bitcast(F32), ALU.max, ALU.subtract)\
                           .then_inc(s.relu_low_done, 1)
                    if k := tile_at(g, u, 0):
                        dve.wait_ge(s.high_done, k.t + 1)
                        dve.tensor_tensor(x_low[:, k.pair, :], p_tr[k.pair][:], x_high[:, k.pair, :].bitcast(F32),
                                          ALU.subtract).then_inc(s.low_done, 1)
                    if k := tile_at(g, u, 3):
                        carry_over(dve, s, aggT, cont, p_agg, k, HC, s.agg_low_done)
                    if k := tile_at(g, u, 6):
                        norm_recip(dve, s, v, k)
                        norm_shift(dve, s, v, k)
                    if k := tile_at(g, u, 5):
                        dve.wait_ge(s.proj_done, k.t + 1)
                        dve.wait_ge(s.res_done, k.t + 1)
                        wait(dve, s.rows_done, k.t - (RING - 1))
                        dve.scalar_tensor_tensor(y[:, k.slot, :], p_out[k.pair][:, 0:FEAT], col(m.rdeg, k.t),
                                                 res[:, k.slot, :], ALU.mult, ALU.add).then_inc(s.y_done, 1)
                        dve.wait_ge(s.y_done, k.t + 1)
                        norm_stats(dve, s, v, y[:, k.slot, :], k)
                        norm_aggregate(dve, s, v, k)
                    if k := tile_at(g, u, 1):
                        select(dve, m, s, key, same, cont, k)
                run_steps(dve, step, 6)




def affine_scalars(s, m, n, base, mean, var, cov, root, out, tmp):
    r1, r3, t, u = tmp
    alpha, beta, gamma = out
    bm, bv = m.bias_mv[0:n, 0:1], m.bias_mv[0:n, 1:2]

    def first(dve, link):
        dve.wait_ge(s.aff_root, base + 1)
        link(dve.reciprocal(r1, root))
        link(dve.scalar_tensor_tensor(t, mean, bm, cov, ALU.mult, ALU.subtract))
        link(dve.tensor_tensor(t, t, r1, ALU.mult))
        link(dve.tensor_tensor(u, r1, r1, ALU.mult))
        link(dve.tensor_tensor(u, u, var, ALU.mult))
        link(dve.scalar_tensor_tensor(u, t, -2.0, u, ALU.mult, ALU.add))
        dve.tensor_scalar(cov, u, bv, None, ALU.add).then_inc(s.aff_ask, 1)
        link(dve.tensor_tensor(t, r1, mean, ALU.mult))
        link(dve.tensor_scalar(t, t, bm, -1.0, ALU.add, ALU.mult))

    def second(dve, link):
        dve.wait_ge(s.aff_root, base + 2)
        link(dve.reciprocal(beta, root))
        link(dve.tensor_tensor(u, beta, beta, ALU.mult))
        dve.tensor_tensor(cov, cov, u, ALU.mult).then_inc(s.aff_ask, 1)
        link(dve.tensor_tensor(alpha, r1, beta, ALU.mult))
        link(dve.tensor_tensor(gamma, t, beta, ALU.mult))

    def third(dve, link):
        dve.wait_ge(s.aff_root, base + 3)
        link(dve.reciprocal(r3, root))
    return first, second, third


def affine_root(act, s, m, n, base, k, var, cov, root):
    act.wait_ge(s.aff_ask, base + k + 1)
    act.activation(root, cov if k else var, ACT.Sqrt, bias=m.eps[0:n]).then_inc(s.aff_root, 1)


def untouched_nodes(nc, d, m, out, n, first, tiles, unroll, batch, piece):
    main = tiles > 1
    pieces, slots = unroll // piece, min(2 * piece, unroll)
    names = ["seen", "dve_chain", "aff_ask", "aff_root", "scalars_done", "scaled", "x3_done", "tr_done", "evac_done",
             "proj_done", "sum_done", "staged", "moments_bn"] + NORM_SEMS
    ctx, s = phase(nc, "untouched" if main else "tail", names, (),
                   [("x_in", pieces), ("out_done", 2), ("found", LOOKUPS)])
    with ctx:
        tag = "main_" if main else "tail_"

        def sb(name, shape, dt=F32):
            return ctx.enter_context(nc.sbuf_tensor(tag + name, shape, dt))
        xin = sb("xin", [n, unroll, FEAT])
        stats, junk = sb("stats", [n, 2, 6]), sb("junk", [n, 2, FEAT])
        mom = sb("moments", [n, 2, 3, batch])
        root_b, out2, tmp = sb("root_b", [n, batch]), sb("out2", [n, 3, batch]), sb("tmpb", [n, 4, batch])
        aff = sb("aff", [n, 2, 3, batch])
        x3, x3T = sb("x3", [n, 3, FEAT]), sb("x3T", [P, 2, FC, n])
        v_norm = norm_space(sb, n, Y_BANKS)
        yrows = sb("yrows", [n, slots, FEAT])
        stage, pos = sb("stage", [P, LOOKUPS], I32), sb("pos", [P, LOOKUPS], I32)
        p_tr, p_out = m.bank[0:2], m.bank[2:2 + Y_BANKS]
        x_at = d.x[first:first + n * tiles, :].rearrange("(p k) f -> p (k f)", p=n)
        out_at = out[first:first + n * tiles, :].rearrange("(p k) f -> p (k f)", p=n)

        def at(g, u, lag):
            k = tile_at(g, u, lag, unroll, tiles)
            return k and k._replace(slot=(u - lag) % unroll % Y_BANKS)

        def steps(eng, step, lag):
            run_steps(eng, step, lag, unroll, tiles, 2)

        def batch_of(g, u, lag):
            v = u - lag
            return g * (unroll // batch) + v // batch, v % unroll // batch, v % batch

        def piece_ap(ap, t):
            size = piece * FEAT
            return ap[:, t * FEAT:t * FEAT + size] if isinstance(t, int) else ap[:, bass.ds(t * FEAT, size)]

        def triple(g, u, lag):
            return (u - lag) % unroll % 3
        A = piece
        B = A + 3 + batch

        with nc.Block() as block:
            @block.sync
            def _(sp):
                def step(g, u):
                    if (k := at(g, u, 0)) and u % piece == 0:
                        hold(sp, s.x3_done, k.t - unroll + piece)
                        lo = k.body_slot
                        sp.dma_start(xin[:, lo:lo + piece, :].rearrange("p k f -> p (k f)"), piece_ap(x_at, k.t))\
                          .then_inc(s.x_in[lo // piece], 16)
                    v = u - (B + 8)
                    if (k := at(g, u, B + 8)) and v % piece == piece - 1:
                        slot = (v % slots) // piece
                        hold(sp, s.rows_done, k.t + 1)
                        lo = slot * piece
                        sp.dma_start(piece_ap(out_at, k.t - (piece - 1)),
                                     yrows[:, lo:lo + piece, :].rearrange("p k f -> p (k f)"))\
                          .then_inc(s.out_done[slot], 16)
                steps(sp, step, B + 8)
                stores = tiles // piece
                for slot in range(2):
                    hold(sp, s.out_done[slot], 16 * ((stores + 1 - slot) // 2))

            @block.gpsimd
            def _(pool):
                def look_up(t, slot, turn):
                    put_away(t, slot, turn)
                    pool.tensor_copy(stage[:, slot:slot + 1], m.idx_l0[:, t:t + 1, 0] if isinstance(t, int) else
                                     m.idx_l0[:, bass.ds(t, 1), 0]).then_inc(s.staged, 1)
                    hold(pool, s.staged, t - (0 if main else TILES - 1) + 1)
                    pool.indirect_dma_start(pos[:, slot:slot + 1], None, m.node_map,
                                            bass.IndirectOffsetOnAxis(ap=stage[:, slot:slot + 1], axis=0))\
                        .then_inc(s.found[slot], 16)

                def put_away(t, slot, turn):
                    if isinstance(turn, int) and turn == 0:
                        return
                    hold(pool, s.found[slot], 16 * turn)
                    t -= LOOKUPS
                    to = m.idx_l1[:, t:t + 1, 0] if isinstance(t, int) else m.idx_l1[:, bass.ds(t, 1), 0]
                    pool.tensor_copy(to, pos[:, slot:slot + 1])

                def step(g, u):
                    if main and u % 2 == 1 and not (isinstance(g, int) and g >= tiles // unroll):
                        j = u // 2
                        look_up(g * (unroll // 2) + j, j % LOOKUPS, g * (unroll // (2 * LOOKUPS)) + j // LOOKUPS)
                steps(pool, step, 0)
                if main:
                    done = tiles // 2
                    for i in range(LOOKUPS):
                        put_away(done + i, (done + i) % LOOKUPS, done // LOOKUPS)
                else:
                    look_up(TILES - 1, 0, 0)
                    put_away(TILES - 1 + LOOKUPS, 0, 1)

            @block.scalar
            def _(act):
                def step(g, u):
                    if k := at(g, u, B + 8):
                        v = u - (B + 8)
                        slot = v % slots
                        if v % piece == 0:
                            wait(act, s.out_done[slot // piece], 16 * (k.t // (2 * piece)) if isinstance(k.t, int)
                                 else 16 * (g * (unroll // (2 * piece)) + v // (2 * piece)))
                        norm_rows(act, s, v_norm, yrows[:, slot, :], p_out[k.slot][0:n, 0:FEAT], k)
                    if k := at(g, u, B + 6):
                        norm_root(act, m, s, v_norm, k, n)
                    if k := at(g, u, B + 3):
                        act.wait_ge(s.tr_done, k.t + 1)
                        wait(act, s.proj_done, k.t - 1)
                        act.copy(x3T[:, k.pair, :, :], p_tr[k.pair][:, 0:FC * n].rearrange("p (c n) -> p c n", c=FC))\
                           .then_inc(s.evac_done, 1)
                    if k := at(g, u, B):
                        number, slot, i = batch_of(g, u, B)
                        act.wait_ge(s.scalars_done, number + 1)
                        wait(act, s.tr_done, k.t - 2)
                        act.activation(x3[:, triple(g, u, B), :], xin[:, k.body_slot, :], ACT.Identity,
                                       bias=aff[:, slot, 2, i:i + 1], scale=aff[:, slot, 0, i:i + 1])\
                           .then_inc(s.scaled, 1)
                    for part in range(3):
                        number, slot, i = batch_of(g, u, A + part)
                        if at(g, u, A + part) and i == batch - 1:
                            affine_root(act, s, m, n, number * 3, part, mom[:, slot, 1, :], mom[:, slot, 2, :], root_b[:])
                steps(act, step, B + 8)

            @block.tensor
            def _(pe):
                def step(g, u):
                    if k := at(g, u, B + 4):
                        pe.wait_ge(s.evac_done, k.t + 1)
                        wait(pe, s.rows_done, k.t - (Y_BANKS - 1))
                        y = p_out[k.slot][0:n, 0:FEAT]
                        pe.matmul(y, m.ones3[:, 0:n], m.res_parts[:], start=True, stop=False)
                        for c in range(FC):
                            ins = pe.matmul(y, x3T[:, k.pair, c, :], m.w_res[:, c, :], start=False, stop=c == FC - 1)
                        ins.then_inc(s.proj_done, 1)
                    if k := at(g, u, B + 2):
                        ring = triple(g, u, B + 2)
                        pe.wait_ge(s.x3_done, k.t + 1)
                        wait(pe, s.evac_done, k.t - 1)
                        for c in range(FC):
                            ins = pe.transpose(p_tr[k.pair][:, c * n:(c + 1) * n], x3[:, ring, c * P:(c + 1) * P],
                                               m.ident[0:n, 0:n])
                        ins.then_inc(s.tr_done, 1)
                steps(pe, step, B + 4)

            @block.vector
            def _(dve):
                def step(g, u):
                    if k7 := at(g, u, B + 7):
                        norm_recip(dve, s, v_norm, k7)
                    if k5 := at(g, u, B + 5):
                        dve.wait_ge(s.proj_done, k5.t + 1)
                        norm_stats(dve, s, v_norm, p_out[k5.slot][0:n, 0:FEAT], k5)
                    if k7:
                        norm_shift(dve, s, v_norm, k7)
                    if k := at(g, u, B + 1):
                        _, slot, i = batch_of(g, u, B + 1)
                        row = x3[:, triple(g, u, B + 1), :]
                        dve.wait_ge(s.scaled, k.t + 1)
                        dve.scalar_tensor_tensor(row, m.bias[0:n], aff[:, slot, 1, i:i + 1], row, ALU.mult, ALU.add)\
                           .then_inc(s.x3_done, 1)
                    if k5:
                        norm_aggregate(dve, s, v_norm, k5)
                    for part in range(3):
                        k = at(g, u, A + 1 + part)
                        number, slot, i = batch_of(g, u, A + 1 + part)
                        if not k or i != batch - 1:
                            continue
                        tm = [tmp[:, j, :] for j in range(4)]
                        parts = affine_scalars(s, m, n, number * 3, *(mom[:, slot, j, :] for j in range(3)),
                                               root_b[:], [out2[:, j, :] for j in range(3)], tm)
                        link = Chain(dve, s.dve_chain, number * (sum(AFFINE_LINKS) + 1) + sum(AFFINE_LINKS[:part]))
                        parts[part](dve, link)
                        if part == 2:
                            wait(dve, s.x3_done, k.t + 1 - 2 * batch)
                            for j in range(3):
                                ins = dve.tensor_tensor(aff[:, slot, j, :], out2[:, j, :], tm[1], ALU.mult)
                            link(ins)
                            dve.sem_inc(s.scalars_done, 1)
                    if k := at(g, u, A):
                        b, slot, i = batch_of(g, u, A)
                        if (u - A) % piece == 0:
                            dve.wait_ge(s.x_in[k.body_slot // piece], 16 * (k.body + 1))
                        wait(dve, s.seen, k.t - 1)
                        dve.bn_stats(stats[:, k.pair, :], xin[:, k.body_slot, :]).then_inc(s.moments_bn, 1)
                        dve.scalar_tensor_tensor(junk[:, k.pair, :], xin[:, k.body_slot, :], 1.0 / FEAT, m.bias[0:n],
                                                 ALU.mult, ALU.mult, accum_out=mom[:, slot, 2, i:i + 1])
                        hold(dve, s.moments_bn, k.t + 1)
                        dve.bn_aggr(mom[:, slot, 0:2, i], stats[:, k.pair, :]).then_inc(s.seen, 1)
                        if i == batch - 1:
                            hold(dve, s.seen, k.t + 1)
                            dve.sem_inc(s.aff_ask, 1)
                steps(dve, step, B + 7)


def gather_pos(pool, m, s, k, to, table, idx, ready):
    pool.indirect_dma_start(to, None, table, bass.IndirectOffsetOnAxis(ap=idx, axis=0),
                            bounds_check=EPAD - 1, oob_is_err=False).then_inc(ready, 16)


def gat_scores(nc, d, m):
    names = ["idx_staged", "bn_done", "seen", "root_done", "recip_done", "scal_done", "put_done", "x1_done", "tr_done", "evac_done",
             "prod_done", "enc_done", "h_done", "mul_done", "red_done", "score_done", "dve_chain", "aff_ask", "aff_root",
             "flags_done", "ones_done"]
    rings = ["src_in", "dst_in", "edge_in", "h_out"]
    ctx, s = phase(nc, "gat_scores", names, rings, [("x_in", UNROLL)])
    with ctx:
        def sb(name, shape, dt=F32):
            return ctx.enter_context(nc.sbuf_tensor("gs_" + name, shape, dt))
        idx = sb("idx", [P, RING, 2], I32)
        xs, xd = sb("xs", [P, UNROLL, FEAT]), sb("xd", [P, RING, FEAT])
        edge = sb("edge", [EDGE_FEAT + 1, RING, P])
        stats, mom, junk = sb("stats", [P, 2, 6]), sb("mom", [P, RING, 3]), sb("junk", [P, 2, FEAT])
        root, rstd, scal = sb("root", [P, RING, 1]), sb("rstd", [P, RING, 1]), sb("scal", [P, RING, 2])
        x1, xT = sb("x1", [P, 2, FEAT]), sb("xT", [P, 2, 2 * FEAT])
        enc, prod, red, h = sb("enc", [P, 2, FEAT]), sb("prod", [P, 2, FEAT]), sb("red", [P, 2, HEADS]), sb("h", [P, RING, FEAT])
        root_all, tmp = sb("root_all", [P, TILES]), sb("tmp", [P, 4, TILES])
        p_tr, p_src, p_dst, p_lin = (m.bank[2 * i:2 * i + 2] for i in range(4))
        neg_un = sb("neg_un", [P, TILES])

        with nc.Block() as block:
            @block.sync
            def _(sp):
                def step(g, u):
                    if k := tile_at(g, u, 0):
                        hold(sp, s.x1_done, k.t - (UNROLL - 1))
                        sp.dma_start(xs[:, k.body_slot, :], tile_rows(m.x_src, k.t)).then_inc(s.x_in[k.body_slot], 16)
                    if k := tile_at(g, u, 4):
                        if isinstance(k.t, int) and k.t == 0:
                            sp.wait_ge(s.ones_done, 1)
                        hold(sp, s.prod_done, k.t - (RING - 1))
                        frm = d.edge_attr_T[:, k.t * P:k.t * P + P] if isinstance(k.t, int) else \
                            d.edge_attr_T[:, bass.ds(k.t * P, P)]
                        sp.dma_start(edge[0:EDGE_FEAT, k.slot, :], frm).then_inc(s.edge_in[k.slot], 16)
                    if k := tile_at(g, u, 12):
                        hold(sp, s.h_done, k.t + 1)
                        sp.dma_start(tile_rows(m.h_src, k.t), h[:, k.slot, :]).then_inc(s.h_out[k.slot], 16)
                run_steps(sp, step, 12)
                for slot in range(RING):
                    sp.wait_ge(s.h_out[slot], 16 * (TILES // RING))

            @block.gpsimd
            def _(pool):
                pool.memset(edge[:], 1.0).then_inc(s.ones_done, 1)

                def step(g, u):
                    if k := tile_at(g, u, 2):
                        hold(pool, s.src_in[k.slot], 16 * k.turn)
                        hold(pool, s.dst_in[k.slot], 16 * k.turn)
                        now = m.idx_l1[:, k.t, :] if isinstance(k.t, int) else \
                            m.idx_l1[:, bass.ds(k.t, 1), :].rearrange("p o k -> p (o k)")
                        pool.tensor_copy(idx[:, k.slot, :], now).then_inc(s.idx_staged, 1)
                        hold(pool, s.idx_staged, k.t + 1)
                        hold(pool, s.x_in[k.body_slot], 16 * (k.body + 1))
                        gather_pos(pool, m, s, k, xs[:, k.body_slot, :], m.state[1], idx[:, k.slot, 0:1], s.src_in[k.slot])
                        hold(pool, s.tr_done, k.t - (RING - 1))
                        gather_pos(pool, m, s, k, xd[:, k.slot, :], m.state[1], idx[:, k.slot, 1:2], s.dst_in[k.slot])
                run_steps(pool, step, 2)

            @block.scalar
            def _(act):
                def step(g, u):
                    if k := tile_at(g, u, 11):
                        act.wait_ge(s.prod_done, k.t + 1)
                        wait(act, s.mul_done, k.t - 1)
                        act.activation(enc[:, k.pair, :], p_dst[k.pair][:, FEAT:2 * FEAT], ACT.Relu).then_inc(s.enc_done, 1)
                        wait(act, s.h_out[k.slot], 16 * k.turn)
                        act.copy(h[:, k.slot, :], p_src[k.pair][:, 0:FEAT]).then_inc(s.h_done, 1)
                    if k := tile_at(g, u, 9):
                        act.wait_ge(s.tr_done, k.t + 1)
                        wait(act, s.prod_done, k.t - 1)
                        act.copy(xT[:, k.pair, :], p_tr[k.pair][:]).then_inc(s.evac_done, 1)
                    if k := tile_at(g, u, 7):
                        act.wait_ge(s.scal_done, k.t + 1)
                        wait(act, s.tr_done, k.t - 1)
                        act.activation(x1[:, k.pair, :], xs[:, k.body_slot, :], ACT.Identity, bias=scal[:, k.slot, 1:2],
                                       scale=scal[:, k.slot, 0:1]).then_inc(s.x1_done, 1)
                    if k := tile_at(g, u, 5):
                        act.wait_ge(s.seen, k.t + 1)
                        wait(act, s.recip_done, k.t - (RING - 1))
                        act.activation(root[:, k.slot, :], mom[:, k.slot, 1:2], ACT.Sqrt, bias=m.eps[:]).then_inc(s.root_done, 1)
                run_steps(act, step, 11)
                for part in range(3):
                    affine_root(act, s, m, P, 0, part, m.row_stat[:, 1, :], m.row_stat[:, 2, :], root_all[:])

            @block.tensor
            def _(pe):
                def step(g, u):
                    if k := tile_at(g, u, 10):
                        pe.wait_ge(s.evac_done, k.t + 1)
                        pe.wait_ge(s.edge_in[k.slot], 16 * (k.turn + 1))
                        wait(pe, s.h_done, k.t - 1)
                        wait(pe, s.mul_done, k.t - 1)
                        src = [xT[:, k.pair, c * P:(c + 1) * P] for c in range(FC)]
                        dst = [xT[:, k.pair, FEAT + c * P:FEAT + (c + 1) * P] for c in range(FC)]
                        pe.matmul(p_dst[k.pair][:, FEAT:2 * FEAT], edge[:, k.slot, :], m.w_enc[:], start=True, stop=True)
                        for c in range(FC):
                            pe.matmul(p_src[k.pair][:, 0:FEAT], src[c], m.w_src[:, c, 0:FEAT], start=c == 0, stop=c == FC - 1)
                        for c in range(FC):
                            pe.matmul(p_dst[k.pair][:, 0:FEAT], dst[c], m.w_src[:, c, 0:FEAT], start=c == 0, stop=c == FC - 1)
                        wait(pe, s.score_done, k.t - 1)
                        linear = [(src[c], m.w_src[:, c, FEAT:FEAT + HEADS]) for c in range(FC)]
                        linear += [(dst[c], m.w_dst[:, c, :]) for c in range(FC)]
                        for i, (rows, wgt) in enumerate(linear):
                            ins = pe.matmul(p_lin[k.pair][:, 0:HEADS], rows, wgt, start=i == 0, stop=i == len(linear) - 1)
                        ins.then_inc(s.prod_done, 1)
                    if k := tile_at(g, u, 8):
                        pe.wait_ge(s.x1_done, k.t + 1)
                        pe.wait_ge(s.dst_in[k.slot], 16 * (k.turn + 1))
                        wait(pe, s.evac_done, k.t - 1)
                        for c in range(FC):
                            pe.transpose(p_tr[k.pair][:, c * P:(c + 1) * P], x1[:, k.pair, c * P:(c + 1) * P], m.ident[:])
                        for c in range(FC):
                            ins = pe.transpose(p_tr[k.pair][:, FEAT + c * P:FEAT + (c + 1) * P],
                                               xd[:, k.slot, c * P:(c + 1) * P], m.ident[:])
                        ins.then_inc(s.tr_done, 1)
                run_steps(pe, step, 10)

            @block.vector
            def _(dve):
                dve.tensor_scalar(m.touched[:], m.idx_l1[:, :, 0], float(NOWHERE), None, ALU.is_lt)
                dve.tensor_scalar(m.untouched[:], m.idx_l1[:, :, 0], float(NOWHERE), None, ALU.is_ge)
                dve.tensor_scalar(neg_un[:], m.idx_l1[:, :, 0], float(NOWHERE), -1.0, ALU.is_ge, ALU.mult).then_inc(s.flags_done, 1)
                dve.wait_ge(s.flags_done, 1)

                def step(g, u):
                    if k := tile_at(g, u, 12):
                        dve.wait_ge(s.mul_done, k.t + 1)
                        wait(dve, s.score_done, k.t - 1)
                        dve.tensor_reduce(red[:, k.pair, :], prod[:, k.pair, :].rearrange("p (h d) -> p h d", h=HEADS),
                                          AX.X, ALU.add).then_inc(s.red_done, 1)
                        dve.wait_ge(s.red_done, k.t + 1)
                        to = m.score[:, k.t, :] if isinstance(k.t, int) else \
                            m.score[:, bass.ds(k.t, 1), :].rearrange("p o h -> p (o h)")
                        dve.tensor_tensor(to, red[:, k.pair, :], p_lin[k.pair][:, 0:HEADS], ALU.add)\
                           .then_inc(s.score_done, 1)
                    if k := tile_at(g, u, 6):
                        dve.wait_ge(s.root_done, k.t + 1)
                        wait(dve, s.x1_done, k.t - (RING - 1))
                        dve.reciprocal(rstd[:, k.slot, :], root[:, k.slot, :]).then_inc(s.recip_done, 1)
                        dve.wait_ge(s.recip_done, k.t + 1)
                        dve.scalar_tensor_tensor(scal[:, k.slot, 0:1], rstd[:, k.slot, :], col(m.untouched, k.t),
                                                 col(m.touched, k.t), ALU.mult, ALU.add)
                        dve.scalar_tensor_tensor(scal[:, k.slot, 1:2], mom[:, k.slot, 0:1], rstd[:, k.slot, :],
                                                 col(neg_un, k.t), ALU.mult, ALU.mult).then_inc(s.scal_done, 1)
                        to = m.row_stat[:, :, k.t] if isinstance(k.t, int) else \
                            m.row_stat[:, :, bass.ds(k.t, 1)].rearrange("p k o -> p (k o)")
                        dve.tensor_copy(to, mom[:, k.slot, :]).then_inc(s.put_done, 1)
                    if k := tile_at(g, u, 4):
                        dve.wait_ge(s.src_in[k.slot], 16 * (k.turn + 1))
                        wait(dve, s.seen, k.t - 1)
                        wait(dve, s.put_done, k.t - (RING - 1))
                        dve.bn_stats(stats[:, k.pair, :], xs[:, k.body_slot, :]).then_inc(s.bn_done, 1)
                        dve.scalar_tensor_tensor(junk[:, k.pair, :], xs[:, k.body_slot, :], 1.0 / FEAT, m.bias[:],
                                                 ALU.mult, ALU.mult, accum_out=mom[:, k.slot, 2:3])
                        hold(dve, s.bn_done, k.t + 1)
                        dve.bn_aggr(mom[:, k.slot, 0:2], stats[:, k.pair, :]).then_inc(s.seen, 1)
                    if k := tile_at(g, u, 11):
                        dve.wait_ge(s.enc_done, k.t + 1)
                        wait(dve, s.red_done, k.t - 1)
                        dve.tensor_tensor(prod[:, k.pair, :], enc[:, k.pair, :], p_dst[k.pair][:, 0:FEAT], ALU.mult)\
                           .then_inc(s.mul_done, 1)
                run_steps(dve, step, 12)
                dve.wait_ge(s.put_done, TILES)
                dve.sem_inc(s.aff_ask, 1)
                link = Chain(dve, s.dve_chain, 0)
                tm = [tmp[:, j, :] for j in range(4)]
                second, third = ([m.affine[:, i, j, :] for j in range(3)] for i in range(2))
                for part in affine_scalars(s, m, P, 0, *(m.row_stat[:, j, :] for j in range(3)), root_all[:], second, tm):
                    part(dve, link)
                for j in range(3):
                    ins = dve.tensor_tensor(third[j], second[j], tm[1], ALU.mult)
                link(ins)
                for part in (*second, *third):
                    ins = dve.tensor_tensor(part, part, m.untouched[:], ALU.mult)
                link(ins)
                for part in (second[0], third[0]):
                    dve.tensor_tensor(part, part, m.touched[:], ALU.add)


def softmax_rows(dve, link, act_exp, m, s, w, score, run, spread, heads, n):
    scan_rows(dve, link, m, s, w, score, run, heads, n, "max")
    scan_rows(dve, link, m, s, w, run, spread, heads, n + 1, "back")
    link(dve.tensor_tensor(score, score, spread, ALU.subtract))
    act_exp()
    scan_rows(dve, link, m, s, w, score, run, heads, n + 2, "sum")
    scan_rows(dve, link, m, s, w, run, spread, heads, n + 3, "back")


def gat_softmax(nc, m):
    ctx, s = phase(nc, "gat_softmax", ["dve_chain", "leaky_done", "in_rows", "exp_ask", "exp_done", "weights_done", "in_cols"] + SCAN_SEMS)
    with ctx:
        def sb(name, shape, dt=F32):
            return ctx.enter_context(nc.sbuf_tensor("sm_" + name, shape, dt))
        shape = [ROWS, HEADS, BLOCKS, P]
        score, run, spread = sb("score", shape), sb("run", shape), sb("spread", shape)
        w = ScanSpace(total=sb("total", [ROWS, BLOCKS, HEADS]), between=sb("between", [HEADS, TILES + 1]),
                            carry=sb("carry", [ROWS, BLOCKS, HEADS]))
        pairs = [(h, b) for h in range(HEADS) for b in range(BLOCKS)]
        with nc.Block() as block:
            @block.tensor
            def _(pe):
                pe.wait_ge(s.leaky_done, 1)
                for k, (h, b) in enumerate(pairs):
                    ins = pe.transpose(m.bank[2 + k // 4][0:ROWS, (k % 4) * P:(k % 4 + 1) * P],
                                       m.score[:, b * ROWS:(b + 1) * ROWS, h], m.ident[:])
                ins.then_inc(s.in_rows, 1)
                for n, back in enumerate((False, True, False, True)):
                    scan_rows_pe(pe, m, s, w, HEADS, n, back)
                pe.wait_ge(s.weights_done, 1)
                for k, (h, b) in enumerate(pairs):
                    ins = pe.transpose(m.bank[2 + k // 4][:, (k % 4) * ROWS:(k % 4 + 1) * ROWS], score[:, h, b, :],
                                       m.ident[0:ROWS, 0:ROWS])
                ins.then_inc(s.in_cols, 1)

            @block.scalar
            def _(act):
                act.wait_ge(s.exp_ask, 1)
                act.activation(score[:], score[:], ACT.Exp).then_inc(s.exp_done, 1)

            @block.vector
            def _(dve):
                link = Chain(dve, s.dve_chain)
                flat = m.score[:].rearrange("p t h -> p (t h)")
                dve.scalar_tensor_tensor(flat, flat, 0.2, flat, ALU.mult, ALU.max).then_inc(s.leaky_done, 1)
                dve.wait_ge(s.in_rows, 1)
                for j in range(4):
                    ins = dve.tensor_copy(score[:, 2 * j:2 * j + 2, :, :].rearrange("r h b e -> r (h b e)"),
                                          m.bank[2 + j][0:ROWS, :])
                link(ins)

                def exp():
                    dve.sem_inc(s.exp_ask, 1)
                    dve.wait_ge(s.exp_done, 1)
                softmax_rows(dve, link, exp, m, s, w, score[:], run[:], spread[:], HEADS, 0)
                link(dve.tensor_scalar(spread[:], spread[:], 1e-10, None, ALU.max))
                link(dve.reciprocal(spread[:], spread[:]))
                dve.tensor_tensor(score[:], score[:], spread[:], ALU.mult).then_inc(s.weights_done, 1)
                dve.wait_ge(s.in_cols, 1)
                for j in range(4):
                    dve.tensor_copy(m.score[:].rearrange("p (b r) h -> p h b r", b=BLOCKS)[:, 2 * j:2 * j + 2, :, :],
                                    m.bank[2 + j][:, 0:4 * ROWS].rearrange("p (h b r) -> p h b r", h=2, b=BLOCKS))


def scalar_softmax(nc, m):
    ctx, s = phase(nc, "scalar_softmax", ["dve_chain", "in_rows", "exp_ask", "exp_done", "weights_done", "in_cols"] + SCAN_SEMS)
    with ctx:
        def sb(name, shape, dt=F32):
            return ctx.enter_context(nc.sbuf_tensor("sq_" + name, shape, dt))
        shape = [ROWS, 1, BLOCKS, P]
        q, k, score, run, spread = (sb(n, shape) for n in ("q", "k", "score", "run", "spread"))
        w = ScanSpace(total=sb("total", [ROWS, BLOCKS, 1]), between=sb("between", [1, TILES + 1]),
                            carry=sb("carry", [ROWS, BLOCKS, 1]))
        with nc.Block() as block:
            @block.tensor
            def _(pe):
                for i, cols in enumerate((m.q_src, m.k_dst)):
                    for b in range(BLOCKS):
                        at = (i * BLOCKS + b) * P
                        ins = pe.transpose(m.bank[2][0:ROWS, at:at + P], cols[:, b * ROWS:(b + 1) * ROWS], m.ident[:])
                ins.then_inc(s.in_rows, 1)
                for n, back in enumerate((True, False, True, False, True)):
                    scan_rows_pe(pe, m, s, w, 1, n, back)
                pe.wait_ge(s.weights_done, 1)
                for b in range(BLOCKS):
                    ins = pe.transpose(m.bank[2][:, b * ROWS:(b + 1) * ROWS], score[:, 0, b, :], m.ident[0:ROWS, 0:ROWS])
                ins.then_inc(s.in_cols, 1)

            @block.scalar
            def _(act):
                act.wait_ge(s.exp_ask, 1)
                act.activation(score[:], score[:], ACT.Exp).then_inc(s.exp_done, 1)

            @block.vector
            def _(dve):
                link = Chain(dve, s.dve_chain)
                dve.wait_ge(s.in_rows, 1)
                dve.tensor_copy(q[:].rearrange("r o b e -> r (o b e)"), m.bank[2][0:ROWS, 0:BLOCKS * P])
                link(dve.tensor_tensor(run[:, 0], m.bank[2][0:ROWS, BLOCKS * P:2 * BLOCKS * P].rearrange("r (b e) -> r b e", b=BLOCKS),
                                       m.last[:], ALU.mult))
                link(dve.tensor_scalar(k[:, 0], m.last[:], -LOW, LOW, ALU.mult, ALU.add))
                link(dve.tensor_tensor(k[:], run[:], k[:], ALU.add))
                scan_rows(dve, link, m, s, w, k[:], spread[:], 1, 0, "back")
                link(dve.tensor_tensor(score[:], q[:], spread[:], ALU.add))
                link(dve.tensor_scalar(score[:], score[:], m.qk_bias[0:ROWS, :], None, ALU.add))
                link(dve.scalar_tensor_tensor(score[:], score[:], 0.2, score[:], ALU.mult, ALU.max))

                def exp():
                    dve.sem_inc(s.exp_ask, 1)
                    dve.wait_ge(s.exp_done, 1)
                softmax_rows(dve, link, exp, m, s, w, score[:], run[:], spread[:], 1, 1)
                link(dve.reciprocal(spread[:], spread[:]))
                dve.tensor_tensor(score[:], score[:], spread[:], ALU.mult).then_inc(s.weights_done, 1)
                dve.wait_ge(s.in_cols, 1)
                dve.tensor_copy(m.attn2[:], m.bank[2][:, 0:TILES])


def select(dve, m, s, key, same, cont, k, weight=None):
    dve.wait_ge(s.key_in[k.slot], 16 * (k.turn + 1))
    wait(dve, s.agg_done, k.t - (RING - 1))
    dve.tensor_scalar(cont[:, k.slot, :], key[:, k.slot, 1:P + 1], key[:, k.slot, 0:1], None, ALU.is_equal)
    if weight is None:
        ins = dve.tensor_scalar(same[:, k.slot, :], key[:, k.slot, 1:P + 1], col(m.dst, k.t), None, ALU.is_equal)
    else:
        ins = dve.tensor_scalar(same[:, k.slot, :], key[:, k.slot, 1:P + 1], col(m.dst, k.t), col(weight, k.t),
                                ALU.is_equal, ALU.mult)
    ins.then_inc(s.sel_done, 1)


def carry_over(dve, s, aggT, cont, p_agg, k, chunks, user_done):
    dve.wait_ge(s.agg_done, k.t + 1)
    wait(dve, user_done, k.t - 1)
    dve.wait_ge(s.sel_done, k.t + 1)
    wait(dve, s.carry_done, k.t)
    for c in range(chunks):
        ins = dve.scalar_tensor_tensor(aggT[:, k.pair, c, :], cont[:, k.slot, :], aggT[:, 1 - k.pair, c, P - 1:P],
                                       p_agg[k.pair][:, c * P:(c + 1) * P], ALU.mult, ALU.add)
    ins.then_inc(s.carry_done, 1)


def gat_sum(nc, d, m):
    names = ["sel_done", "weigh_done", "agg_done", "carry_done", "sum_done", "y_done", "zero_done", "k_done"] + NORM_SEMS
    ctx, s = phase(nc, "gat_sum", names, ["key_in", "h_in", "own_in", "state_out"])
    with ctx:
        def sb(name, shape, dt=F32):
            return ctx.enter_context(nc.sbuf_tensor("gc_" + name, shape, dt))
        key, same, cont = sb("key", [P, RING, P + 1]), sb("same", [P, RING, P]), sb("cont", [P, RING, P])
        h, own, msg = sb("h", [P, RING, FEAT]), sb("own", [P, RING, FEAT]), sb("msg", [P, 2, FEAT])
        aggT, junk = sb("aggT", [P, 2, FC, P]), sb("junk", [P, 2, FEAT])
        y, rows = sb("y", [P, RING, FEAT]), sb("rows", [P, RING, FEAT])
        v = norm_space(sb)
        p_agg, p_y = m.bank[0:2], m.bank[2:4]

        with nc.Block() as block:
            @block.sync
            def _(sp):
                def step(g, u):
                    if k := tile_at(g, u, 0):
                        load_key(sp, m, s, key, k)
                        hold(sp, s.weigh_done, k.t - (RING - 1))
                        sp.dma_start(h[:, k.slot, :], tile_rows(m.h_src, k.t)).then_inc(s.h_in[k.slot], 16)
                        hold(sp, s.sum_done, k.t - (RING - 1))
                        sp.dma_start(own[:, k.slot, :], tile_rows(m.state[1], k.t)).then_inc(s.own_in[k.slot], 16)
                    if k := tile_at(g, u, 11):
                        hold(sp, s.rows_done, k.t + 1)
                        sp.dma_start(tile_rows(m.state[2], k.t), rows[:, k.slot, :]).then_inc(s.state_out[k.slot], 16)
                run_steps(sp, step, 11)
                for slot in range(RING):
                    sp.wait_ge(s.state_out[slot], 16 * (TILES // RING))

            @block.gpsimd
            def _(pool):
                def step(g, u):
                    if k := tile_at(g, u, 2):
                        hold(pool, s.h_in[k.slot], 16 * (k.turn + 1))
                        hold(pool, s.agg_done, k.t - 1)
                        attn = m.score[:, k.t, :] if isinstance(k.t, int) else \
                            m.score[:, bass.ds(k.t, 1), :].rearrange("p o h -> p (o h)")
                        pool.tensor_tensor(msg[:, k.pair, :].rearrange("p (h d) -> p h d", h=HEADS),
                                           h[:, k.slot, :].rearrange("p (h d) -> p h d", h=HEADS),
                                           attn.unsqueeze(2).to_broadcast([P, HEADS, HEAD_DIM]), ALU.mult)\
                            .then_inc(s.weigh_done, 1)
                run_steps(pool, step, 2)

            @block.scalar
            def _(act):
                def step(g, u):
                    if k := tile_at(g, u, 10):
                        wait(act, s.state_out[k.slot], 16 * k.turn)
                        wait(act, s.k_done, k.t - (RING - 1))
                        norm_rows(act, s, v, rows[:, k.slot, :], y[:, k.slot, :], k)
                    if k := tile_at(g, u, 8):
                        norm_root(act, m, s, v, k)
                    if k := tile_at(g, u, 6):
                        act.wait_ge(s.sum_done, k.t + 1)
                        act.copy(y[:, k.slot, :], p_y[k.pair][:, 0:FEAT]).then_inc(s.y_done, 1)
                run_steps(act, step, 10)

            @block.tensor
            def _(pe):
                def step(g, u):
                    if k := tile_at(g, u, 5):
                        wait(pe, s.y_done, k.t - 1)
                        pe.matmul(p_y[k.pair][:, 0:FEAT], m.ones3[:], m.bias_parts[:], start=True, stop=False)
                        pe.wait_ge(s.own_in[k.slot], 16 * (k.turn + 1))
                        pe.matmul(p_y[k.pair][:, 0:FEAT], m.ident[:], own[:, k.slot, :], start=False, stop=False)
                        pe.wait_ge(s.carry_done, k.t + 1)
                        for c in range(FC):
                            ins = pe.matmul(p_y[k.pair][:, c * P:(c + 1) * P], aggT[:, k.pair, c, :], m.ident[:],
                                            start=False, stop=c == FC - 1)
                        ins.then_inc(s.sum_done, 1)
                    if k := tile_at(g, u, 3):
                        pe.wait_ge(s.weigh_done, k.t + 1)
                        pe.wait_ge(s.sel_done, k.t + 1)
                        wait(pe, s.carry_done, k.t - 1)
                        for c in range(FC):
                            ins = pe.matmul(p_agg[k.pair][:, c * P:(c + 1) * P], msg[:, k.pair, c * P:(c + 1) * P],
                                            same[:, k.slot, :], start=True, stop=True)
                        ins.then_inc(s.agg_done, 1)
                run_steps(pe, step, 5)

            @block.vector
            def _(dve):
                dve.memset(aggT[:, 1, :, P - 1], 0.0).then_inc(s.zero_done, 1)
                dve.wait_ge(s.zero_done, 1)

                def step(g, u):
                    if k := tile_at(g, u, 11):
                        wait(dve, s.k_done, k.t - 1)
                        dve.wait_ge(s.rows_done, k.t + 1)
                        dve.scalar_tensor_tensor(junk[:, k.pair, :], rows[:, k.slot, :], 1.0, m.k_row[:], ALU.mult, ALU.mult,
                                                 accum_out=col(m.k_dst, k.t)).then_inc(s.k_done, 1)
                    if k := tile_at(g, u, 9):
                        norm_recip(dve, s, v, k)
                        norm_shift(dve, s, v, k)
                    if k := tile_at(g, u, 4):
                        carry_over(dve, s, aggT, cont, p_agg, k, FC, s.sum_done)
                    if k := tile_at(g, u, 7):
                        dve.wait_ge(s.y_done, k.t + 1)
                        norm_stats(dve, s, v, y[:, k.slot, :], k)
                        norm_aggregate(dve, s, v, k)
                    if k := tile_at(g, u, 2):
                        select(dve, m, s, key, same, cont, k)
                run_steps(dve, step, 11)


def load_sources(sp, m, s, xs, free, k):
    hold(sp, free, k.t - (RING - 1))
    sp.dma_start(xs[:, k.slot, :], tile_rows(m.x_src, k.t)).then_inc(s.x_in[k.slot], 16)


def overlay(pool, m, s, xs, idx, table, k):
    hold(pool, s.src_in[k.slot], 16 * k.turn)
    pool.tensor_copy(idx[:, k.slot:k.slot + 1], m.idx_l1[:, k.t:k.t + 1, 0] if isinstance(k.t, int) else
                     m.idx_l1[:, bass.ds(k.t, 1), 0]).then_inc(s.idx_staged, 1)
    hold(pool, s.idx_staged, k.t + 1)
    hold(pool, s.x_in[k.slot], 16 * (k.turn + 1))
    gather_pos(pool, m, s, k, xs[:, k.slot, :], table, idx[:, k.slot:k.slot + 1], s.src_in[k.slot])


def scalar_scores(nc, d, m):
    ctx, s = phase(nc, "scalar_scores", ["idx_staged", "scaled", "x2_done", "q_done"], ["x_in", "src_in", "x2_out"])
    with ctx:
        def sb(name, shape, dt=F32):
            return ctx.enter_context(nc.sbuf_tensor("ss_" + name, shape, dt))
        idx, xs = sb("idx", [P, RING], I32), sb("xs", [P, RING, FEAT])
        ax, x2, junk = sb("ax", [P, 2, FEAT]), sb("x2", [P, RING, FEAT]), sb("junk", [P, 2, FEAT])
        alpha, beta, gamma = (m.affine[:, 0, j, :] for j in range(3))
        with nc.Block() as block:
            @block.sync
            def _(sp):
                def step(g, u):
                    if k := tile_at(g, u, 0):
                        load_sources(sp, m, s, xs, s.scaled, k)
                    if k := tile_at(g, u, 5):
                        hold(sp, s.x2_done, k.t + 1)
                        sp.dma_start(tile_rows(m.x2_src, k.t), x2[:, k.slot, :]).then_inc(s.x2_out[k.slot], 16)
                run_steps(sp, step, 5)
                for slot in range(RING):
                    sp.wait_ge(s.x2_out[slot], 16 * (TILES // RING))

            @block.gpsimd
            def _(pool):
                def step(g, u):
                    if k := tile_at(g, u, 0):
                        overlay(pool, m, s, xs, idx, m.state[2], k)
                run_steps(pool, step, 0)

            @block.scalar
            def _(act):
                def step(g, u):
                    if k := tile_at(g, u, 3):
                        act.wait_ge(s.src_in[k.slot], 16 * (k.turn + 1))
                        wait(act, s.x2_done, k.t - 1)
                        act.activation(ax[:, k.pair, :], xs[:, k.slot, :], ACT.Identity, bias=col(gamma, k.t),
                                       scale=col(alpha, k.t)).then_inc(s.scaled, 1)
                run_steps(act, step, 3)

            @block.vector
            def _(dve):
                def step(g, u):
                    if k := tile_at(g, u, 4):
                        wait(dve, s.x2_out[k.slot], 16 * k.turn)
                        dve.wait_ge(s.scaled, k.t + 1)
                        dve.scalar_tensor_tensor(x2[:, k.slot, :], m.bias[:], col(beta, k.t), ax[:, k.pair, :],
                                                 ALU.mult, ALU.add).then_inc(s.x2_done, 1)
                        wait(dve, s.q_done, k.t - 1)
                        dve.wait_ge(s.x2_done, k.t + 1)
                        dve.scalar_tensor_tensor(junk[:, k.pair, :], x2[:, k.slot, :], 1.0, m.q_row[:], ALU.mult, ALU.mult,
                                                 accum_out=col(m.q_src, k.t)).then_inc(s.q_done, 1)
                run_steps(dve, step, 4)


def scalar_sum(nc, d, m):
    names = ["sel_done", "agg_done", "carry_done", "sum_done", "y_done", "zero_done", "scaled", "res_done"] + NORM_SEMS
    ctx, s = phase(nc, "scalar_sum", names, ["key_in", "x_in", "own_in", "state_out", "res_out"])
    with ctx:
        def sb(name, shape, dt=F32):
            return ctx.enter_context(nc.sbuf_tensor("sc_" + name, shape, dt))
        key, same, cont = sb("key", [P, RING, P + 1]), sb("same", [P, RING, P]), sb("cont", [P, RING, P])
        xs, own = sb("xs", [P, RING, FEAT]), sb("own", [P, RING, FEAT])
        aggT, y, rows = sb("aggT", [P, 2, FC, P]), sb("y", [P, RING, FEAT]), sb("rows", [P, RING, FEAT])
        z, res = sb("z", [P, RING, FEAT]), sb("res", [P, RING, FEAT])
        v = norm_space(sb)
        p_agg, p_y = m.bank[0:2], m.bank[2:4]

        with nc.Block() as block:
            @block.sync
            def _(sp):
                def step(g, u):
                    if k := tile_at(g, u, 0):
                        load_key(sp, m, s, key, k)
                        hold(sp, s.agg_done, k.t - (RING - 1))
                        sp.dma_start(xs[:, k.slot, :], tile_rows(m.x2_src, k.t)).then_inc(s.x_in[k.slot], 16)
                        hold(sp, s.sum_done, k.t - (RING - 1))
                        sp.dma_start(own[:, k.slot, :], tile_rows(m.state[2], k.t)).then_inc(s.own_in[k.slot], 16)
                    if k := tile_at(g, u, 12):
                        hold(sp, s.scaled, k.t + 1)
                        sp.dma_start(tile_rows(m.state[3], k.t), z[:, k.slot, :]).then_inc(s.state_out[k.slot], 16)
                        hold(sp, s.res_done, k.t + 1)
                        sp.dma_start(tile_rows(m.res3, k.t), res[:, k.slot, :]).then_inc(s.res_out[k.slot], 16)
                run_steps(sp, step, 12)
                for slot in range(RING):
                    sp.wait_ge(s.state_out[slot], 16 * (TILES // RING))
                    sp.wait_ge(s.res_out[slot], 16 * (TILES // RING))

            @block.gpsimd
            def _(pool):
                def step(g, u):
                    if k := tile_at(g, u, 11):
                        hold(pool, s.rows_done, k.t + 1)
                        hold(pool, s.res_out[k.slot], 16 * k.turn)
                        pool.tensor_tensor(res[:, k.slot, :], rows[:, k.slot, :], m.res_bias[:], ALU.add).then_inc(s.res_done, 1)
                run_steps(pool, step, 11)

            @block.scalar
            def _(act):
                def step(g, u):
                    if k := tile_at(g, u, 11):
                        wait(act, s.state_out[k.slot], 16 * k.turn)
                        act.wait_ge(s.rows_done, k.t + 1)
                        act.activation(z[:, k.slot, :], rows[:, k.slot, :], ACT.Copy, scale=col(m.dinv, k.t)).then_inc(s.scaled, 1)
                    if k := tile_at(g, u, 10):
                        wait(act, s.res_done, k.t - (RING - 1))
                        wait(act, s.scaled, k.t - (RING - 1))
                        norm_rows(act, s, v, rows[:, k.slot, :], y[:, k.slot, :], k)
                    if k := tile_at(g, u, 8):
                        norm_root(act, m, s, v, k)
                    if k := tile_at(g, u, 6):
                        act.wait_ge(s.sum_done, k.t + 1)
                        act.copy(y[:, k.slot, :], p_y[k.pair][:, 0:FEAT]).then_inc(s.y_done, 1)
                run_steps(act, step, 11)

            @block.tensor
            def _(pe):
                def step(g, u):
                    if k := tile_at(g, u, 5):
                        wait(pe, s.y_done, k.t - 1)
                        pe.matmul(p_y[k.pair][:, 0:FEAT], m.ones3[:], m.bv_parts[:], start=True, stop=False)
                        pe.wait_ge(s.own_in[k.slot], 16 * (k.turn + 1))
                        pe.matmul(p_y[k.pair][:, 0:FEAT], m.ident[:], own[:, k.slot, :], start=False, stop=False)
                        pe.wait_ge(s.carry_done, k.t + 1)
                        for c in range(FC):
                            ins = pe.matmul(p_y[k.pair][:, 0:FEAT], aggT[:, k.pair, c, :], m.wv[:, c, :],
                                            start=False, stop=c == FC - 1)
                        ins.then_inc(s.sum_done, 1)
                    if k := tile_at(g, u, 3):
                        pe.wait_ge(s.x_in[k.slot], 16 * (k.turn + 1))
                        pe.wait_ge(s.sel_done, k.t + 1)
                        wait(pe, s.carry_done, k.t - 1)
                        for c in range(FC):
                            ins = pe.matmul(p_agg[k.pair][:, c * P:(c + 1) * P], xs[:, k.slot, c * P:(c + 1) * P],
                                            same[:, k.slot, :], start=True, stop=True)
                        ins.then_inc(s.agg_done, 1)
                run_steps(pe, step, 5)

            @block.vector
            def _(dve):
                dve.memset(aggT[:, 1, :, P - 1], 0.0).then_inc(s.zero_done, 1)
                dve.wait_ge(s.zero_done, 1)

                def step(g, u):
                    if k := tile_at(g, u, 9):
                        norm_recip(dve, s, v, k)
                        norm_shift(dve, s, v, k)
                    if k := tile_at(g, u, 4):
                        carry_over(dve, s, aggT, cont, p_agg, k, FC, s.sum_done)
                    if k := tile_at(g, u, 7):
                        dve.wait_ge(s.y_done, k.t + 1)
                        norm_stats(dve, s, v, y[:, k.slot, :], k)
                        norm_aggregate(dve, s, v, k)
                    if k := tile_at(g, u, 2):
                        select(dve, m, s, key, same, cont, k, m.attn2)
                run_steps(dve, step, 9)


def gcn(nc, d, m, out):
    names = ["idx_staged", "scaled", "x3_done", "sel_done", "agg_done", "carry_done", "total_done", "proj_done", "y_done",
             "zero_done", "out_staged"] + NORM_SEMS
    ctx, s = phase(nc, "gcn", names, ["key_in", "x_in", "src_in", "own_in", "res_in", "out_done"])
    with ctx:
        def sb(name, shape, dt=F32):
            return ctx.enter_context(nc.sbuf_tensor("gn_" + name, shape, dt))
        idx, out_idx = sb("idx", [P, RING], I32), sb("out_idx", [P, RING], I32)
        key, same, cont = sb("key", [P, RING, P + 1]), sb("same", [P, RING, P]), sb("cont", [P, RING, P])
        xs, own, res = sb("xs", [P, RING, FEAT]), sb("own", [P, RING, FEAT]), sb("res", [P, RING, FEAT])
        ax, x3 = sb("ax", [P, 2, FEAT]), sb("x3", [P, 2, FEAT])
        aggT, totT = sb("aggT", [P, 2, FC, P]), sb("totT", [P, 2, FC, P])
        y, rows = sb("y", [P, RING, FEAT]), sb("rows", [P, RING, FEAT])
        v = norm_space(sb)
        p_agg, p_out = m.bank[0:2], m.bank[2:4]
        alpha, beta, gamma = (m.affine[:, 1, j, :] for j in range(3))

        with nc.Block() as block:
            @block.sync
            def _(sp):
                def step(g, u):
                    if k := tile_at(g, u, 0):
                        load_sources(sp, m, s, xs, s.scaled, k)
                        load_key(sp, m, s, key, k)
                        hold(sp, s.agg_done, k.t - (RING - 1))
                        sp.dma_start(own[:, k.slot, :], tile_rows(m.state[3], k.t)).then_inc(s.own_in[k.slot], 16)
                    if k := tile_at(g, u, 2):
                        hold(sp, s.y_done, k.t - (RING - 1))
                        sp.dma_start(res[:, k.slot, :], tile_rows(m.res3, k.t)).then_inc(s.res_in[k.slot], 16)
                run_steps(sp, step, 2)

            @block.gpsimd
            def _(pool):
                def step(g, u):
                    if k := tile_at(g, u, 0):
                        overlay(pool, m, s, xs, idx, m.state[3], k)
                    if k := tile_at(g, u, 12):
                        hold(pool, s.out_done[k.slot], 16 * k.turn)
                        pool.tensor_copy(out_idx[:, k.slot:k.slot + 1], col(m.map_idx, k.t)).then_inc(s.out_staged, 1)
                        hold(pool, s.out_staged, k.t + 1)
                        hold(pool, s.rows_done, k.t + 1)
                        pool.indirect_dma_start(out, bass.IndirectOffsetOnAxis(ap=out_idx[:, k.slot:k.slot + 1], axis=0),
                                                rows[:, k.slot, :], None, bounds_check=NODES - 1, oob_is_err=False)\
                            .then_inc(s.out_done[k.slot], 16)
                run_steps(pool, step, 12)
                for slot in range(RING):
                    pool.wait_ge(s.out_done[slot], 16 * (TILES // RING))

            @block.scalar
            def _(act):
                def step(g, u):
                    if k := tile_at(g, u, 10):
                        norm_root(act, m, s, v, k)
                    if k := tile_at(g, u, 3):
                        act.wait_ge(s.src_in[k.slot], 16 * (k.turn + 1))
                        wait(act, s.x3_done, k.t - 1)
                        act.activation(ax[:, k.pair, :], xs[:, k.slot, :], ACT.Identity, bias=col(gamma, k.t),
                                       scale=col(alpha, k.t)).then_inc(s.scaled, 1)
                    if k := tile_at(g, u, 11):
                        wait(act, s.out_done[k.slot], 16 * k.turn)
                        norm_rows(act, s, v, rows[:, k.slot, :], y[:, k.slot, :], k)
                run_steps(act, step, 11)

            @block.tensor
            def _(pe):
                def step(g, u):
                    if k := tile_at(g, u, 7):
                        pe.wait_ge(s.total_done, k.t + 1)
                        wait(pe, s.y_done, k.t - 1)
                        for c in range(FC):
                            ins = pe.matmul(p_out[k.pair][:, 0:FEAT], totT[:, k.pair, c, :], m.w_gcn[:, c, :],
                                            start=c == 0, stop=c == FC - 1)
                        ins.then_inc(s.proj_done, 1)
                    if k := tile_at(g, u, 5):
                        pe.wait_ge(s.own_in[k.slot], 16 * (k.turn + 1))
                        wait(pe, s.total_done, k.t - 1)
                        for c in range(FC):
                            pe.transpose(p_agg[k.pair][:, FEAT + c * P:FEAT + (c + 1) * P],
                                         own[:, k.slot, c * P:(c + 1) * P], m.ident[:])
                        pe.wait_ge(s.x3_done, k.t + 1)
                        pe.wait_ge(s.sel_done, k.t + 1)
                        for c in range(FC):
                            ins = pe.matmul(p_agg[k.pair][:, c * P:(c + 1) * P], x3[:, k.pair, c * P:(c + 1) * P],
                                            same[:, k.slot, :], start=True, stop=True)
                        ins.then_inc(s.agg_done, 1)
                run_steps(pe, step, 7)

            @block.vector
            def _(dve):
                dve.memset(aggT[:, 1, :, P - 1], 0.0).then_inc(s.zero_done, 1)
                dve.wait_ge(s.zero_done, 1)

                def step(g, u):
                    if k := tile_at(g, u, 8):
                        dve.wait_ge(s.proj_done, k.t + 1)
                        dve.wait_ge(s.res_in[k.slot], 16 * (k.turn + 1))
                        wait(dve, s.rows_done, k.t - (RING - 1))
                        dve.scalar_tensor_tensor(y[:, k.slot, :], p_out[k.pair][:, 0:FEAT], col(m.dinv, k.t),
                                                 res[:, k.slot, :], ALU.mult, ALU.add).then_inc(s.y_done, 1)
                    if k := tile_at(g, u, 6):
                        carry_over(dve, s, aggT, cont, p_agg, k, FC, s.total_done)
                    if k := tile_at(g, u, 9):
                        dve.wait_ge(s.y_done, k.t + 1)
                        norm_stats(dve, s, v, y[:, k.slot, :], k)
                        norm_aggregate(dve, s, v, k)
                    if k := tile_at(g, u, 6):
                        dve.wait_ge(s.carry_done, k.t + 1)
                        wait(dve, s.proj_done, k.t - 1)
                        dve.tensor_tensor(totT[:, k.pair, :, :], aggT[:, k.pair, :, :],
                                          p_agg[k.pair][:, FEAT:2 * FEAT].rearrange("p (c n) -> p c n", c=FC), ALU.add)\
                           .then_inc(s.total_done, 1)
                    if k := tile_at(g, u, 4):
                        select(dve, m, s, key, same, cont, k)
                        dve.wait_ge(s.scaled, k.t + 1)
                        wait(dve, s.agg_done, k.t - 1)
                        dve.scalar_tensor_tensor(x3[:, k.pair, :], m.bias[:], col(beta, k.t), ax[:, k.pair, :],
                                                 ALU.mult, ALU.add).then_inc(s.x3_done, 1)
                    if k := tile_at(g, u, 10):
                        norm_recip(dve, s, v, k)
                        norm_shift(dve, s, v, k)
                run_steps(dve, step, 10)


_OUTS = [((NODES, FEAT), "float32")]


def kernel(x, src, dst, edge_attr_3, L0_gnn_W1, L0_gnn_b1, L0_gnn_W2, L0_gnn_b2, L1_gnn_W, L1_gnn_a_src,
           L1_gnn_a_dst, L1_gnn_edge_W, L1_gnn_edge_b, L1_gnn_bias, L2_gnn_Wv, L2_gnn_bv, L2_gnn_wq, L2_gnn_bq,
           L2_gnn_wk, L2_gnn_bk, L3_gnn_W_conv, L3_gnn_b_conv, L3_gnn_W_lin, L3_gnn_b_lin):
    import numpy as np
    import concourse.bacc as bacc
    from concourse.bass_utils import run_bass_kernel_spmd

    c = np.ascontiguousarray
    x, src, dst, edge_attr_3 = (np.asarray(a) for a in (x, src, dst, edge_attr_3))
    pad = EPAD - EDGES
    heads = np.arange(FEAT)[:, None] // HEAD_DIM == np.arange(HEADS)[None, :]
    arrays = {
        "x": c(x),
        "dst_pad": np.concatenate([np.full(1, -1, np.int32), dst, np.full(pad, NODES, np.int32),
                                   np.full(1, NODES + 1, np.int32)]),
        "src_pad": np.concatenate([src, np.zeros(pad, np.int32)]),
        "edge_attr_T": c(np.concatenate([edge_attr_3, np.zeros((pad, EDGE_FEAT), np.float32)]).T),
        "head_mask": heads.astype(np.float32),
        "L0_W1": c(L0_gnn_W1), "L0_b1": c(L0_gnn_b1), "L0_W2": c(L0_gnn_W2), "L0_b2": c(L0_gnn_b2),
        "L1_W": c(L1_gnn_W), "L1_WT": c(np.asarray(L1_gnn_W).T), "L1_a_src": c(L1_gnn_a_src).reshape(FEAT, 1),
        "L1_a_dst": c(L1_gnn_a_dst).reshape(FEAT, 1), "L1_eWT": c(np.asarray(L1_gnn_edge_W).T),
        "L1_eb": c(L1_gnn_edge_b), "L1_bias": c(L1_gnn_bias),
        "L2_Wv": c(L2_gnn_Wv), "L2_WvT": c(np.asarray(L2_gnn_Wv).T), "L2_bv": c(L2_gnn_bv),
        "L2_wq": c(L2_gnn_wq).reshape(FEAT, 1), "L2_wk": c(L2_gnn_wk).reshape(FEAT, 1),
        "L2_bq": c(L2_gnn_bq).reshape(1), "L2_bk": c(L2_gnn_bk).reshape(1),
        "L3_WcT": c(np.asarray(L3_gnn_W_conv).T), "L3_bc": c(L3_gnn_b_conv).reshape(GCN_HIDDEN, 1),
        "L3_Wl": c(L3_gnn_W_lin), "L3_bl": c(L3_gnn_b_lin),
    }
    arrays = {n: np.asarray(a) for n, a in arrays.items()}
    nc = bacc.Bacc("TRN2", target_bir_lowering=False, num_devices=1)
    d = namedtuple("Inputs", list(arrays))(*(nc.dram_tensor(n, a.shape, mybir.dt.from_np(a.dtype), kind="ExternalInput").ap()
                                             for n, a in arrays.items()))
    (shape, dtype), = _OUTS
    out = nc.dram_tensor("out", shape, mybir.dt.from_np(np.dtype(dtype)), kind="ExternalOutput").ap()
    build(nc, d, out)
    r = run_bass_kernel_spmd(nc, [arrays], core_ids=[0])
    return r.results[0]["out"]
```

```python
from collections import namedtuple
from contextlib import ExitStack

import concourse.bass as bass
from concourse import mybir

F32 = mybir.dt.float32
F32R = mybir.dt.float32r
BF16 = mybir.dt.bfloat16
I32 = mybir.dt.int32
ALU = mybir.AluOpType
ACT = mybir.ActivationFunctionType
AX = mybir.AxisListType

P = 128
NODES = 50000
EDGES = 25000
FEAT = 256
HIDDEN = 512
HEADS = 8
HEAD_DIM = FEAT // HEADS
EDGE_FEAT = 3
WIDE = FEAT + HEADS
GCN_HIDDEN = 128
FC = FEAT // P
HC = HIDDEN // P
RING = 7
UNROLL = 2 * RING
TILES = -(-EDGES // (P * UNROLL)) * UNROLL
EPAD = TILES * P
BLOCKS = 2
ROWS = TILES // BLOCKS
MAP_COLS = -(-NODES // P)
PLAIN_COLS = NODES // P
TAIL = NODES - PLAIN_COLS * P
BATCH = 15
PIECE = 5
LOOKUPS = 5
Y_BANKS = 5
AFFINE_LINKS = (8, 4, 1)
NOWHERE = 1 << 20
LOW = -1.0e30
EPS = 1e-5

Tile = namedtuple("Tile", "t slot pair turn body_slot body")
ScanSpace = namedtuple("ScanSpace", "total between carry")


class Memory:
    pass


def tile_at(g, u, lag, unroll=UNROLL, tiles=TILES):
    v = u - lag
    t = g * unroll + v
    if isinstance(g, int) and not 0 <= t < tiles:
        return None
    return Tile(t, v % unroll % RING, v % unroll % 2, g * (unroll // RING) + v // RING, v % unroll, g + v // unroll)


def run_steps(eng, step, lag, unroll=UNROLL, tiles=TILES, peeled=None):
    bodies = tiles // unroll
    peeled = min(bodies, peeled or 1 + -(-lag // unroll))
    for j in range(peeled * unroll):
        step(j // unroll, j % unroll)
    if bodies > peeled:
        with eng.Fori(peeled, bodies) as g:
            for u in range(unroll):
                step(g, u)
    for u in range(lag):
        step(bodies + u // unroll, u % unroll)


def wait(eng, sem, value):
    if not (isinstance(value, int) and value <= 0):
        eng.wait_ge(sem, value)


def hold(eng, sem, value):
    if not (isinstance(value, int) and value <= 0):
        eng.wait_ge(sem, value)
        eng.nop(nofuse=True)


def col(ap, t, n=1):
    return ap[:, t:t + n] if isinstance(t, int) else ap[:, bass.ds(t, n)]


def tile_rows(ap, t):
    return ap[t * P:(t + 1) * P, :] if isinstance(t, int) else ap[bass.ds(t * P, P), :]


class Chain:

    def __init__(self, eng, sem, base=0):
        self.eng, self.sem, self.base, self.n = eng, sem, base, 0

    def __call__(self, ins):
        self.n += 1
        ins.then_inc(self.sem, 1)
        self.eng.wait_ge(self.sem, self.base + self.n)


def phase(nc, label, names, rings=(), more=()):
    taken = []

    def take(name):
        taken.append(nc.alloc_semaphore(f"{label}_{name}"))
        return taken[-1]

    def clear():
        nc.clear_and_free_semaphores(taken)
        nc.all_engine_barrier()
    ctx = ExitStack()
    ctx.callback(clear)
    sized = [(n, RING) for n in rings] + list(more)
    found = [take(n) for n in names] + [[take(f"{n}{i}") for i in range(size)] for n, size in sized]
    return ctx, namedtuple("Semaphores", list(names) + [n for n, _ in sized])(*found)


def build(nc, d, out):
    ctx = ExitStack()
    with ctx:
        def sb(name, shape, dt=F32):
            return ctx.enter_context(nc.sbuf_tensor(name, shape, dt))

        def dram(name, shape, dt=F32):
            return nc.dram_tensor(name, shape, dt).ap()

        bank = [ctx.enter_context(nc.psum_tensor(f"bank{i}", [P, 512], F32)) for i in range(8)]
        m = Memory()
        m.bank = bank
        m.dst_f = dram("dst_f", [EPAD + 2])
        m.node_map = dram("node_map", [MAP_COLS * P, 1], I32)
        m.x_src = dram("x_src", [EPAD, FEAT])
        m.h_src = dram("h_src", [EPAD, FEAT])
        m.x2_src = dram("x2_src", [EPAD, FEAT])
        m.state = [None] + [dram(f"state{i}", [EPAD, FEAT]) for i in (1, 2, 3)]
        m.res3 = dram("res3", [EPAD, FEAT])
        m.ident = sb("ident", [P, P])
        m.eps = sb("eps", [P, 1])
        m.dst = sb("dst_col", [P, TILES])
        m.idx_l0 = sb("idx_l0", [P, TILES, 2], I32)
        m.idx_l1 = sb("idx_l1", [P, TILES, 2], I32)
        m.map_idx = sb("map_idx", [P, TILES], I32)
        m.edge_id = sb("edge_id", [P, TILES], I32)
        m.indeg = sb("indeg", [P, TILES])
        m.rdeg = sb("rdeg", [P, TILES])
        m.sdeg = sb("sdeg", [P, TILES])
        m.dinv = sb("dinv", [P, TILES])
        m.dinv_end = sb("dinv_end", [P, TILES])
        m.keep = sb("keep", [ROWS, BLOCKS, P])
        m.pen_f = sb("pen_f", [ROWS, BLOCKS, P])
        m.pen_b = sb("pen_b", [ROWS, BLOCKS, P])
        m.last = sb("last_row", [ROWS, BLOCKS, P])
        m.open_row = sb("open_row", [HEADS, 3, TILES])
        m.row_stat = sb("row_stat", [P, 3, TILES])
        m.touched = sb("touched", [P, TILES])
        m.untouched = sb("untouched", [P, TILES])
        m.affine = sb("affine", [P, 2, 3, TILES])
        m.score = sb("score", [P, TILES, HEADS])
        m.q_src = sb("q_src", [P, TILES])
        m.k_dst = sb("k_dst", [P, TILES])
        m.attn2 = sb("attn2", [P, TILES])
        weights(nc, d, m, sb)
        structure(nc, d, m, ctx)
        edge_mlp(nc, d, m)
        untouched_nodes(nc, d, m, out, P, 0, PLAIN_COLS, 2 * BATCH, BATCH, PIECE)
        untouched_nodes(nc, d, m, out, TAIL, P * PLAIN_COLS, 1, 1, 1, 1)
        gat_scores(nc, d, m)
        gat_softmax(nc, m)
        gat_sum(nc, d, m)
        scalar_scores(nc, d, m)
        scalar_softmax(nc, m)
        scalar_sum(nc, d, m)
        gcn(nc, d, m, out)


def weights(nc, d, m, sb):
    m.w1, m.w2 = sb("w1", [P, 2, 2 * FC, HIDDEN], F32R), sb("w2", [P, 2, HC, FEAT], F32R)
    m.b1, m.ones3 = sb("b1_all", [P, HIDDEN]), sb("ones3", [3, P], BF16)
    m.res_parts, m.bias_parts, m.bv_parts = (sb(n, [3, FEAT], BF16) for n in ("res_parts", "bias_parts", "bv_parts"))
    m.w_src = sb("w_src", [P, FC, FEAT + HEADS])
    m.w_dst = sb("w_dst", [P, FC, FEAT + HEADS])
    m.w_enc = sb("w_enc", [EDGE_FEAT + 1, FEAT])
    m.wv = sb("wv", [P, FC, FEAT])
    m.w_gcn = sb("w_gcn", [P, FC, FEAT])
    m.w_res = sb("w_res", [P, FC, FEAT])
    rows = ("b2", "bias", "bv", "bl", "q_row", "k_row")
    m.b2, m.bias, m.bv, m.res_bias, m.q_row, m.k_row = (sb(n + "_all", [P, FEAT]) for n in rows)
    m.bias_mv, m.bias_var_eps, m.qk_bias = sb("bias_mv", [P, 2]), sb("bias_var_eps", [P, 1]), sb("qk_bias", [P, 1])
    names = ["ident_done", "load_done", "dve_chain", "parts_done", "parts_in", "masked", "prod_done"]
    ctx, s = phase(nc, "weights", names)
    with (ctx, nc.Block() as block):
        def tmp(name, shape, dt=F32):
            return ctx.enter_context(nc.sbuf_tensor("tmp_" + name, shape, dt))
        rest = tmp("rest", [1, FEAT])
        res_split, bias_split, bv_split = (tmp(n, [1, 3, FEAT], BF16) for n in ("res_split", "bias_split", "bv_split"))
        w1, w2 = tmp("w1", [P, 2 * FC, HIDDEN]), tmp("w2", [P, HC, FEAT])
        w_nat, mask, a_col = tmp("w_nat", [P, FC, FEAT]), tmp("mask", [P, FC, HEADS]), tmp("a_col", [P, 2, FC])
        masked = tmp("masked", [P, 2, FC, HEADS])
        wvT, qk_col, qk_all = tmp("wvT", [P, FC, FEAT]), tmp("qk_col", [P, 2, FC]), tmp("qk_all", [P, 2, FC, P])
        bv_col, bv_all, qk_sum, qk_b = tmp("bv_col", [P, FC]), tmp("bv_all", [P, FC, P]), tmp("qk_sum", [P, FC]), tmp("qk_b", [P, 2])
        wcT, wl, bc_col, bc_all = tmp("wcT", [P, FEAT]), tmp("wl", [P, FEAT]), tmp("bc_col", [P, 1]), tmp("bc_all", [P, P])
        stats = tmp("bias_stats", [P, 6])

        def chunks(ap):
            return ap.rearrange("(c p) n -> p c n", p=P)

        def column(ap):
            return ap.rearrange("(c p) o -> p (c o)", p=P)
        loads = [
            (w1[:], chunks(d.L0_W1)), (w2[:], chunks(d.L0_W2)), (m.b2[:], d.L0_b2.partition_broadcast(P)), (m.b1[:], d.L0_b1.partition_broadcast(P)),
            (m.w_src[:, :, 0:FEAT], chunks(d.L1_WT)), (m.w_dst[:, :, 0:FEAT], chunks(d.L1_WT)), (w_nat[:], chunks(d.L1_W)), (mask[:], chunks(d.head_mask)),
            (a_col[:, 0, :], column(d.L1_a_src)), (a_col[:, 1, :], column(d.L1_a_dst)),
            (m.w_enc[0:EDGE_FEAT, :], d.L1_eWT), (m.w_enc[EDGE_FEAT:EDGE_FEAT + 1, :], d.L1_eb.unsqueeze(0)),
            (m.bias[:], d.L1_bias.partition_broadcast(P)),
            (m.wv[:], chunks(d.L2_Wv)), (wvT[:], chunks(d.L2_WvT)), (m.bv[:], d.L2_bv.partition_broadcast(P)),
            (qk_col[:, 0, :], column(d.L2_wq)), (qk_col[:, 1, :], column(d.L2_wk)),
            (bv_col[:], column(d.L2_bv.unsqueeze(1))),
            (qk_b[:, 0:1], d.L2_bq.partition_broadcast(P)), (qk_b[:, 1:2], d.L2_bk.partition_broadcast(P)),
            (wcT[:], d.L3_WcT), (wl[:], d.L3_Wl), (bc_col[:], d.L3_bc), (m.res_bias[:], d.L3_bl.partition_broadcast(P)),
        ]

        @block.sync
        def _(sp):
            with nc.allow_non_contiguous_dma("columns of small vectors"):
                for to, frm in loads:
                    sp.dma_start(to, frm).then_inc(s.load_done, 16)
            sp.wait_ge(s.parts_done, 1)
            for to, parts in ((m.res_parts, res_split), (m.bias_parts, bias_split), (m.bv_parts, bv_split)):
                sp.dma_start(to[:], parts[:].rearrange("o k n -> o (k n)")).then_inc(s.parts_in, 16)
            sp.wait_ge(s.parts_in, 48)

        @block.gpsimd
        def _(pool):
            pool.memset(m.ident[:], 0.0).then_inc(s.ident_done, 1)
            pool.wait_ge(s.ident_done, 1)
            pool.affine_select(out=m.ident[:], in_=m.ident[:], compare_op=ALU.not_equal, fill=1.0,
                               base=0, pattern=[[-1, P]], channel_multiplier=1).then_inc(s.ident_done, 1)
            pool.memset(m.eps[:], EPS)
            pool.memset(m.ones3[:], 1.0)

        @block.tensor
        def _(pe):
            pe.wait_ge(s.masked, 1)
            for k in range(2):
                for c in range(FC):
                    at = (k * FC + c) * HEADS
                    for o in range(FC):
                        pe.matmul(m.bank[0][:, at:at + HEADS], w_nat[:, o, c * P:(c + 1) * P], masked[:, k, o, :],
                                  start=o == 0, stop=o == FC - 1)
            for k in range(2):
                for o in range(FC):
                    pe.matmul(m.bank[1][:, k * FEAT:(k + 1) * FEAT], qk_all[:, k, o, :], wvT[:, o, :],
                              start=o == 0, stop=o == FC - 1)
            for o in range(FC):
                pe.matmul(m.bank[2][:, 0:1], bv_all[:, o, :], qk_sum[:, o:o + 1], start=o == 0, stop=o == FC - 1)
            for c in range(FC):
                pe.matmul(m.bank[3][:, c * FEAT:(c + 1) * FEAT], wcT[:, c * P:(c + 1) * P], wl[:], start=True, stop=True)
            pe.matmul(m.bank[4][:, 0:FEAT], bc_all[:], wl[:], start=True, stop=True).then_inc(s.prod_done, 1)

        @block.vector
        def _(dve):
            link = Chain(dve, s.dve_chain)

            def split(row, parts, n):
                link(dve.tensor_copy(parts[:, 0, :], row))
                link(dve.tensor_tensor(rest[:, 0:n], row, parts[:, 0, :], ALU.subtract))
                link(dve.tensor_copy(parts[:, 1, :], rest[:, 0:n]))
                link(dve.tensor_tensor(rest[:, 0:n], rest[:, 0:n], parts[:, 1, :], ALU.subtract))
                return dve.tensor_copy(parts[:, 2, :], rest[:, 0:n])

            dve.wait_ge(s.load_done, 16 * len(loads))
            link(dve.tensor_tensor(w1[:, 0:FC, :], w1[:, 0:FC, :], w1[:, FC:2 * FC, :], ALU.subtract))
            dve.tensor_copy(m.w1[:, 0], w1[:])
            link(dve.tensor_copy(m.w2[:, 0], w2[:]))
            dve.tensor_tensor(m.w1[:, 1], w1[:], m.w1[:, 0].bitcast(F32), ALU.subtract)
            dve.tensor_tensor(m.w2[:, 1], w2[:], m.w2[:, 0].bitcast(F32), ALU.subtract)
            for k in range(2):
                for o in range(FC):
                    dve.tensor_scalar(masked[:, k, o, :], mask[:, o, :], a_col[:, k, o:o + 1], None, ALU.mult)
                    dve.tensor_copy(qk_all[:, k, o, :], qk_col[:, k, o:o + 1].to_broadcast([P, P]))
            for o in range(FC):
                dve.tensor_copy(bv_all[:, o, :], bv_col[:, o:o + 1].to_broadcast([P, P]))
            dve.tensor_tensor(qk_sum[:], qk_col[:, 0, :], qk_col[:, 1, :], ALU.add)
            link(dve.tensor_copy(bc_all[:], bc_col[:].to_broadcast([P, P])))
            dve.sem_inc(s.masked, 1)
            link(dve.bn_stats(stats[:], m.bias[:]))
            dve.nop(nofuse=True)
            link(dve.bn_aggr(m.bias_mv[:], stats[:]))
            dve.tensor_scalar(m.bias_var_eps[:], m.bias_mv[:, 1:2], EPS, None, ALU.add)
            link(split(m.bias[0:1, :], bias_split, FEAT))
            link(split(m.bv[0:1, :], bv_split, FEAT))
            dve.wait_ge(s.prod_done, 1)
            dve.wait_ge(s.ident_done, 2)
            dve.tensor_copy(m.w_src[:, :, FEAT:FEAT + HEADS],
                            m.bank[0][:, 0:FC * HEADS].rearrange("p (c h) -> p c h", c=FC))
            dve.tensor_copy(m.w_dst[:, :, FEAT:FEAT + HEADS],
                            m.bank[0][:, FC * HEADS:2 * FC * HEADS].rearrange("p (c h) -> p c h", c=FC))
            dve.tensor_copy(m.q_row[:], m.bank[1][:, 0:FEAT])
            dve.tensor_copy(m.k_row[:], m.bank[1][:, FEAT:2 * FEAT])
            dve.tensor_tensor(m.qk_bias[:], qk_b[:, 0:1], qk_b[:, 1:2], ALU.add)
            dve.tensor_copy(m.w_gcn[:], m.bank[3][:].rearrange("p (c n) -> p c n", c=FC))
            link(dve.tensor_tensor(m.res_bias[:], m.bank[4][:, 0:FEAT], m.res_bias[:], ALU.add))
            dve.tensor_tensor(m.qk_bias[:], m.bank[2][:, 0:1], m.qk_bias[:], ALU.add)
            link(dve.tensor_copy(m.w_res[:], m.w_gcn[:]))
            for c in range(FC):
                block_c = m.w_res[:, c, c * P:(c + 1) * P]
                dve.tensor_tensor(block_c, block_c, m.ident[:], ALU.add)
            split(m.res_bias[0:1, :], res_split, FEAT).then_inc(s.parts_done, 1)


def scan_rows(dve, link, m, s, w, vals, out, heads, n, kind):
    back = kind == "back"
    weight, op0, op1, start, which = {
        "max": (m.pen_f, ALU.add, ALU.max, LOW, 0), "sum": (m.keep, ALU.mult, ALU.add, 0.0, 1),
        "back": (m.pen_b, ALU.add, ALU.max, LOW, 2)}[kind]
    turn = slice(None, None, -1) if back else slice(None)

    def scans(initial):
        for h in range(heads):
            for b in range(BLOCKS):
                first = start if initial is None else initial[:, b, h:h + 1]
                ins = dve.tensor_tensor_scan(out[:, h, b, turn], weight[:, b, turn], vals[:, h, b, turn],
                                             first, op0, op1)
        return ins

    link(scans(None))
    dve.tensor_copy(w.total[:, :, 0:heads].rearrange("r b h -> r h b"),
                    out[:, :, :, 0 if back else P - 1]).then_inc(s.totals_ready, 1)
    link(dve.memset(w.between[0:heads, TILES if back else 0:TILES + 1 if back else 1], start))
    dve.wait_ge(s.totals_in_row, n + 1)
    tot = m.bank[0][0:heads, 0:TILES]
    opens = m.open_row[0:heads, which, :]
    if back:
        dve.tensor_tensor_scan(w.between[0:heads, 0:TILES][:, ::-1], opens[:, ::-1], tot[:, ::-1], start,
                               op0, op1).then_inc(s.between_ready, 1)
    else:
        dve.tensor_tensor_scan(w.between[0:heads, 1:TILES + 1], opens, tot, start,
                               op0, op1).then_inc(s.between_ready, 1)
    dve.wait_ge(s.carry_ready, n + 1)
    link(dve.tensor_copy(w.carry[:, :, 0:heads],
                         m.bank[1][0:ROWS, 0:BLOCKS * heads].rearrange("r (b h) -> r b h", b=BLOCKS)))
    link(scans(w.carry))


def scan_rows_pe(pe, m, s, w, heads, n, back):
    pe.wait_ge(s.totals_ready, n + 1)
    for b in range(BLOCKS):
        ins = pe.transpose(m.bank[0][0:heads, b * ROWS:(b + 1) * ROWS], w.total[:, b, 0:heads],
                           m.ident[0:ROWS, 0:ROWS])
    ins.then_inc(s.totals_in_row, 1)
    pe.wait_ge(s.between_ready, n + 1)
    for b in range(BLOCKS):
        at = b * ROWS + (1 if back else 0)
        ins = pe.transpose(m.bank[1][0:ROWS, b * heads:(b + 1) * heads], w.between[0:heads, at:at + ROWS],
                           m.ident[0:heads, 0:heads])
    ins.then_inc(s.carry_ready, 1)


SCAN_SEMS = ["totals_ready", "totals_in_row", "between_ready", "carry_ready"]


def structure(nc, d, m, outer):
    names = ["rows_in", "ids_ready", "dve_chain", "rows_out", "flags_ready", "opens_ready", "cols_ready",
             "cols_done", "map_ready", "map_in", "act_done", "deg_ready", "flat_in", "end_ready"] + SCAN_SEMS
    ctx, s = phase(nc, "structure", names)
    R = [ROWS, BLOCKS, P]
    with ctx:
        def sb(name, shape, dt=F32):
            return ctx.enter_context(nc.sbuf_tensor(name, shape, dt))
        dst_i, prev_i, next_i, src_i, id_i = (sb(n, R, I32) for n in ("dst_i", "prev_i", "next_i", "src_i", "id_i"))
        dst, prev, nxt, src, eid, first = (sb(n, R) for n in ("dst_r", "prev_r", "next_r", "src_r", "id_r", "first_r"))
        count, end = sb("count_r", [ROWS, 1, BLOCKS, P]), sb("end_r", [ROWS, 1, BLOCKS, P])
        ones = sb("ones_r", [ROWS, 1, BLOCKS, P])
        map_i = sb("map_r", R)
        opens = sb("opens_r", [ROWS, BLOCKS, 3, HEADS])
        flag = sb("flag_r", [ROWS, BLOCKS, 2])
        nowhere = sb("nowhere", [P, MAP_COLS], I32)
        gathered = sb("dst_gather", [P, TILES])
        w = ScanSpace(total=sb("total_s", [ROWS, BLOCKS, HEADS]), between=sb("between_s", [HEADS, TILES + 1]),
                            carry=sb("carry_s", [ROWS, BLOCKS, HEADS]))
        flat = [(dst_i, d.dst_pad, 1), (prev_i, d.dst_pad, 0), (next_i, d.dst_pad, 2), (src_i, d.src_pad, 0)]
        cols = [dst, src, map_i, eid, count[:, 0], end[:, 0]]

        with nc.Block() as block:
            @block.sync
            def _(sp):
                for to, frm, off in flat:
                    sp.dma_start(to[:], frm[off:off + EPAD].rearrange("(b r e) -> r b e", b=BLOCKS, e=P))\
                      .then_inc(s.rows_in, 16)
                sp.wait_ge(s.rows_out, 1)
                sp.dma_start(m.dst_f[1:1 + EPAD].rearrange("(b r e) -> r b e", b=BLOCKS, e=P), dst[:])\
                  .then_inc(s.flat_in, 16)
                sp.dma_start(m.dst_f[0:1].unsqueeze(0), prev[0:1, 0, 0:1]).then_inc(s.flat_in, 16)
                sp.wait_ge(s.map_ready, 1)
                sp.dma_start(m.node_map.rearrange("(p c) o -> p (c o)", p=P), nowhere[:]).then_inc(s.map_in, 16)
                sp.wait_ge(s.flat_in, 32)
                sp.wait_ge(s.map_in, 16)

            @block.gpsimd
            def _(pool):
                pool.iota(id_i[:], pattern=[[ROWS * P, BLOCKS], [1, P]], base=0, channel_multiplier=P)\
                    .then_inc(s.ids_ready, 1)
                pool.memset(nowhere[:], NOWHERE).then_inc(s.map_ready, 1)

            @block.scalar
            def _(act):
                act.wait_ge(s.deg_ready, 1)
                act.activation(m.sdeg[:], m.sdeg[:], ACT.Sqrt).then_inc(s.act_done, 1)

            @block.vector
            def _(dve):
                link = Chain(dve, s.dve_chain)
                dve.wait_ge(s.rows_in, 16 * len(flat))
                dve.wait_ge(s.ids_ready, 1)
                for to, frm in ((dst, dst_i), (prev, prev_i), (nxt, next_i), (src, src_i), (eid, id_i)):
                    ins = dve.tensor_copy(to[:], frm[:])
                link(ins)
                dve.sem_inc(s.rows_out, 1)
                dve.tensor_tensor(m.keep[:], dst[:], prev[:], ALU.is_equal)
                dve.tensor_tensor(first[:], dst[:], prev[:], ALU.not_equal)
                link(dve.tensor_tensor(m.last[:], dst[:], nxt[:], ALU.not_equal))
                dve.tensor_scalar(m.pen_f[:], first[:], LOW, None, ALU.mult)
                dve.tensor_scalar(m.pen_b[:], m.last[:], LOW, None, ALU.mult)
                dve.tensor_scalar(map_i[:], m.last[:], -float(NOWHERE), float(NOWHERE), ALU.mult, ALU.add)
                dve.tensor_reduce(flag[:, :, 0:1], first[:], AX.X, ALU.max)
                link(dve.tensor_reduce(flag[:, :, 1:2], m.last[:], AX.X, ALU.max))
                dve.tensor_tensor(map_i[:], map_i[:], dst[:], ALU.add)
                for h in range(HEADS):
                    dve.tensor_scalar(opens[:, :, 0, h:h + 1], flag[:, :, 0:1], LOW, None, ALU.mult)
                    dve.tensor_scalar(opens[:, :, 1, h:h + 1], flag[:, :, 0:1], -1.0, 1.0, ALU.mult, ALU.add)
                    ins = dve.tensor_scalar(opens[:, :, 2, h:h + 1], flag[:, :, 1:2], LOW, None, ALU.mult)
                ins.then_inc(s.flags_ready, 1)
                link(dve.memset(ones[:], 1.0))
                dve.wait_ge(s.opens_ready, 1)
                link(dve.tensor_copy(m.open_row[:, 0:2, :], m.bank[2][0:HEADS, 0:2 * TILES].rearrange("h (k t) -> h k t", k=2)))
                link(dve.tensor_copy(m.open_row[:, 2, :], m.bank[3][0:HEADS, 0:TILES]))
                scan_rows(dve, link, m, s, w, ones, count, 1, 0, "sum")
                scan_rows(dve, link, m, s, w, eid[:].unsqueeze(1), end, 1, 1, "back")
                dve.sem_inc(s.cols_ready, 1)
                dve.wait_ge(s.cols_done, 1)
                c = [m.bank[4 + k // 2][:, (k % 2) * TILES:(k % 2 + 1) * TILES] for k in range(len(cols))]
                dve.tensor_copy(m.dst[:], c[0])
                dve.tensor_copy(m.idx_l0[:, :, 0], c[1])
                dve.tensor_scalar(gathered[:], c[0], float(NODES - 1), None, ALU.min)
                dve.tensor_copy(m.map_idx[:], c[2])
                dve.tensor_copy(m.edge_id[:], c[3])
                dve.tensor_copy(m.indeg[:], c[4])
                link(dve.tensor_copy(m.idx_l1[:, :, 1], c[5]))
                dve.tensor_copy(m.idx_l0[:, :, 1], gathered[:])
                dve.tensor_scalar(m.rdeg[:], m.indeg[:], 1e-8, None, ALU.add)
                link(dve.tensor_scalar(m.sdeg[:], m.indeg[:], 1.0, None, ALU.add))
                dve.sem_inc(s.deg_ready, 1)
                link(dve.reciprocal(m.rdeg[:], m.rdeg[:]))
                dve.wait_ge(s.act_done, 1)
                link(dve.reciprocal(m.dinv[:], m.sdeg[:]))
                dve.tensor_scalar(m.sdeg[:], m.map_idx[:], float(NOWHERE), None, ALU.is_lt).then_inc(s.end_ready, 1)
                dve.wait_ge(s.end_ready, 1)
                dve.tensor_tensor(m.dinv_end[:], m.dinv[:], m.sdeg[:], ALU.mult)

            @block.tensor
            def _(pe):
                pe.wait_ge(s.flags_ready, 1)
                for k in range(3):
                    for b in range(BLOCKS):
                        at = (k % 2) * TILES + b * ROWS
                        ins = pe.transpose(m.bank[2 + k // 2][0:HEADS, at:at + ROWS], opens[:, b, k, :],
                                           m.ident[0:ROWS, 0:ROWS])
                ins.then_inc(s.opens_ready, 1)
                scan_rows_pe(pe, m, s, w, 1, 0, False)
                scan_rows_pe(pe, m, s, w, 1, 1, True)
                pe.wait_ge(s.cols_ready, 1)
                for k, rows in enumerate(cols):
                    for b in range(BLOCKS):
                        at = (k % 2) * TILES + b * ROWS
                        ins = pe.transpose(m.bank[4 + k // 2][:, at:at + ROWS], rows[:, b, :],
                                           m.ident[0:ROWS, 0:ROWS])
                ins.then_inc(s.cols_done, 1)


def load_key(sp, m, s, key, k):
    if k.slot:
        return
    half = k.body_slot // RING
    hold(sp, s.sel_done, k.t - RING)
    frm = m.dst_f[k.t * P:(k.t + RING) * P + 1] if isinstance(k.t, int) else m.dst_f[bass.ds(k.t * P, RING * P + 1)]
    sp.dma_start(key[:, half, :], frm.partition_broadcast(P)).then_inc(s.key_in[half], 16)


NORM_SEMS = ["bn_done", "mv_done", "root_done", "recip_done", "shift_done", "rows_done"]
NormSpace = namedtuple("NormSpace", "ring stats mv root rstd shift")


def norm_space(sb, n=P, ring=RING):
    return NormSpace(ring, sb("ystats", [n, ring, 6]), sb("mv", [n, ring, 2]), sb("root", [n, ring, 1]),
                     sb("rstd", [n, ring, 1]), sb("shift", [n, ring, 1]))


def norm_stats(dve, s, v, y, k):
    dve.bn_stats(v.stats[:, k.slot, :], y).then_inc(s.bn_done, 1)


def norm_aggregate(dve, s, v, k):
    hold(dve, s.bn_done, k.t + 1)
    dve.bn_aggr(v.mv[:, k.slot, :], v.stats[:, k.slot, :]).then_inc(s.mv_done, 1)


def norm_root(act, m, s, v, k, n=P):
    wait(act, s.recip_done, k.t - (v.ring - 1))
    act.wait_ge(s.mv_done, k.t + 1)
    act.activation(v.root[:, k.slot, :], v.mv[:, k.slot, 1:2], ACT.Sqrt, bias=m.eps[0:n]).then_inc(s.root_done, 1)


def norm_recip(dve, s, v, k):
    wait(dve, s.rows_done, k.t - (v.ring - 1))
    dve.wait_ge(s.root_done, k.t + 1)
    dve.reciprocal(v.rstd[:, k.slot, :], v.root[:, k.slot, :]).then_inc(s.recip_done, 1)


def norm_shift(dve, s, v, k):
    dve.wait_ge(s.recip_done, k.t + 1)
    dve.scalar_tensor_tensor(v.shift[:, k.slot, :], v.mv[:, k.slot, 0:1], -1.0, v.rstd[:, k.slot, :],
                             ALU.mult, ALU.mult).then_inc(s.shift_done, 1)


def norm_rows(act, s, v, to, y, k):
    act.wait_ge(s.shift_done, k.t + 1)
    act.activation(to, y, ACT.Identity, bias=v.shift[:, k.slot, :], scale=v.rstd[:, k.slot, :]).then_inc(s.rows_done, 1)


def edge_mlp(nc, d, m):
    names = ["idx_staged", "tr_done", "high_done", "low_done", "hid_done", "biased", "relu_done", "sel_done",
             "agg_done", "carry_done", "agg_high_done", "agg_low_done", "proj_done", "res_done", "y_done",
             "zero_done", "map_staged"] + NORM_SEMS
    rings = ["src_in", "dst_in", "src_out", "state_out", "map_out"]
    ctx, s = phase(nc, "edge_mlp", names, rings, [("key_in", 2)])
    with ctx:
        def sb(name, shape, dt=F32):
            return ctx.enter_context(nc.sbuf_tensor("mlp_" + name, shape, dt))
        idx = sb("idx", [P, RING, 2], I32)
        map_at, map_val = sb("map_at", [P, RING], I32), sb("map_val", [P, RING], I32)
        xs, xd = sb("xs", [P, RING, FEAT]), sb("xd", [P, RING, FEAT])
        key = sb("key", [P, 2, RING * P + 1])
        x_high, x_low = sb("x_high", [P, 2, 2 * FEAT], F32R), sb("x_low", [P, 2, 2 * FEAT], F32R)
        hb, h = sb("hb", [P, 2, HIDDEN]), sb("h", [P, 2, HIDDEN])
        same, cont = sb("same", [P, RING, P]), sb("cont", [P, RING, P])
        aggT = sb("aggT", [P, 2, HC, P])
        a_high, a_low = sb("a_high", [P, 2, HC, P], F32R), sb("a_low", [P, 2, HC, P], F32R)
        res, y, rows = sb("res", [P, RING, FEAT]), sb("y", [P, RING, FEAT]), sb("rows", [P, RING, FEAT])
        v = norm_space(sb)
        p_tr, p_hid, p_agg, p_out = (m.bank[2 * i:2 * i + 2] for i in range(4))

        with nc.Block() as block:
            @block.gpsimd
            def _(pool):
                def step(g, u):
                    if k := tile_at(g, u, 0):
                        hold(pool, s.src_in[k.slot], 16 * k.turn)
                        hold(pool, s.dst_in[k.slot], 16 * k.turn)
                        now = m.idx_l0[:, k.t, :] if isinstance(k.t, int) else \
                            m.idx_l0[:, bass.ds(k.t, 1), :].rearrange("p o k -> p (o k)")
                        pool.tensor_copy(idx[:, k.slot, :], now).then_inc(s.idx_staged, 1)
                        hold(pool, s.tr_done, k.t - (RING - 1))
                        hold(pool, s.src_out[k.slot], 16 * k.turn)
                        hold(pool, s.idx_staged, k.t + 1)
                        pool.indirect_dma_start(xs[:, k.slot, :], None, d.x,
                                                bass.IndirectOffsetOnAxis(ap=idx[:, k.slot, 0:1], axis=0))\
                            .then_inc(s.src_in[k.slot], 16)
                        hold(pool, s.res_done, k.t - (RING - 1))
                        pool.indirect_dma_start(xd[:, k.slot, :], None, d.x,
                                                bass.IndirectOffsetOnAxis(ap=idx[:, k.slot, 1:2], axis=0))\
                            .then_inc(s.dst_in[k.slot], 16)
                        hold(pool, s.map_out[k.slot], 16 * k.turn)
                        pool.tensor_copy(map_at[:, k.slot:k.slot + 1], col(m.map_idx, k.t))
                        pool.tensor_copy(map_val[:, k.slot:k.slot + 1], col(m.edge_id, k.t)).then_inc(s.map_staged, 1)
                        hold(pool, s.map_staged, k.t + 1)
                        pool.indirect_dma_start(m.node_map,
                                                bass.IndirectOffsetOnAxis(ap=map_at[:, k.slot:k.slot + 1], axis=0),
                                                map_val[:, k.slot:k.slot + 1], None,
                                                bounds_check=NODES - 1, oob_is_err=False)\
                            .then_inc(s.map_out[k.slot], 16)
                    if k := tile_at(g, u, 1):
                        hold(pool, s.dst_in[k.slot], 16 * (k.turn + 1))
                        hold(pool, s.y_done, k.t - (RING - 1))
                        pool.tensor_tensor(res[:, k.slot, :], xd[:, k.slot, :], m.b2[:], ALU.add).then_inc(s.res_done, 1)
                run_steps(pool, step, 1)
                for slot in range(RING):
                    pool.wait_ge(s.map_out[slot], 16 * (TILES // RING))

            @block.sync
            def _(sp):
                def step(g, u):
                    if k := tile_at(g, u, 0):
                        load_key(sp, m, s, key, k)
                    if k := tile_at(g, u, 1):
                        hold(sp, s.src_in[k.slot], 16 * (k.turn + 1))
                        sp.dma_start(tile_rows(m.x_src, k.t), xs[:, k.slot, :]).then_inc(s.src_out[k.slot], 16)
                    if k := tile_at(g, u, 8):
                        hold(sp, s.rows_done, k.t + 1)
                        sp.dma_start(tile_rows(m.state[1], k.t), rows[:, k.slot, :]).then_inc(s.state_out[k.slot], 16)
                run_steps(sp, step, 8)
                for slot in range(RING):
                    sp.wait_ge(s.src_out[slot], 16 * (TILES // RING))
                    sp.wait_ge(s.state_out[slot], 16 * (TILES // RING))

            @block.tensor
            def _(pe):
                def products(out_ap, high, low, w):
                    for c in range(len(high)):
                        for j, (a, b) in enumerate(((high[c], w[:, 0, c, :]), (high[c], w[:, 1, c, :]), (low[c], w[:, 0, c, :]))):
                            ins = pe.matmul(out_ap, a, b, start=c == 0 and j == 0,
                                            stop=c == len(high) - 1 and j == 2)
                    return ins

                def step(g, u):
                    if k := tile_at(g, u, 0):
                        pe.wait_ge(s.src_in[k.slot], 16 * (k.turn + 1))
                        pe.wait_ge(s.dst_in[k.slot], 16 * (k.turn + 1))
                        wait(pe, s.low_done, k.t - 1)
                        for c in range(FC):
                            pe.transpose(p_tr[k.pair][:, c * P:(c + 1) * P], xd[:, k.slot, c * P:(c + 1) * P], m.ident[:])
                        for c in range(FC):
                            ins = pe.transpose(p_tr[k.pair][:, FEAT + c * P:FEAT + (c + 1) * P],
                                               xs[:, k.slot, c * P:(c + 1) * P], m.ident[:])
                        ins.then_inc(s.tr_done, 1)
                    if k := tile_at(g, u, 1):
                        wait(pe, s.biased, k.t - 1)
                        pe.wait_ge(s.low_done, k.t + 1)
                        cut = [slice(c * P, (c + 1) * P) for c in range(2 * FC)]
                        products(p_hid[k.pair][:], [x_high[:, k.pair, c] for c in cut], [x_low[:, k.pair, c] for c in cut],
                                 m.w1).then_inc(s.hid_done, 1)
                    if k := tile_at(g, u, 2):
                        pe.wait_ge(s.relu_done, k.t + 1)
                        pe.wait_ge(s.sel_done, k.t + 1)
                        wait(pe, s.carry_done, k.t - 1)
                        for c in range(HC):
                            ins = pe.matmul(p_agg[k.pair][:, c * P:(c + 1) * P], h[:, k.pair, c * P:(c + 1) * P],
                                            same[:, k.slot, :], start=True, stop=True)
                        ins.then_inc(s.agg_done, 1)
                    if k := tile_at(g, u, 4):
                        pe.wait_ge(s.agg_low_done, k.t + 1)
                        wait(pe, s.y_done, k.t - 1)
                        products(p_out[k.pair][:, 0:FEAT], [a_high[:, k.pair, c, :] for c in range(HC)],
                                 [a_low[:, k.pair, c, :] for c in range(HC)], m.w2).then_inc(s.proj_done, 1)
                run_steps(pe, step, 4)

            @block.scalar
            def _(act):
                def step(g, u):
                    if k := tile_at(g, u, 7):
                        wait(act, s.state_out[k.slot], 16 * k.turn)
                        norm_rows(act, s, v, rows[:, k.slot, :], y[:, k.slot, :], k)
                    if k := tile_at(g, u, 0):
                        act.wait_ge(s.tr_done, k.t + 1)
                        wait(act, s.hid_done, k.t - 1)
                        act.copy(x_high[:, k.pair, :], p_tr[k.pair][:]).then_inc(s.high_done, 1)
                    if k := tile_at(g, u, 2):
                        act.wait_ge(s.biased, k.t + 1)
                        wait(act, s.agg_done, k.t - 1)
                        act.activation(h[:, k.pair, :], hb[:, k.pair, :], ACT.Relu).then_inc(s.relu_done, 1)
                    if k := tile_at(g, u, 3):
                        act.wait_ge(s.carry_done, k.t + 1)
                        wait(act, s.proj_done, k.t - 1)
                        act.copy(a_high[:, k.pair, :, :], aggT[:, k.pair, :, :]).then_inc(s.agg_high_done, 1)
                    if k := tile_at(g, u, 5):
                        norm_root(act, m, s, v, k)
                run_steps(act, step, 7)

            @block.vector
            def _(dve):
                dve.memset(aggT[:, 1, :, P - 1], 0.0).then_inc(s.zero_done, 1)
                dve.wait_ge(s.zero_done, 1)

                def step(g, u):
                    if recip := tile_at(g, u, 6):
                        norm_recip(dve, s, v, recip)
                    if k := tile_at(g, u, 4):
                        dve.wait_ge(s.agg_high_done, k.t + 1)
                        dve.tensor_tensor(a_low[:, k.pair, :, :], aggT[:, k.pair, :, :],
                                          a_high[:, k.pair, :, :].bitcast(F32), ALU.subtract).then_inc(s.agg_low_done, 1)
                    if k := tile_at(g, u, 2):
                        dve.wait_ge(s.hid_done, k.t + 1)
                        wait(dve, s.relu_done, k.t - 1)
                        dve.tensor_tensor(hb[:, k.pair, :], p_hid[k.pair][:], m.b1[:], ALU.add).then_inc(s.biased, 1)
                    if recip:
                        norm_shift(dve, s, v, recip)
                    if k := tile_at(g, u, 0):
                        dve.wait_ge(s.high_done, k.t + 1)
                        dve.tensor_tensor(x_low[:, k.pair, :], p_tr[k.pair][:], x_high[:, k.pair, :].bitcast(F32),
                                          ALU.subtract).then_inc(s.low_done, 1)
                    if k := tile_at(g, u, 3):
                        carry_over(dve, s, aggT, cont, p_agg, k, HC, s.agg_low_done)
                    if k := tile_at(g, u, 5):
                        dve.wait_ge(s.proj_done, k.t + 1)
                        dve.wait_ge(s.res_done, k.t + 1)
                        wait(dve, s.rows_done, k.t - (RING - 1))
                        dve.scalar_tensor_tensor(y[:, k.slot, :], p_out[k.pair][:, 0:FEAT], col(m.rdeg, k.t),
                                                 res[:, k.slot, :], ALU.mult, ALU.add).then_inc(s.y_done, 1)
                        dve.wait_ge(s.y_done, k.t + 1)
                        norm_stats(dve, s, v, y[:, k.slot, :], k)
                    stats = k
                    if k := tile_at(g, u, 1):
                        select(dve, m, s, key, same, cont, k)
                    if stats:
                        norm_aggregate(dve, s, v, stats)
                run_steps(dve, step, 6)




def affine_scalars(s, m, n, base, mean, var, cov, root, out, tmp):
    r1, r3, t, u = tmp
    alpha, beta, gamma = out
    bm, bv = m.bias_mv[0:n, 0:1], m.bias_mv[0:n, 1:2]

    def first(dve, link):
        dve.wait_ge(s.aff_root, base + 1)
        link(dve.reciprocal(r1, root))
        link(dve.scalar_tensor_tensor(t, mean, bm, cov, ALU.mult, ALU.subtract))
        link(dve.tensor_tensor(t, t, r1, ALU.mult))
        link(dve.tensor_tensor(u, r1, r1, ALU.mult))
        link(dve.tensor_tensor(u, u, var, ALU.mult))
        link(dve.scalar_tensor_tensor(u, t, -2.0, u, ALU.mult, ALU.add))
        dve.tensor_scalar(cov, u, bv, None, ALU.add).then_inc(s.aff_ask, 1)
        link(dve.tensor_tensor(t, r1, mean, ALU.mult))
        link(dve.tensor_scalar(t, t, bm, -1.0, ALU.add, ALU.mult))

    def second(dve, link):
        dve.wait_ge(s.aff_root, base + 2)
        link(dve.reciprocal(beta, root))
        link(dve.tensor_tensor(u, beta, beta, ALU.mult))
        dve.tensor_tensor(cov, cov, u, ALU.mult).then_inc(s.aff_ask, 1)
        link(dve.tensor_tensor(alpha, r1, beta, ALU.mult))
        link(dve.tensor_tensor(gamma, t, beta, ALU.mult))

    def third(dve, link):
        dve.wait_ge(s.aff_root, base + 3)
        link(dve.reciprocal(r3, root))
    return first, second, third


def affine_root(act, s, m, n, base, k, var, cov, root):
    act.wait_ge(s.aff_ask, base + k + 1)
    act.activation(root, cov if k else var, ACT.Sqrt, bias=m.eps[0:n]).then_inc(s.aff_root, 1)


def untouched_nodes(nc, d, m, out, n, first, tiles, unroll, batch, piece):
    main = tiles > 1
    pieces, slots = unroll // piece, min(2 * piece, unroll)
    names = ["seen", "dve_chain", "aff_ask", "aff_root", "scalars_done", "scaled", "x3_done", "tr_done", "evac_done",
             "proj_done", "staged", "moments_bn"] + NORM_SEMS
    ctx, s = phase(nc, "untouched" if main else "tail", names, (),
                   [("x_in", pieces), ("out_done", 2), ("found", LOOKUPS)])
    with ctx:
        tag = "main_" if main else "tail_"

        def sb(name, shape, dt=F32):
            return ctx.enter_context(nc.sbuf_tensor(tag + name, shape, dt))
        xin = sb("xin", [n, unroll, FEAT])
        stats, junk = sb("stats", [n, 2, 6]), sb("junk", [n, 2, FEAT])
        mom = sb("moments", [n, 2, 3, batch])
        root_b, out2, tmp = sb("root_b", [n, batch]), sb("out2", [n, 3, batch]), sb("tmpb", [n, 4, batch])
        aff = sb("aff", [n, 2, 3, batch])
        x3, x3T = sb("x3", [n, 3, FEAT]), sb("x3T", [P, 2, FC, n])
        v_norm = norm_space(sb, n, Y_BANKS)
        yrows = sb("yrows", [n, slots, FEAT])
        stage, pos = sb("stage", [P, LOOKUPS], I32), sb("pos", [P, LOOKUPS], I32)
        p_tr, p_out = m.bank[0:2], m.bank[2:2 + Y_BANKS]
        x_at = d.x[first:first + n * tiles, :].rearrange("(p k) f -> p (k f)", p=n)
        out_at = out[first:first + n * tiles, :].rearrange("(p k) f -> p (k f)", p=n)

        def at(g, u, lag):
            k = tile_at(g, u, lag, unroll, tiles)
            return k and k._replace(slot=(u - lag) % unroll % Y_BANKS)

        def steps(eng, step, lag):
            run_steps(eng, step, lag, unroll, tiles, 2)

        def batch_of(g, u, lag):
            v = u - lag
            return g * (unroll // batch) + v // batch, v % unroll // batch, v % batch

        def piece_ap(ap, t):
            size = piece * FEAT
            return ap[:, t * FEAT:t * FEAT + size] if isinstance(t, int) else ap[:, bass.ds(t * FEAT, size)]

        def triple(g, u, lag):
            return (u - lag) % unroll % 3
        A = piece
        B = A + 3 + batch

        with nc.Block() as block:
            @block.sync
            def _(sp):
                def step(g, u):
                    if (k := at(g, u, 0)) and u % piece == 0:
                        hold(sp, s.x3_done, k.t - unroll + piece)
                        lo = k.body_slot
                        sp.dma_start(xin[:, lo:lo + piece, :].rearrange("p k f -> p (k f)"), piece_ap(x_at, k.t))\
                          .then_inc(s.x_in[lo // piece], 16)
                    v = u - (B + 8)
                    if (k := at(g, u, B + 8)) and v % piece == piece - 1:
                        slot = (v % slots) // piece
                        hold(sp, s.rows_done, k.t + 1)
                        lo = slot * piece
                        sp.dma_start(piece_ap(out_at, k.t - (piece - 1)),
                                     yrows[:, lo:lo + piece, :].rearrange("p k f -> p (k f)"))\
                          .then_inc(s.out_done[slot], 16)
                steps(sp, step, B + 8)
                stores = tiles // piece
                for slot in range(2):
                    hold(sp, s.out_done[slot], 16 * ((stores + 1 - slot) // 2))

            @block.gpsimd
            def _(pool):
                def look_up(t, slot, turn):
                    put_away(t, slot, turn)
                    pool.tensor_copy(stage[:, slot:slot + 1], m.idx_l0[:, t:t + 1, 0] if isinstance(t, int) else
                                     m.idx_l0[:, bass.ds(t, 1), 0]).then_inc(s.staged, 1)
                    hold(pool, s.staged, t - (0 if main else TILES - 1) + 1)
                    pool.indirect_dma_start(pos[:, slot:slot + 1], None, m.node_map,
                                            bass.IndirectOffsetOnAxis(ap=stage[:, slot:slot + 1], axis=0))\
                        .then_inc(s.found[slot], 16)

                def put_away(t, slot, turn):
                    if isinstance(turn, int) and turn == 0:
                        return
                    hold(pool, s.found[slot], 16 * turn)
                    t -= LOOKUPS
                    to = m.idx_l1[:, t:t + 1, 0] if isinstance(t, int) else m.idx_l1[:, bass.ds(t, 1), 0]
                    pool.tensor_copy(to, pos[:, slot:slot + 1])

                def step(g, u):
                    if main and u % 2 == 1 and not (isinstance(g, int) and g >= tiles // unroll):
                        j = u // 2
                        look_up(g * (unroll // 2) + j, j % LOOKUPS, g * (unroll // (2 * LOOKUPS)) + j // LOOKUPS)
                steps(pool, step, 0)
                if main:
                    done = tiles // 2
                    for i in range(LOOKUPS):
                        put_away(done + i, (done + i) % LOOKUPS, done // LOOKUPS)
                else:
                    look_up(TILES - 1, 0, 0)
                    put_away(TILES - 1 + LOOKUPS, 0, 1)

            @block.scalar
            def _(act):
                def step(g, u):
                    if k := at(g, u, B + 8):
                        v = u - (B + 8)
                        slot = v % slots
                        if v % piece == 0:
                            wait(act, s.out_done[slot // piece], 16 * (k.t // (2 * piece)) if isinstance(k.t, int)
                                 else 16 * (g * (unroll // (2 * piece)) + v // (2 * piece)))
                        norm_rows(act, s, v_norm, yrows[:, slot, :], p_out[k.slot][0:n, 0:FEAT], k)
                    if k := at(g, u, B + 6):
                        norm_root(act, m, s, v_norm, k, n)
                    if k := at(g, u, B + 3):
                        act.wait_ge(s.tr_done, k.t + 1)
                        wait(act, s.proj_done, k.t - 1)
                        act.copy(x3T[:, k.pair, :, :], p_tr[k.pair][:, 0:FC * n].rearrange("p (c n) -> p c n", c=FC))\
                           .then_inc(s.evac_done, 1)
                    if k := at(g, u, B):
                        number, slot, i = batch_of(g, u, B)
                        act.wait_ge(s.scalars_done, number + 1)
                        wait(act, s.tr_done, k.t - 2)
                        act.activation(x3[:, triple(g, u, B), :], xin[:, k.body_slot, :], ACT.Identity,
                                       bias=aff[:, slot, 2, i:i + 1], scale=aff[:, slot, 0, i:i + 1])\
                           .then_inc(s.scaled, 1)
                    for part in range(3):
                        number, slot, i = batch_of(g, u, A + part)
                        if at(g, u, A + part) and i == batch - 1:
                            affine_root(act, s, m, n, number * 3, part, mom[:, slot, 1, :], mom[:, slot, 2, :], root_b[:])
                steps(act, step, B + 8)

            @block.tensor
            def _(pe):
                def step(g, u):
                    if k := at(g, u, B + 4):
                        pe.wait_ge(s.evac_done, k.t + 1)
                        wait(pe, s.rows_done, k.t - (Y_BANKS - 1))
                        y = p_out[k.slot][0:n, 0:FEAT]
                        pe.matmul(y, m.ones3[:, 0:n], m.res_parts[:], start=True, stop=False)
                        for c in range(FC):
                            ins = pe.matmul(y, x3T[:, k.pair, c, :], m.w_res[:, c, :], start=False, stop=c == FC - 1)
                        ins.then_inc(s.proj_done, 1)
                    if k := at(g, u, B + 2):
                        ring = triple(g, u, B + 2)
                        pe.wait_ge(s.x3_done, k.t + 1)
                        wait(pe, s.evac_done, k.t - 1)
                        for c in range(FC):
                            ins = pe.transpose(p_tr[k.pair][:, c * n:(c + 1) * n], x3[:, ring, c * P:(c + 1) * P],
                                               m.ident[0:n, 0:n])
                        ins.then_inc(s.tr_done, 1)
                steps(pe, step, B + 4)

            @block.vector
            def _(dve):
                def step(g, u):
                    if k7 := at(g, u, B + 7):
                        norm_recip(dve, s, v_norm, k7)
                    if k5 := at(g, u, B + 5):
                        dve.wait_ge(s.proj_done, k5.t + 1)
                        norm_stats(dve, s, v_norm, p_out[k5.slot][0:n, 0:FEAT], k5)
                    if k7:
                        norm_shift(dve, s, v_norm, k7)
                    if k := at(g, u, B + 1):
                        _, slot, i = batch_of(g, u, B + 1)
                        row = x3[:, triple(g, u, B + 1), :]
                        dve.wait_ge(s.scaled, k.t + 1)
                        dve.scalar_tensor_tensor(row, m.bias[0:n], aff[:, slot, 1, i:i + 1], row, ALU.mult, ALU.add)\
                           .then_inc(s.x3_done, 1)
                    if k5:
                        norm_aggregate(dve, s, v_norm, k5)
                    for part in range(3):
                        k = at(g, u, A + 1 + part)
                        number, slot, i = batch_of(g, u, A + 1 + part)
                        if not k or i != batch - 1:
                            continue
                        tm = [tmp[:, j, :] for j in range(4)]
                        parts = affine_scalars(s, m, n, number * 3, *(mom[:, slot, j, :] for j in range(3)),
                                               root_b[:], [out2[:, j, :] for j in range(3)], tm)
                        link = Chain(dve, s.dve_chain, number * (sum(AFFINE_LINKS) + 1) + sum(AFFINE_LINKS[:part]))
                        parts[part](dve, link)
                        if part == 2:
                            wait(dve, s.x3_done, k.t + 1 - 2 * batch)
                            for j in range(3):
                                ins = dve.tensor_tensor(aff[:, slot, j, :], out2[:, j, :], tm[1], ALU.mult)
                            link(ins)
                            dve.sem_inc(s.scalars_done, 1)
                    if k := at(g, u, A):
                        b, slot, i = batch_of(g, u, A)
                        if (u - A) % piece == 0:
                            dve.wait_ge(s.x_in[k.body_slot // piece], 16 * (k.body + 1))
                        wait(dve, s.seen, k.t - 1)
                        dve.bn_stats(stats[:, k.pair, :], xin[:, k.body_slot, :]).then_inc(s.moments_bn, 1)
                        dve.scalar_tensor_tensor(junk[:, k.pair, :], xin[:, k.body_slot, :], 1.0 / FEAT, m.bias[0:n],
                                                 ALU.mult, ALU.mult, accum_out=mom[:, slot, 2, i:i + 1])
                        hold(dve, s.moments_bn, k.t + 1)
                        dve.bn_aggr(mom[:, slot, 0:2, i], stats[:, k.pair, :]).then_inc(s.seen, 1)
                        if i == batch - 1:
                            hold(dve, s.seen, k.t + 1)
                            dve.sem_inc(s.aff_ask, 1)
                steps(dve, step, B + 7)


def gather_pos(pool, m, s, k, to, table, idx, ready):
    pool.indirect_dma_start(to, None, table, bass.IndirectOffsetOnAxis(ap=idx, axis=0),
                            bounds_check=EPAD - 1, oob_is_err=False).then_inc(ready, 16)


def gat_scores(nc, d, m):
    names = ["idx_staged", "bn_done", "seen", "root_done", "recip_done", "scal_done", "put_done", "x1_done", "tr_done", "evac_done",
             "prod_done", "enc_done", "h_done", "mul_done", "red_done", "score_done", "dve_chain", "aff_ask", "aff_root",
             "flags_done", "ones_done", "enc_ready"]
    rings = ["src_in", "dst_in", "edge_in", "h_out"]
    ctx, s = phase(nc, "gat_scores", names, rings, [("x_in", UNROLL)])
    with ctx:
        def sb(name, shape, dt=F32):
            return ctx.enter_context(nc.sbuf_tensor("gs_" + name, shape, dt))
        idx = sb("idx", [P, RING, 2], I32)
        xs, xd = sb("xs", [P, UNROLL, FEAT]), sb("xd", [P, RING, FEAT])
        edge = sb("edge", [EDGE_FEAT + 1, RING, P])
        stats, mom, junk = sb("stats", [P, 2, 6]), sb("mom", [P, RING, 3]), sb("junk", [P, 2, FEAT])
        root, rstd, scal = sb("root", [P, RING, 1]), sb("rstd", [P, RING, 1]), sb("scal", [P, RING, 2])
        x1, xT = sb("x1", [P, 2, FEAT]), sb("xT", [P, 2, 2 * FEAT])
        enc, prod, h = sb("enc", [P, 2, WIDE]), sb("prod", [P, 2, WIDE]), sb("h", [P, RING, WIDE])
        red, both = sb("red", [P, 2, HEADS]), sb("both", [P, 2, HEADS])
        root_all, tmp = sb("root_all", [P, TILES]), sb("tmp", [P, 4, TILES])
        p_tr, p_src, p_dst, p_enc = (m.bank[2 * i:2 * i + 2] for i in range(4))
        neg_un = sb("neg_un", [P, TILES])

        with nc.Block() as block:
            @block.sync
            def _(sp):
                def step(g, u):
                    if k := tile_at(g, u, 0):
                        hold(sp, s.x1_done, k.t - (UNROLL - 1))
                        sp.dma_start(xs[:, k.body_slot, :], tile_rows(m.x_src, k.t)).then_inc(s.x_in[k.body_slot], 16)
                    if k := tile_at(g, u, 4):
                        if isinstance(k.t, int) and k.t == 0:
                            sp.wait_ge(s.ones_done, 1)
                        hold(sp, s.prod_done, k.t - (RING - 1))
                        frm = d.edge_attr_T[:, k.t * P:k.t * P + P] if isinstance(k.t, int) else \
                            d.edge_attr_T[:, bass.ds(k.t * P, P)]
                        sp.dma_start(edge[0:EDGE_FEAT, k.slot, :], frm).then_inc(s.edge_in[k.slot], 16)
                    if k := tile_at(g, u, 12):
                        hold(sp, s.h_done, k.t + 1)
                        sp.dma_start(tile_rows(m.h_src, k.t), h[:, k.slot, 0:FEAT]).then_inc(s.h_out[k.slot], 16)
                run_steps(sp, step, 12)
                for slot in range(RING):
                    sp.wait_ge(s.h_out[slot], 16 * (TILES // RING))

            @block.gpsimd
            def _(pool):
                pool.memset(edge[:], 1.0).then_inc(s.ones_done, 1)

                def step(g, u):
                    if k := tile_at(g, u, 2):
                        hold(pool, s.src_in[k.slot], 16 * k.turn)
                        hold(pool, s.dst_in[k.slot], 16 * k.turn)
                        now = m.idx_l1[:, k.t, :] if isinstance(k.t, int) else \
                            m.idx_l1[:, bass.ds(k.t, 1), :].rearrange("p o k -> p (o k)")
                        pool.tensor_copy(idx[:, k.slot, :], now).then_inc(s.idx_staged, 1)
                        hold(pool, s.idx_staged, k.t + 1)
                        hold(pool, s.x_in[k.body_slot], 16 * (k.body + 1))
                        gather_pos(pool, m, s, k, xs[:, k.body_slot, :], m.state[1], idx[:, k.slot, 0:1], s.src_in[k.slot])
                        hold(pool, s.tr_done, k.t - (RING - 1))
                        gather_pos(pool, m, s, k, xd[:, k.slot, :], m.state[1], idx[:, k.slot, 1:2], s.dst_in[k.slot])
                run_steps(pool, step, 2)

            @block.scalar
            def _(act):
                def step(g, u):
                    if k := tile_at(g, u, 11):
                        act.wait_ge(s.prod_done, k.t + 1)
                        wait(act, s.mul_done, k.t - 1)
                        act.activation(enc[:, k.pair, 0:FEAT], p_enc[k.pair][:, 0:FEAT], ACT.Relu).then_inc(s.enc_done, 1)
                        wait(act, s.h_out[k.slot], 16 * k.turn)
                        wait(act, s.score_done, k.t - (RING - 1))
                        act.copy(h[:, k.slot, :], p_src[k.pair][:, 0:WIDE]).then_inc(s.h_done, 1)
                    if k := tile_at(g, u, 9):
                        act.wait_ge(s.tr_done, k.t + 1)
                        wait(act, s.prod_done, k.t - 1)
                        act.copy(xT[:, k.pair, :], p_tr[k.pair][:]).then_inc(s.evac_done, 1)
                    if k := tile_at(g, u, 7):
                        act.wait_ge(s.scal_done, k.t + 1)
                        wait(act, s.tr_done, k.t - 1)
                        act.activation(x1[:, k.pair, :], xs[:, k.body_slot, :], ACT.Identity, bias=scal[:, k.slot, 1:2],
                                       scale=scal[:, k.slot, 0:1]).then_inc(s.x1_done, 1)
                    if k := tile_at(g, u, 5):
                        act.wait_ge(s.seen, k.t + 1)
                        wait(act, s.recip_done, k.t - (RING - 1))
                        act.activation(root[:, k.slot, :], mom[:, k.slot, 1:2], ACT.Sqrt, bias=m.eps[:]).then_inc(s.root_done, 1)
                run_steps(act, step, 11)
                for part in range(3):
                    affine_root(act, s, m, P, 0, part, m.row_stat[:, 1, :], m.row_stat[:, 2, :], root_all[:])

            @block.tensor
            def _(pe):
                def step(g, u):
                    if k := tile_at(g, u, 10):
                        pe.wait_ge(s.evac_done, k.t + 1)
                        pe.wait_ge(s.edge_in[k.slot], 16 * (k.turn + 1))
                        wait(pe, s.h_done, k.t - 1)
                        wait(pe, s.mul_done, k.t - 1)
                        src = [xT[:, k.pair, c * P:(c + 1) * P] for c in range(FC)]
                        dst = [xT[:, k.pair, FEAT + c * P:FEAT + (c + 1) * P] for c in range(FC)]
                        pe.matmul(p_enc[k.pair][:, 0:FEAT], edge[:, k.slot, :], m.w_enc[:], start=True, stop=True)
                        for c in range(FC):
                            pe.matmul(p_src[k.pair][:, 0:WIDE], src[c], m.w_src[:, c, :], start=c == 0, stop=c == FC - 1)
                        for c in range(FC):
                            ins = pe.matmul(p_dst[k.pair][:, 0:WIDE], dst[c], m.w_dst[:, c, :], start=c == 0, stop=c == FC - 1)
                        ins.then_inc(s.prod_done, 1)
                    if k := tile_at(g, u, 8):
                        pe.wait_ge(s.x1_done, k.t + 1)
                        pe.wait_ge(s.dst_in[k.slot], 16 * (k.turn + 1))
                        wait(pe, s.evac_done, k.t - 1)
                        for c in range(FC):
                            pe.transpose(p_tr[k.pair][:, c * P:(c + 1) * P], x1[:, k.pair, c * P:(c + 1) * P], m.ident[:])
                        for c in range(FC):
                            ins = pe.transpose(p_tr[k.pair][:, FEAT + c * P:FEAT + (c + 1) * P],
                                               xd[:, k.slot, c * P:(c + 1) * P], m.ident[:])
                        ins.then_inc(s.tr_done, 1)
                run_steps(pe, step, 10)

            @block.vector
            def _(dve):
                dve.tensor_scalar(m.touched[:], m.idx_l1[:, :, 0], float(NOWHERE), None, ALU.is_lt)
                dve.tensor_scalar(m.untouched[:], m.idx_l1[:, :, 0], float(NOWHERE), None, ALU.is_ge)
                dve.tensor_scalar(neg_un[:], m.idx_l1[:, :, 0], float(NOWHERE), -1.0, ALU.is_ge, ALU.mult).then_inc(s.flags_done, 1)
                dve.memset(enc[:, :, FEAT:WIDE], 1.0).then_inc(s.enc_ready, 1)
                dve.wait_ge(s.flags_done, 1)
                dve.wait_ge(s.enc_ready, 1)

                def step(g, u):
                    if k := tile_at(g, u, 12):
                        dve.wait_ge(s.mul_done, k.t + 1)
                        wait(dve, s.score_done, k.t - 1)
                        dve.wait_ge(s.h_done, k.t + 1)
                        dve.tensor_tensor(both[:, k.pair, :], prod[:, k.pair, FEAT:WIDE], h[:, k.slot, FEAT:WIDE], ALU.add)
                        dve.tensor_reduce(red[:, k.pair, :], prod[:, k.pair, 0:FEAT].rearrange("p (h d) -> p h d", h=HEADS),
                                          AX.X, ALU.add).then_inc(s.red_done, 1)
                    if k := tile_at(g, u, 6):
                        dve.wait_ge(s.root_done, k.t + 1)
                        wait(dve, s.x1_done, k.t - (RING - 1))
                        dve.reciprocal(rstd[:, k.slot, :], root[:, k.slot, :]).then_inc(s.recip_done, 1)
                        dve.wait_ge(s.recip_done, k.t + 1)
                        dve.scalar_tensor_tensor(scal[:, k.slot, 0:1], rstd[:, k.slot, :], col(m.untouched, k.t),
                                                 col(m.touched, k.t), ALU.mult, ALU.add)
                        dve.scalar_tensor_tensor(scal[:, k.slot, 1:2], mom[:, k.slot, 0:1], rstd[:, k.slot, :],
                                                 col(neg_un, k.t), ALU.mult, ALU.mult).then_inc(s.scal_done, 1)
                        to = m.row_stat[:, :, k.t] if isinstance(k.t, int) else \
                            m.row_stat[:, :, bass.ds(k.t, 1)].rearrange("p k o -> p (k o)")
                        dve.tensor_copy(to, mom[:, k.slot, :]).then_inc(s.put_done, 1)
                    if k := tile_at(g, u, 4):
                        dve.wait_ge(s.src_in[k.slot], 16 * (k.turn + 1))
                        wait(dve, s.seen, k.t - 1)
                        wait(dve, s.put_done, k.t - (RING - 1))
                        dve.bn_stats(stats[:, k.pair, :], xs[:, k.body_slot, :]).then_inc(s.bn_done, 1)
                        dve.scalar_tensor_tensor(junk[:, k.pair, :], xs[:, k.body_slot, :], 1.0 / FEAT, m.bias[:],
                                                 ALU.mult, ALU.mult, accum_out=mom[:, k.slot, 2:3])
                        hold(dve, s.bn_done, k.t + 1)
                        dve.bn_aggr(mom[:, k.slot, 0:2], stats[:, k.pair, :]).then_inc(s.seen, 1)
                    if k := tile_at(g, u, 12):
                        dve.wait_ge(s.red_done, k.t + 1)
                        to = m.score[:, k.t, :] if isinstance(k.t, int) else \
                            m.score[:, bass.ds(k.t, 1), :].rearrange("p o h -> p (o h)")
                        dve.tensor_tensor(to, red[:, k.pair, :], both[:, k.pair, :], ALU.add).then_inc(s.score_done, 1)
                    if k := tile_at(g, u, 11):
                        dve.wait_ge(s.enc_done, k.t + 1)
                        wait(dve, s.score_done, k.t - 1)
                        dve.tensor_tensor(prod[:, k.pair, :], enc[:, k.pair, :], p_dst[k.pair][:, 0:WIDE], ALU.mult)\
                           .then_inc(s.mul_done, 1)
                run_steps(dve, step, 12)
                dve.wait_ge(s.put_done, TILES)
                dve.sem_inc(s.aff_ask, 1)
                link = Chain(dve, s.dve_chain, 0)
                tm = [tmp[:, j, :] for j in range(4)]
                second, third = ([m.affine[:, i, j, :] for j in range(3)] for i in range(2))
                for part in affine_scalars(s, m, P, 0, *(m.row_stat[:, j, :] for j in range(3)), root_all[:], second, tm):
                    part(dve, link)
                for j in range(3):
                    ins = dve.tensor_tensor(third[j], second[j], tm[1], ALU.mult)
                link(ins)
                for part in (*second, *third):
                    ins = dve.tensor_tensor(part, part, m.untouched[:], ALU.mult)
                link(ins)
                for part in (second[0], third[0]):
                    dve.tensor_tensor(part, part, m.touched[:], ALU.add)


def softmax_rows(dve, link, act_exp, m, s, w, score, run, spread, heads, n):
    scan_rows(dve, link, m, s, w, score, run, heads, n, "max")
    scan_rows(dve, link, m, s, w, run, spread, heads, n + 1, "back")
    link(dve.tensor_tensor(score, score, spread, ALU.subtract))
    act_exp()
    scan_rows(dve, link, m, s, w, score, run, heads, n + 2, "sum")
    scan_rows(dve, link, m, s, w, run, spread, heads, n + 3, "back")


def gat_softmax(nc, m):
    ctx, s = phase(nc, "gat_softmax", ["dve_chain", "leaky_done", "in_rows", "exp_ask", "exp_done", "weights_done", "in_cols"] + SCAN_SEMS)
    with ctx:
        def sb(name, shape, dt=F32):
            return ctx.enter_context(nc.sbuf_tensor("sm_" + name, shape, dt))
        shape = [ROWS, HEADS, BLOCKS, P]
        score, run, spread = sb("score", shape), sb("run", shape), sb("spread", shape)
        w = ScanSpace(total=sb("total", [ROWS, BLOCKS, HEADS]), between=sb("between", [HEADS, TILES + 1]),
                            carry=sb("carry", [ROWS, BLOCKS, HEADS]))
        pairs = [(h, b) for h in range(HEADS) for b in range(BLOCKS)]
        with nc.Block() as block:
            @block.tensor
            def _(pe):
                pe.wait_ge(s.leaky_done, 1)
                for k, (h, b) in enumerate(pairs):
                    ins = pe.transpose(m.bank[2 + k // 4][0:ROWS, (k % 4) * P:(k % 4 + 1) * P],
                                       m.score[:, b * ROWS:(b + 1) * ROWS, h], m.ident[:])
                ins.then_inc(s.in_rows, 1)
                for n, back in enumerate((False, True, False, True)):
                    scan_rows_pe(pe, m, s, w, HEADS, n, back)
                pe.wait_ge(s.weights_done, 1)
                for k, (h, b) in enumerate(pairs):
                    ins = pe.transpose(m.bank[2 + k // 4][:, (k % 4) * ROWS:(k % 4 + 1) * ROWS], score[:, h, b, :],
                                       m.ident[0:ROWS, 0:ROWS])
                ins.then_inc(s.in_cols, 1)

            @block.scalar
            def _(act):
                act.wait_ge(s.exp_ask, 1)
                act.activation(score[:], score[:], ACT.Exp).then_inc(s.exp_done, 1)

            @block.vector
            def _(dve):
                link = Chain(dve, s.dve_chain)
                flat = m.score[:].rearrange("p t h -> p (t h)")
                dve.scalar_tensor_tensor(flat, flat, 0.2, flat, ALU.mult, ALU.max).then_inc(s.leaky_done, 1)
                dve.wait_ge(s.in_rows, 1)
                for j in range(4):
                    ins = dve.tensor_copy(score[:, 2 * j:2 * j + 2, :, :].rearrange("r h b e -> r (h b e)"),
                                          m.bank[2 + j][0:ROWS, :])
                link(ins)

                def exp():
                    dve.sem_inc(s.exp_ask, 1)
                    dve.wait_ge(s.exp_done, 1)
                softmax_rows(dve, link, exp, m, s, w, score[:], run[:], spread[:], HEADS, 0)
                link(dve.tensor_scalar(spread[:], spread[:], 1e-10, None, ALU.max))
                link(dve.reciprocal(spread[:], spread[:]))
                dve.tensor_tensor(score[:], score[:], spread[:], ALU.mult).then_inc(s.weights_done, 1)
                dve.wait_ge(s.in_cols, 1)
                for j in range(4):
                    dve.tensor_copy(m.score[:].rearrange("p (b r) h -> p h b r", b=BLOCKS)[:, 2 * j:2 * j + 2, :, :],
                                    m.bank[2 + j][:, 0:4 * ROWS].rearrange("p (h b r) -> p h b r", h=2, b=BLOCKS))


def scalar_softmax(nc, m):
    ctx, s = phase(nc, "scalar_softmax", ["dve_chain", "in_rows", "exp_ask", "exp_done", "weights_done", "in_cols"] + SCAN_SEMS)
    with ctx:
        def sb(name, shape, dt=F32):
            return ctx.enter_context(nc.sbuf_tensor("sq_" + name, shape, dt))
        shape = [ROWS, 1, BLOCKS, P]
        q, k, score, run, spread = (sb(n, shape) for n in ("q", "k", "score", "run", "spread"))
        w = ScanSpace(total=sb("total", [ROWS, BLOCKS, 1]), between=sb("between", [1, TILES + 1]),
                            carry=sb("carry", [ROWS, BLOCKS, 1]))
        with nc.Block() as block:
            @block.tensor
            def _(pe):
                for i, cols in enumerate((m.q_src, m.k_dst)):
                    for b in range(BLOCKS):
                        at = (i * BLOCKS + b) * P
                        ins = pe.transpose(m.bank[2][0:ROWS, at:at + P], cols[:, b * ROWS:(b + 1) * ROWS], m.ident[:])
                ins.then_inc(s.in_rows, 1)
                for n, back in enumerate((True, False, True, False, True)):
                    scan_rows_pe(pe, m, s, w, 1, n, back)
                pe.wait_ge(s.weights_done, 1)
                for b in range(BLOCKS):
                    ins = pe.transpose(m.bank[2][:, b * ROWS:(b + 1) * ROWS], score[:, 0, b, :], m.ident[0:ROWS, 0:ROWS])
                ins.then_inc(s.in_cols, 1)

            @block.scalar
            def _(act):
                act.wait_ge(s.exp_ask, 1)
                act.activation(score[:], score[:], ACT.Exp).then_inc(s.exp_done, 1)

            @block.vector
            def _(dve):
                link = Chain(dve, s.dve_chain)
                dve.wait_ge(s.in_rows, 1)
                dve.tensor_copy(q[:].rearrange("r o b e -> r (o b e)"), m.bank[2][0:ROWS, 0:BLOCKS * P])
                link(dve.tensor_tensor(run[:, 0], m.bank[2][0:ROWS, BLOCKS * P:2 * BLOCKS * P].rearrange("r (b e) -> r b e", b=BLOCKS),
                                       m.last[:], ALU.mult))
                link(dve.tensor_scalar(k[:, 0], m.last[:], -LOW, LOW, ALU.mult, ALU.add))
                link(dve.tensor_tensor(k[:], run[:], k[:], ALU.add))
                scan_rows(dve, link, m, s, w, k[:], spread[:], 1, 0, "back")
                link(dve.tensor_tensor(score[:], q[:], spread[:], ALU.add))
                link(dve.tensor_scalar(score[:], score[:], m.qk_bias[0:ROWS, :], None, ALU.add))
                link(dve.scalar_tensor_tensor(score[:], score[:], 0.2, score[:], ALU.mult, ALU.max))

                def exp():
                    dve.sem_inc(s.exp_ask, 1)
                    dve.wait_ge(s.exp_done, 1)
                softmax_rows(dve, link, exp, m, s, w, score[:], run[:], spread[:], 1, 1)
                link(dve.reciprocal(spread[:], spread[:]))
                dve.tensor_tensor(score[:], score[:], spread[:], ALU.mult).then_inc(s.weights_done, 1)
                dve.wait_ge(s.in_cols, 1)
                dve.tensor_copy(m.attn2[:], m.bank[2][:, 0:TILES])


def select(dve, m, s, key, same, cont, k, weight=None):
    half, at = k.body_slot // RING, k.slot * P
    before, own = key[:, half, at:at + 1], key[:, half, at + 1:at + P + 1]
    dve.wait_ge(s.key_in[half], 16 * (k.body + 1))
    wait(dve, s.agg_done, k.t - (RING - 1))
    dve.tensor_scalar(cont[:, k.slot, :], own, before, None, ALU.is_equal)
    if weight is None:
        ins = dve.tensor_scalar(same[:, k.slot, :], own, col(m.dst, k.t), None, ALU.is_equal)
    else:
        ins = dve.tensor_scalar(same[:, k.slot, :], own, col(m.dst, k.t), col(weight, k.t), ALU.is_equal, ALU.mult)
    ins.then_inc(s.sel_done, 1)


def carry_over(dve, s, aggT, cont, p_agg, k, chunks, user_done):
    dve.wait_ge(s.agg_done, k.t + 1)
    wait(dve, user_done, k.t - 1)
    dve.wait_ge(s.sel_done, k.t + 1)
    wait(dve, s.carry_done, k.t)
    for c in range(chunks):
        ins = dve.scalar_tensor_tensor(aggT[:, k.pair, c, :], cont[:, k.slot, :], aggT[:, 1 - k.pair, c, P - 1:P],
                                       p_agg[k.pair][:, c * P:(c + 1) * P], ALU.mult, ALU.add)
    ins.then_inc(s.carry_done, 1)


def gat_sum(nc, d, m):
    names = ["sel_done", "weigh_done", "agg_done", "carry_done", "sum_done", "y_done", "zero_done", "k_done"] + NORM_SEMS
    ctx, s = phase(nc, "gat_sum", names, ["h_in", "own_in", "state_out"], [("key_in", 2)])
    with ctx:
        def sb(name, shape, dt=F32):
            return ctx.enter_context(nc.sbuf_tensor("gc_" + name, shape, dt))
        key, same, cont = sb("key", [P, 2, RING * P + 1]), sb("same", [P, RING, P]), sb("cont", [P, RING, P])
        h, own, msg = sb("h", [P, RING, FEAT]), sb("own", [P, RING, FEAT]), sb("msg", [P, 2, FEAT])
        aggT, junk = sb("aggT", [P, 2, FC, P]), sb("junk", [P, 2, FEAT])
        y, rows = sb("y", [P, RING, FEAT]), sb("rows", [P, RING, FEAT])
        v = norm_space(sb)
        p_agg, p_y = m.bank[0:2], m.bank[2:4]

        with nc.Block() as block:
            @block.sync
            def _(sp):
                def step(g, u):
                    if k := tile_at(g, u, 0):
                        load_key(sp, m, s, key, k)
                    if k := tile_at(g, u, 3):
                        hold(sp, s.weigh_done, k.t - (RING - 1))
                        sp.dma_start(h[:, k.slot, :], tile_rows(m.h_src, k.t)).then_inc(s.h_in[k.slot], 16)
                        hold(sp, s.sum_done, k.t - (RING - 1))
                        sp.dma_start(own[:, k.slot, :], tile_rows(m.state[1], k.t)).then_inc(s.own_in[k.slot], 16)
                run_steps(sp, step, 3)
                for slot in range(RING):
                    sp.wait_ge(s.state_out[slot], 16 * (TILES // RING))

            @block.gpsimd
            def _(pool):
                def step(g, u):
                    if k := tile_at(g, u, 5):
                        hold(pool, s.h_in[k.slot], 16 * (k.turn + 1))
                        hold(pool, s.agg_done, k.t - 1)
                        attn = m.score[:, k.t, :] if isinstance(k.t, int) else \
                            m.score[:, bass.ds(k.t, 1), :].rearrange("p o h -> p (o h)")
                        pool.tensor_tensor(msg[:, k.pair, :].rearrange("p (h d) -> p h d", h=HEADS),
                                           h[:, k.slot, :].rearrange("p (h d) -> p h d", h=HEADS),
                                           attn.unsqueeze(2).to_broadcast([P, HEADS, HEAD_DIM]), ALU.mult)\
                            .then_inc(s.weigh_done, 1)
                run_steps(pool, step, 5)

            @block.scalar
            def _(act):
                def step(g, u):
                    if k := tile_at(g, u, 14):
                        hold(act, s.rows_done, k.t + 1)
                        act.dma_start(tile_rows(m.state[2], k.t), rows[:, k.slot, :]).then_inc(s.state_out[k.slot], 16)
                    if k := tile_at(g, u, 13):
                        wait(act, s.state_out[k.slot], 16 * k.turn)
                        wait(act, s.k_done, k.t - (RING - 1))
                        norm_rows(act, s, v, rows[:, k.slot, :], y[:, k.slot, :], k)
                    if k := tile_at(g, u, 11):
                        norm_root(act, m, s, v, k)
                    if k := tile_at(g, u, 9):
                        act.wait_ge(s.sum_done, k.t + 1)
                        act.copy(y[:, k.slot, :], p_y[k.pair][:, 0:FEAT]).then_inc(s.y_done, 1)
                run_steps(act, step, 14)

            @block.tensor
            def _(pe):
                def step(g, u):
                    if k := tile_at(g, u, 8):
                        wait(pe, s.y_done, k.t - 1)
                        pe.matmul(p_y[k.pair][:, 0:FEAT], m.ones3[:], m.bias_parts[:], start=True, stop=False)
                        pe.wait_ge(s.own_in[k.slot], 16 * (k.turn + 1))
                        pe.matmul(p_y[k.pair][:, 0:FEAT], m.ident[:], own[:, k.slot, :], start=False, stop=False)
                        pe.wait_ge(s.carry_done, k.t + 1)
                        for c in range(FC):
                            ins = pe.matmul(p_y[k.pair][:, c * P:(c + 1) * P], aggT[:, k.pair, c, :], m.ident[:],
                                            start=False, stop=c == FC - 1)
                        ins.then_inc(s.sum_done, 1)
                    if k := tile_at(g, u, 6):
                        pe.wait_ge(s.weigh_done, k.t + 1)
                        pe.wait_ge(s.sel_done, k.t + 1)
                        wait(pe, s.carry_done, k.t - 1)
                        for c in range(FC):
                            ins = pe.matmul(p_agg[k.pair][:, c * P:(c + 1) * P], msg[:, k.pair, c * P:(c + 1) * P],
                                            same[:, k.slot, :], start=True, stop=True)
                        ins.then_inc(s.agg_done, 1)
                run_steps(pe, step, 8)

            @block.vector
            def _(dve):
                dve.memset(aggT[:, 1, :, P - 1], 0.0).then_inc(s.zero_done, 1)
                dve.wait_ge(s.zero_done, 1)

                def step(g, u):
                    if recip := tile_at(g, u, 12):
                        norm_recip(dve, s, v, recip)
                    if k := tile_at(g, u, 14):
                        wait(dve, s.k_done, k.t - 1)
                        dve.wait_ge(s.rows_done, k.t + 1)
                        dve.scalar_tensor_tensor(junk[:, k.pair, :], rows[:, k.slot, :], 1.0, m.k_row[:], ALU.mult, ALU.mult,
                                                 accum_out=col(m.k_dst, k.t)).then_inc(s.k_done, 1)
                    if stats := tile_at(g, u, 10):
                        dve.wait_ge(s.y_done, stats.t + 1)
                        norm_stats(dve, s, v, y[:, stats.slot, :], stats)
                    if recip:
                        norm_shift(dve, s, v, recip)
                    if k := tile_at(g, u, 7):
                        carry_over(dve, s, aggT, cont, p_agg, k, FC, s.sum_done)
                    if stats:
                        norm_aggregate(dve, s, v, stats)
                    if k := tile_at(g, u, 5):
                        select(dve, m, s, key, same, cont, k)
                run_steps(dve, step, 14)


def load_sources(sp, m, s, xs, free, k):
    hold(sp, free, k.t - (RING - 1))
    sp.dma_start(xs[:, k.slot, :], tile_rows(m.x_src, k.t)).then_inc(s.x_in[k.slot], 16)


def stage_indices(pool, s, staged, source, done, k):
    if k.slot:
        return
    half = k.body_slot // RING
    for slot in range(RING):
        hold(pool, done[slot], 16 * (k.turn - 1))
    to = staged[:, half * RING:(half + 1) * RING]
    pool.tensor_copy(to, source[:, k.t:k.t + RING] if isinstance(k.t, int) else source[:, bass.ds(k.t, RING)])\
        .then_inc(s.idx_staged, 1)


def overlay(pool, m, s, xs, idx, table, k):
    stage_indices(pool, s, idx, m.idx_l1[:, :, 0], s.src_in, k)
    hold(pool, s.x_in[k.slot], 16 * (k.turn + 1))
    if k.slot == 0:
        hold(pool, s.idx_staged, k.turn + 1)
    at = k.body_slot
    gather_pos(pool, m, s, k, xs[:, k.slot, :], table, idx[:, at:at + 1], s.src_in[k.slot])


def scalar_scores(nc, d, m):
    ctx, s = phase(nc, "scalar_scores", ["idx_staged", "scaled", "x2_done", "q_done"], ["x_in", "src_in", "x2_out"])
    with ctx:
        def sb(name, shape, dt=F32):
            return ctx.enter_context(nc.sbuf_tensor("ss_" + name, shape, dt))
        idx, xs = sb("idx", [P, UNROLL], I32), sb("xs", [P, RING, FEAT])
        ax, x2, junk = sb("ax", [P, 2, FEAT]), sb("x2", [P, RING, FEAT]), sb("junk", [P, 2, FEAT])
        alpha, beta, gamma = (m.affine[:, 0, j, :] for j in range(3))
        with nc.Block() as block:
            @block.sync
            def _(sp):
                def step(g, u):
                    if k := tile_at(g, u, 0):
                        load_sources(sp, m, s, xs, s.scaled, k)
                    if k := tile_at(g, u, 8):
                        hold(sp, s.x2_done, k.t + 1)
                        sp.dma_start(tile_rows(m.x2_src, k.t), x2[:, k.slot, :]).then_inc(s.x2_out[k.slot], 16)
                run_steps(sp, step, 8)
                for slot in range(RING):
                    sp.wait_ge(s.x2_out[slot], 16 * (TILES // RING))

            @block.gpsimd
            def _(pool):
                def step(g, u):
                    if k := tile_at(g, u, 2):
                        overlay(pool, m, s, xs, idx, m.state[2], k)
                run_steps(pool, step, 2)

            @block.scalar
            def _(act):
                def step(g, u):
                    if k := tile_at(g, u, 6):
                        act.wait_ge(s.src_in[k.slot], 16 * (k.turn + 1))
                        wait(act, s.x2_done, k.t - 1)
                        act.activation(ax[:, k.pair, :], xs[:, k.slot, :], ACT.Identity, bias=col(gamma, k.t),
                                       scale=col(alpha, k.t)).then_inc(s.scaled, 1)
                run_steps(act, step, 6)

            @block.vector
            def _(dve):
                def step(g, u):
                    if k := tile_at(g, u, 7):
                        wait(dve, s.x2_out[k.slot], 16 * k.turn)
                        dve.wait_ge(s.scaled, k.t + 1)
                        dve.scalar_tensor_tensor(x2[:, k.slot, :], m.bias[:], col(beta, k.t), ax[:, k.pair, :],
                                                 ALU.mult, ALU.add).then_inc(s.x2_done, 1)
                        wait(dve, s.q_done, k.t - 1)
                        dve.wait_ge(s.x2_done, k.t + 1)
                        dve.scalar_tensor_tensor(junk[:, k.pair, :], x2[:, k.slot, :], 1.0, m.q_row[:], ALU.mult, ALU.mult,
                                                 accum_out=col(m.q_src, k.t)).then_inc(s.q_done, 1)
                run_steps(dve, step, 7)


def scalar_sum(nc, d, m):
    names = ["sel_done", "agg_done", "carry_done", "sum_done", "y_done", "zero_done", "scaled", "res_done"] + NORM_SEMS
    ctx, s = phase(nc, "scalar_sum", names, ["x_in", "own_in", "state_out", "res_out"], [("key_in", 2)])
    with ctx:
        def sb(name, shape, dt=F32):
            return ctx.enter_context(nc.sbuf_tensor("sc_" + name, shape, dt))
        key, same, cont = sb("key", [P, 2, RING * P + 1]), sb("same", [P, RING, P]), sb("cont", [P, RING, P])
        xs, own = sb("xs", [P, RING, FEAT]), sb("own", [P, RING, FEAT])
        aggT, y, rows = sb("aggT", [P, 2, FC, P]), sb("y", [P, RING, FEAT]), sb("rows", [P, RING, FEAT])
        z, res = sb("z", [P, RING, FEAT]), sb("res", [P, RING, FEAT])
        v = norm_space(sb)
        p_agg, p_y = m.bank[0:2], m.bank[2:4]

        with nc.Block() as block:
            @block.sync
            def _(sp):
                def step(g, u):
                    if k := tile_at(g, u, 0):
                        load_key(sp, m, s, key, k)
                    if k := tile_at(g, u, 2):
                        hold(sp, s.agg_done, k.t - (RING - 1))
                        sp.dma_start(xs[:, k.slot, :], tile_rows(m.x2_src, k.t)).then_inc(s.x_in[k.slot], 16)
                        hold(sp, s.y_done, k.t - (RING - 1))
                        sp.dma_start(own[:, k.slot, :], tile_rows(m.state[2], k.t)).then_inc(s.own_in[k.slot], 16)
                    if k := tile_at(g, u, 14):
                        hold(sp, s.res_done, k.t + 1)
                        sp.dma_start(tile_rows(m.res3, k.t), res[:, k.slot, :]).then_inc(s.res_out[k.slot], 16)
                run_steps(sp, step, 14)
                for slot in range(RING):
                    sp.wait_ge(s.state_out[slot], 16 * (TILES // RING))
                    sp.wait_ge(s.res_out[slot], 16 * (TILES // RING))

            @block.gpsimd
            def _(pool):
                def step(g, u):
                    if k := tile_at(g, u, 13):
                        hold(pool, s.rows_done, k.t + 1)
                        hold(pool, s.res_out[k.slot], 16 * k.turn)
                        pool.tensor_tensor(res[:, k.slot, :], rows[:, k.slot, :], m.res_bias[:], ALU.add).then_inc(s.res_done, 1)
                run_steps(pool, step, 13)

            @block.scalar
            def _(act):
                def step(g, u):
                    if k := tile_at(g, u, 14):
                        hold(act, s.scaled, k.t + 1)
                        act.dma_start(tile_rows(m.state[3], k.t), z[:, k.slot, :]).then_inc(s.state_out[k.slot], 16)
                    if k := tile_at(g, u, 13):
                        wait(act, s.state_out[k.slot], 16 * k.turn)
                        act.wait_ge(s.rows_done, k.t + 1)
                        act.activation(z[:, k.slot, :], rows[:, k.slot, :], ACT.Copy, scale=col(m.dinv_end, k.t)).then_inc(s.scaled, 1)
                    if k := tile_at(g, u, 12):
                        wait(act, s.res_done, k.t - (RING - 1))
                        wait(act, s.scaled, k.t - (RING - 1))
                        norm_rows(act, s, v, rows[:, k.slot, :], y[:, k.slot, :], k)
                    if k := tile_at(g, u, 10):
                        norm_root(act, m, s, v, k)
                run_steps(act, step, 14)

            @block.tensor
            def _(pe):
                def step(g, u):
                    if k := tile_at(g, u, 7):
                        wait(pe, s.y_done, k.t - 1)
                        pe.matmul(p_y[k.pair][:, 0:FEAT], m.ones3[:], m.bv_parts[:], start=True, stop=False)
                        pe.wait_ge(s.carry_done, k.t + 1)
                        for c in range(FC):
                            ins = pe.matmul(p_y[k.pair][:, 0:FEAT], aggT[:, k.pair, c, :], m.wv[:, c, :],
                                            start=False, stop=c == FC - 1)
                        ins.then_inc(s.sum_done, 1)
                    if k := tile_at(g, u, 5):
                        pe.wait_ge(s.x_in[k.slot], 16 * (k.turn + 1))
                        pe.wait_ge(s.sel_done, k.t + 1)
                        wait(pe, s.carry_done, k.t - 1)
                        for c in range(FC):
                            ins = pe.matmul(p_agg[k.pair][:, c * P:(c + 1) * P], xs[:, k.slot, c * P:(c + 1) * P],
                                            same[:, k.slot, :], start=True, stop=True)
                        ins.then_inc(s.agg_done, 1)
                run_steps(pe, step, 7)

            @block.vector
            def _(dve):
                dve.memset(aggT[:, 1, :, P - 1], 0.0).then_inc(s.zero_done, 1)
                dve.wait_ge(s.zero_done, 1)

                def step(g, u):
                    if recip := tile_at(g, u, 11):
                        norm_recip(dve, s, v, recip)
                    if stats := tile_at(g, u, 9):
                        dve.wait_ge(s.y_done, stats.t + 1)
                        norm_stats(dve, s, v, y[:, stats.slot, :], stats)
                    if recip:
                        norm_shift(dve, s, v, recip)
                    if k := tile_at(g, u, 6):
                        carry_over(dve, s, aggT, cont, p_agg, k, FC, s.sum_done)
                    if stats:
                        norm_aggregate(dve, s, v, stats)
                    if k := tile_at(g, u, 8):
                        dve.wait_ge(s.sum_done, k.t + 1)
                        dve.wait_ge(s.own_in[k.slot], 16 * (k.turn + 1))
                        wait(dve, s.rows_done, k.t - (RING - 1))
                        dve.tensor_tensor(y[:, k.slot, :], p_y[k.pair][:, 0:FEAT], own[:, k.slot, :], ALU.add)\
                           .then_inc(s.y_done, 1)
                    if k := tile_at(g, u, 4):
                        select(dve, m, s, key, same, cont, k, m.attn2)
                run_steps(dve, step, 11)


def gcn(nc, d, m, out):
    names = ["idx_staged", "scaled", "x3_done", "sel_done", "agg_done", "carry_done", "proj_done", "y_done",
             "zero_done", "out_staged"] + NORM_SEMS
    ctx, s = phase(nc, "gcn", names, ["x_in", "src_in", "own_in", "res_in", "out_done"], [("key_in", 2)])
    with ctx:
        def sb(name, shape, dt=F32):
            return ctx.enter_context(nc.sbuf_tensor("gn_" + name, shape, dt))
        idx, out_idx = sb("idx", [P, UNROLL], I32), sb("out_idx", [P, UNROLL], I32)
        key, same, cont = sb("key", [P, 2, RING * P + 1]), sb("same", [P, RING, P]), sb("cont", [P, RING, P])
        xs, own, res = sb("xs", [P, RING, FEAT]), sb("own", [P, RING, FEAT]), sb("res", [P, RING, FEAT])
        ax, x3 = sb("ax", [P, 2, FEAT]), sb("x3", [P, 2, FEAT])
        aggT = sb("aggT", [P, 2, FC, P])
        y, rows = sb("y", [P, RING, FEAT]), sb("rows", [P, RING, FEAT])
        v = norm_space(sb)
        p_agg, p_out = m.bank[0:2], m.bank[2:4]
        alpha, beta, gamma = (m.affine[:, 1, j, :] for j in range(3))

        with nc.Block() as block:
            @block.sync
            def _(sp):
                def step(g, u):
                    if k := tile_at(g, u, 0):
                        load_sources(sp, m, s, xs, s.scaled, k)
                        load_key(sp, m, s, key, k)
                        hold(sp, s.agg_done, k.t - (RING - 1))
                        sp.dma_start(own[:, k.slot, :], tile_rows(m.state[3], k.t)).then_inc(s.own_in[k.slot], 16)
                    if k := tile_at(g, u, 2):
                        hold(sp, s.y_done, k.t - (RING - 1))
                        sp.dma_start(res[:, k.slot, :], tile_rows(m.res3, k.t)).then_inc(s.res_in[k.slot], 16)
                run_steps(sp, step, 2)

            @block.gpsimd
            def _(pool):
                def step(g, u):
                    if k := tile_at(g, u, 0):
                        overlay(pool, m, s, xs, idx, m.state[3], k)
                    if k := tile_at(g, u, 12):
                        if k.slot == 0:
                            for slot in range(RING):
                                hold(pool, s.out_done[slot], 16 * (k.turn - 1))
                            half = k.body_slot // RING * RING
                            pool.tensor_copy(out_idx[:, half:half + RING], col(m.map_idx, k.t, RING)).then_inc(s.out_staged, 1)
                            hold(pool, s.out_staged, k.turn + 1)
                        hold(pool, s.rows_done, k.t + 1)
                        at = k.body_slot
                        pool.indirect_dma_start(out, bass.IndirectOffsetOnAxis(ap=out_idx[:, at:at + 1], axis=0),
                                                rows[:, k.slot, :], None, bounds_check=NODES - 1, oob_is_err=False)\
                            .then_inc(s.out_done[k.slot], 16)
                run_steps(pool, step, 12)
                for slot in range(RING):
                    pool.wait_ge(s.out_done[slot], 16 * (TILES // RING))

            @block.scalar
            def _(act):
                def step(g, u):
                    if k := tile_at(g, u, 10):
                        norm_root(act, m, s, v, k)
                    if k := tile_at(g, u, 3):
                        act.wait_ge(s.src_in[k.slot], 16 * (k.turn + 1))
                        wait(act, s.x3_done, k.t - 1)
                        act.activation(ax[:, k.pair, :], xs[:, k.slot, :], ACT.Identity, bias=col(gamma, k.t),
                                       scale=col(alpha, k.t)).then_inc(s.scaled, 1)
                    if k := tile_at(g, u, 11):
                        wait(act, s.out_done[k.slot], 16 * k.turn)
                        norm_rows(act, s, v, rows[:, k.slot, :], y[:, k.slot, :], k)
                run_steps(act, step, 11)

            @block.tensor
            def _(pe):
                def step(g, u):
                    if k := tile_at(g, u, 7):
                        pe.wait_ge(s.carry_done, k.t + 1)
                        wait(pe, s.y_done, k.t - 1)
                        for c in range(FC):
                            ins = pe.matmul(p_out[k.pair][:, 0:FEAT], aggT[:, k.pair, c, :], m.w_gcn[:, c, :],
                                            start=c == 0, stop=c == FC - 1)
                        ins.then_inc(s.proj_done, 1)
                    if k := tile_at(g, u, 5):
                        pe.wait_ge(s.own_in[k.slot], 16 * (k.turn + 1))
                        wait(pe, s.carry_done, k.t - 1)
                        pe.wait_ge(s.x3_done, k.t + 1)
                        pe.wait_ge(s.sel_done, k.t + 1)
                        for c in range(FC):
                            to = p_agg[k.pair][:, c * P:(c + 1) * P]
                            pe.matmul(to, own[:, k.slot, c * P:(c + 1) * P], m.ident[:], start=True, stop=False)
                            ins = pe.matmul(to, x3[:, k.pair, c * P:(c + 1) * P], same[:, k.slot, :], start=False, stop=True)
                        ins.then_inc(s.agg_done, 1)
                run_steps(pe, step, 7)

            @block.vector
            def _(dve):
                dve.memset(aggT[:, 1, :, P - 1], 0.0).then_inc(s.zero_done, 1)
                dve.wait_ge(s.zero_done, 1)

                def step(g, u):
                    if recip := tile_at(g, u, 10):
                        norm_recip(dve, s, v, recip)
                    if stats := tile_at(g, u, 9):
                        dve.wait_ge(s.y_done, stats.t + 1)
                        norm_stats(dve, s, v, y[:, stats.slot, :], stats)
                    if recip:
                        norm_shift(dve, s, v, recip)
                    if k := tile_at(g, u, 6):
                        carry_over(dve, s, aggT, cont, p_agg, k, FC, s.proj_done)
                    if stats:
                        norm_aggregate(dve, s, v, stats)
                    if k := tile_at(g, u, 8):
                        dve.wait_ge(s.proj_done, k.t + 1)
                        dve.wait_ge(s.res_in[k.slot], 16 * (k.turn + 1))
                        wait(dve, s.rows_done, k.t - (RING - 1))
                        dve.scalar_tensor_tensor(y[:, k.slot, :], p_out[k.pair][:, 0:FEAT], col(m.dinv, k.t),
                                                 res[:, k.slot, :], ALU.mult, ALU.add).then_inc(s.y_done, 1)
                    if k := tile_at(g, u, 4):
                        dve.wait_ge(s.scaled, k.t + 1)
                        wait(dve, s.agg_done, k.t - 1)
                        dve.scalar_tensor_tensor(x3[:, k.pair, :], m.bias[:], col(beta, k.t), ax[:, k.pair, :],
                                                 ALU.mult, ALU.add).then_inc(s.x3_done, 1)
                        select(dve, m, s, key, same, cont, k)
                run_steps(dve, step, 10)


_OUTS = [((NODES, FEAT), "float32")]


def kernel(x, src, dst, edge_attr_3, L0_gnn_W1, L0_gnn_b1, L0_gnn_W2, L0_gnn_b2, L1_gnn_W, L1_gnn_a_src,
           L1_gnn_a_dst, L1_gnn_edge_W, L1_gnn_edge_b, L1_gnn_bias, L2_gnn_Wv, L2_gnn_bv, L2_gnn_wq, L2_gnn_bq,
           L2_gnn_wk, L2_gnn_bk, L3_gnn_W_conv, L3_gnn_b_conv, L3_gnn_W_lin, L3_gnn_b_lin):
    import numpy as np
    import concourse.bacc as bacc
    from concourse.bass_utils import run_bass_kernel_spmd

    c = np.ascontiguousarray
    x, src, dst, edge_attr_3 = (np.asarray(a) for a in (x, src, dst, edge_attr_3))
    pad = EPAD - EDGES
    heads = np.arange(FEAT)[:, None] // HEAD_DIM == np.arange(HEADS)[None, :]
    arrays = {
        "x": c(x),
        "dst_pad": np.concatenate([np.full(1, -1, np.int32), dst, np.full(pad, NODES, np.int32),
                                   np.full(1, NODES + 1, np.int32)]),
        "src_pad": np.concatenate([src, np.zeros(pad, np.int32)]),
        "edge_attr_T": c(np.concatenate([edge_attr_3, np.zeros((pad, EDGE_FEAT), np.float32)]).T),
        "head_mask": heads.astype(np.float32),
        "L0_W1": c(L0_gnn_W1), "L0_b1": c(L0_gnn_b1), "L0_W2": c(L0_gnn_W2), "L0_b2": c(L0_gnn_b2),
        "L1_W": c(L1_gnn_W), "L1_WT": c(np.asarray(L1_gnn_W).T), "L1_a_src": c(L1_gnn_a_src).reshape(FEAT, 1),
        "L1_a_dst": c(L1_gnn_a_dst).reshape(FEAT, 1), "L1_eWT": c(np.asarray(L1_gnn_edge_W).T),
        "L1_eb": c(L1_gnn_edge_b), "L1_bias": c(L1_gnn_bias),
        "L2_Wv": c(L2_gnn_Wv), "L2_WvT": c(np.asarray(L2_gnn_Wv).T), "L2_bv": c(L2_gnn_bv),
        "L2_wq": c(L2_gnn_wq).reshape(FEAT, 1), "L2_wk": c(L2_gnn_wk).reshape(FEAT, 1),
        "L2_bq": c(L2_gnn_bq).reshape(1), "L2_bk": c(L2_gnn_bk).reshape(1),
        "L3_WcT": c(np.asarray(L3_gnn_W_conv).T), "L3_bc": c(L3_gnn_b_conv).reshape(GCN_HIDDEN, 1),
        "L3_Wl": c(L3_gnn_W_lin), "L3_bl": c(L3_gnn_b_lin),
    }
    arrays = {n: np.asarray(a) for n, a in arrays.items()}
    nc = bacc.Bacc("TRN2", target_bir_lowering=False, num_devices=1)
    d = namedtuple("Inputs", list(arrays))(*(nc.dram_tensor(n, a.shape, mybir.dt.from_np(a.dtype), kind="ExternalInput").ap()
                                             for n, a in arrays.items()))
    (shape, dtype), = _OUTS
    out = nc.dram_tensor("out", shape, mybir.dt.from_np(np.dtype(dtype)), kind="ExternalOutput").ap()
    build(nc, d, out)
    r = run_bass_kernel_spmd(nc, [arrays], core_ids=[0])
    return r.results[0]["out"]
```
